# Optimizing a Trainium2 kernel written in Bass

```python
import numpy as np
import jax
import jax.numpy as jnp

def _softmax(x, axis=-1):
    return jax.nn.softmax(x, axis=axis)
def _gelu(x):
    return jax.nn.gelu(x, approximate=True)
def _silu(x):
    return jax.nn.silu(x)
def _sigmoid(x):
    return jax.nn.sigmoid(x)
def _layernorm(x, axis=-1, eps=1e-5):
    m = jnp.mean(x, axis=axis, keepdims=True)
    v = jnp.var(x, axis=axis, keepdims=True)
    return (x - m) / jnp.sqrt(v + eps)
def _scatter_add(tgt, idx, src, axis=0):
    return tgt.at[idx].add(src)
def _segment_sum(src, seg, n):
    return jax.ops.segment_sum(src, seg, n)

kernel_name = 'mk_metaformer_d2_conv_nchw128_def079'

def setup_inputs(seed: int = 0):
    np.random.seed(seed)
    _w = jnp.asarray
    def _rec_inputs():
        import jax
        import jax.numpy as jnp
        _gk = jax.random.key(seed)
        x = -0.0002928 + 1 * jax.random.normal(jax.random.fold_in(_gk, 1), (8, 128, 64, 64), jnp.float32)
        return x
    x = _rec_inputs()
    def _L0_conv_setup():
        import jax, jax.numpy as jnp
        import numpy as np
        K = 3
        HEADS = 8
        EPS = 1e-05

        def _layernorm(x, g, b):
            m = jnp.mean(x, axis=-1, keepdims=True)
            v = jnp.mean(jnp.square(x - m), axis=-1, keepdims=True)
            return (x - m) * jax.lax.rsqrt(v + EPS) * g + b
        key = jax.random.key(seed)
        ks = jax.random.split(key, 4)
        B, C, H, W = (8, 128, 64, 64)
        x = jax.random.normal(ks[0], (B, C, H, W), dtype=jnp.float32)
        w_qkv = jax.random.normal(ks[1], (3 * C, C), dtype=jnp.float32) * C ** (-0.5)
        w_proj = jax.random.normal(ks[2], (C, C), dtype=jnp.float32) * C ** (-0.5)
        b_proj = jnp.zeros((C,), dtype=jnp.float32)
        ln1_g = jnp.ones((C,), dtype=jnp.float32)
        ln1_b = jnp.zeros((C,), dtype=jnp.float32)
        ln2_g = jnp.ones((C,), dtype=jnp.float32)
        ln2_b = jnp.zeros((C,), dtype=jnp.float32)
        return {'x': x, 'w_qkv': w_qkv, 'w_proj': w_proj, 'b_proj': b_proj, 'ln1_g': ln1_g, 'ln1_b': ln1_b, 'ln2_g': ln2_g, 'ln2_b': ln2_b}
    _L0_conv_all = _L0_conv_setup()
    _L0_conv_in = {k: v for k, v in _L0_conv_all.items() if k in ('w_qkv', 'w_proj', 'b_proj', 'ln1_g', 'ln1_b', 'ln2_g', 'ln2_b', )}
    del _L0_conv_all

    def _L0_ffn_setup():
        import jax, jax.numpy as jnp
        import numpy as np
        B, N, D, C, E, K = (8, 8192, 128, 128, 8, 2)
        key = jax.random.key(seed)
        k0, k1, k2 = jax.random.split(key, 3)
        x = jax.random.normal(k0, (B, N, D), dtype=jnp.float32)
        router_w = jax.random.normal(k1, (D, E), dtype=jnp.float32) * 0.05
        router_b = jnp.zeros((E,), dtype=jnp.float32)
        expert_w = jax.random.normal(k2, (E, D, C), dtype=jnp.float32) * (1.0 / np.sqrt(D))
        expert_b = jnp.zeros((E, C), dtype=jnp.float32)
        return {'x': x, 'router_w': router_w, 'router_b': router_b, 'expert_w': expert_w, 'expert_b': expert_b}
    _L0_ffn_all = _L0_ffn_setup()
    _L0_ffn_in = {k: v for k, v in _L0_ffn_all.items() if k in ('router_w', 'router_b', 'expert_w', 'expert_b', )}
    del _L0_ffn_all

    def _L1_conv_setup():
        import jax
        import jax.numpy as jnp
        import numpy as np
        from jax import lax
        SCOPE = 27
        DECAY = 0.05
        MAX_STEPS = 20
        STD = 2.0

        def mexican_hat(scope: int, std: float) -> jnp.ndarray:
            x = jnp.arange(scope, dtype=jnp.float32) - scope // 2
            a = 2.0 / (np.sqrt(3.0 * std) * np.pi ** 0.25)
            return a * (1.0 - (x / std) ** 2) * jnp.exp(-x ** 2 / (2.0 * std ** 2))

        def _conv_channel(x: jnp.ndarray, weight: jnp.ndarray) -> jnp.ndarray:
            pad = SCOPE // 2
            return lax.conv_general_dilated(x, weight, window_strides=(1, 1, 1), padding=[(pad, pad), (0, 0), (0, 0)], dimension_numbers=('NCDHW', 'OIDHW', 'NCDHW'))
        key = jax.random.key(seed)
        k1, _ = jax.random.split(key)
        activations = jax.random.normal(k1, (64, 128, 56, 56), dtype=jnp.float32)
        weight = mexican_hat(SCOPE, STD).reshape(1, 1, SCOPE, 1, 1)
        return {'activations': activations, 'weight': weight}
    _L1_conv_all = _L1_conv_setup()
    _L1_conv_in = {k: v for k, v in _L1_conv_all.items() if k in ('weight', )}
    del _L1_conv_all

    def _L1_ffn_setup():
        import jax, jax.numpy as jnp
        import numpy as np
        BN_EPS = 1e-05
        key = jax.random.key(seed)
        k1, k2, k3 = jax.random.split(key, 3)
        B, T, I, H = (64, 2048, 128, 128)
        x = jax.random.normal(k1, (B, T, I), dtype=jnp.float32)
        W = jax.random.normal(k2, (H, I), dtype=jnp.float32) * (1.0 / np.sqrt(I))
        V = jnp.linalg.qr(jax.random.normal(k3, (H, H), dtype=jnp.float32))[0]
        gamma = jnp.ones((H,), dtype=jnp.float32)
        beta = jnp.zeros((H,), dtype=jnp.float32)
        return {'x': x, 'W': W, 'V': V, 'gamma': gamma, 'beta': beta}
    _L1_ffn_all = _L1_ffn_setup()
    _L1_ffn_in = {k: v for k, v in _L1_ffn_all.items() if k in ('W', 'V', 'gamma', 'beta', )}
    del _L1_ffn_all

    return {
        "x": x,
        "L0_conv_w_qkv": _L0_conv_in["w_qkv"],
        "L0_conv_w_proj": _L0_conv_in["w_proj"],
        "L0_conv_b_proj": _L0_conv_in["b_proj"],
        "L0_conv_ln1_g": _L0_conv_in["ln1_g"],
        "L0_conv_ln1_b": _L0_conv_in["ln1_b"],
        "L0_conv_ln2_g": _L0_conv_in["ln2_g"],
        "L0_conv_ln2_b": _L0_conv_in["ln2_b"],
        "L0_ffn_router_w": _L0_ffn_in["router_w"],
        "L0_ffn_router_b": _L0_ffn_in["router_b"],
        "L0_ffn_expert_w": _L0_ffn_in["expert_w"],
        "L0_ffn_expert_b": _L0_ffn_in["expert_b"],
        "L1_conv_weight": _L1_conv_in["weight"],
        "L1_ffn_W": _L1_ffn_in["W"],
        "L1_ffn_V": _L1_ffn_in["V"],
        "L1_ffn_gamma": _L1_ffn_in["gamma"],
        "L1_ffn_beta": _L1_ffn_in["beta"],
    }

def reference(x, L0_conv_w_qkv, L0_conv_w_proj, L0_conv_b_proj, L0_conv_ln1_g, L0_conv_ln1_b, L0_conv_ln2_g, L0_conv_ln2_b, L0_ffn_router_w, L0_ffn_router_b, L0_ffn_expert_w, L0_ffn_expert_b, L1_conv_weight, L1_ffn_W, L1_ffn_V, L1_ffn_gamma, L1_ffn_beta):
    import jax
    import jax.numpy as jnp
    def _L0_conv_ref(x, w_qkv, w_proj, b_proj, ln1_g, ln1_b, ln2_g, ln2_b):
        import jax, jax.numpy as jnp
        import numpy as np
        K = 3
        HEADS = 8
        EPS = 1e-05

        def _layernorm(x, g, b):
            m = jnp.mean(x, axis=-1, keepdims=True)
            v = jnp.mean(jnp.square(x - m), axis=-1, keepdims=True)
            return (x - m) * jax.lax.rsqrt(v + EPS) * g + b
        B, C, H, W = x.shape
        Ho, Wo = (H - K + 1, W - K + 1)
        P = K * K
        NW = Ho * Wo
        hd = C // HEADS
        patches = jnp.stack([x[:, :, i:i + Ho, j:j + Wo] for i in range(K) for j in range(K)], axis=2)
        xs = patches.reshape(B, C, P, NW).transpose(0, 3, 2, 1).reshape(B * NW, P, C)
        xs = _layernorm(xs, ln1_g, ln1_b)
        qkv = xs @ w_qkv.T
        qkv = qkv.reshape(B * NW, P, 3, HEADS, hd).transpose(2, 0, 3, 1, 4)
        q, k, v = (qkv[0], qkv[1], qkv[2])
        attn = jax.nn.softmax(jnp.einsum('bhpd,bhqd->bhpq', q, k) * hd ** (-0.5), axis=-1)
        o = jnp.einsum('bhpq,bhqd->bhpd', attn, v)
        o = o.transpose(0, 2, 1, 3).reshape(B * NW, P, C)
        o = o @ w_proj.T + b_proj
        o = _layernorm(o, ln2_g, ln2_b)
        po = o.reshape(B, NW, P, C).transpose(0, 3, 2, 1).reshape(B, C, P, Ho, Wo)
        out = jnp.zeros((B, C, H, W), dtype=x.dtype)
        idx = 0
        for i in range(K):
            for j in range(K):
                out = out.at[:, :, i:i + Ho, j:j + Wo].add(po[:, :, idx])
                idx += 1
        return out

    def _L0_ffn_ref(x, router_w, router_b, expert_w, expert_b):
        import jax, jax.numpy as jnp
        import numpy as np
        B, N, D, C, E, K = (8, 8192, 128, 128, 8, 2)
        router_probs = jax.nn.softmax(x @ router_w + router_b, axis=-1)
        top_p, top_i = jax.lax.top_k(router_probs, K)
        top_p = top_p / jnp.sum(top_p, axis=-1, keepdims=True)
        expert_out = jnp.einsum('bnd,edc->bnec', x, expert_w) + expert_b
        gathered = jnp.take_along_axis(expert_out, top_i[..., None], axis=2)
        return jnp.einsum('bnk,bnkc->bnc', top_p, gathered)

    def _L1_conv_ref(activations, weight):
        import jax
        import jax.numpy as jnp
        import numpy as np
        from jax import lax
        SCOPE = 27
        DECAY = 0.05
        MAX_STEPS = 20
        STD = 2.0

        def mexican_hat(scope: int, std: float) -> jnp.ndarray:
            x = jnp.arange(scope, dtype=jnp.float32) - scope // 2
            a = 2.0 / (np.sqrt(3.0 * std) * np.pi ** 0.25)
            return a * (1.0 - (x / std) ** 2) * jnp.exp(-x ** 2 / (2.0 * std ** 2))

        def _conv_channel(x: jnp.ndarray, weight: jnp.ndarray) -> jnp.ndarray:
            pad = SCOPE // 2
            return lax.conv_general_dilated(x, weight, window_strides=(1, 1, 1), padding=[(pad, pad), (0, 0), (0, 0)], dimension_numbers=('NCDHW', 'OIDHW', 'NCDHW'))
        x = activations[:, None]
        inhib_in = _conv_channel(x, weight)

        def step(state, _):
            inhib_rec = _conv_channel(state, weight)
            phi = (inhib_in + inhib_rec) * 0.5
            state = (1.0 - DECAY) * state + DECAY * phi
            return (state, None)
        converged, _ = lax.scan(step, inhib_in, None, length=MAX_STEPS)
        return converged[:, 0]

    def _L1_ffn_ref(x, W, V, gamma, beta):
        import jax, jax.numpy as jnp
        import numpy as np
        BN_EPS = 1e-05
        B, T, H = (x.shape[0], x.shape[1], W.shape[0])
        Wx = jnp.einsum('bti,hi->bth', x, W)
        flat = Wx.reshape(B * T, H)
        mean = jnp.mean(flat, axis=0)
        var = jnp.var(flat, axis=0)
        Wx = ((flat - mean) * jax.lax.rsqrt(var + BN_EPS) * gamma + beta).reshape(B, T, H)
        Vt = V.T

        def step(yt, wx_t):
            yt = jax.nn.sigmoid(wx_t + yt @ Vt)
            return (yt, yt)
        y0 = jnp.zeros((B, H), dtype=Wx.dtype)
        _, ys = jax.lax.scan(step, y0, jnp.swapaxes(Wx, 0, 1))
        return jnp.swapaxes(ys, 0, 1)

    def _gn(v, G=32, eps=1e-5):
        B_, C_, H_, W_ = v.shape
        g = v.reshape(B_, G, C_ // G, H_, W_)
        m = jnp.mean(g, axis=(2, 3, 4), keepdims=True)
        s = jnp.var(g, axis=(2, 3, 4), keepdims=True)
        return ((g - m) / jnp.sqrt(s + eps)).reshape(v.shape)

    def _ln_c(v, eps=1e-6):
        m = jnp.mean(v, axis=1, keepdims=True)
        s = jnp.var(v, axis=1, keepdims=True)
        return (v - m) / jnp.sqrt(s + eps)

    def _ln_t(v, eps=1e-5):
        m = jnp.mean(v, axis=-1, keepdims=True)
        s = jnp.var(v, axis=-1, keepdims=True)
        return (v - m) / jnp.sqrt(s + eps)

    def _to_tokens(v):
        B_, C_, H_, W_ = v.shape
        return v.reshape(B_, C_, H_ * W_).transpose(0, 2, 1)
    def _from_tokens(t, like):
        B_, C_, H_, W_ = like.shape
        return t.transpose(0, 2, 1).reshape(B_, C_, H_, W_)

    x = x + _L0_conv_ref(_ln_c(x), L0_conv_w_qkv, L0_conv_w_proj, L0_conv_b_proj, L0_conv_ln1_g, L0_conv_ln1_b, L0_conv_ln2_g, L0_conv_ln2_b)
    t = _to_tokens(x)
    t = t + _L0_ffn_ref(_ln_t(t), L0_ffn_router_w, L0_ffn_router_b, L0_ffn_expert_w, L0_ffn_expert_b)
    x = _from_tokens(t, x)
    x = x + _L1_conv_ref(_ln_c(x), L1_conv_weight)
    t = _to_tokens(x)
    t = t + _L1_ffn_ref(_ln_t(t), L1_ffn_W, L1_ffn_V, L1_ffn_gamma, L1_ffn_beta)
    x = _from_tokens(t, x)
    return x


_drawn_inputs = setup_inputs


def setup_inputs(seed=0):
    import zlib

    import numpy as np

    out = dict(_drawn_inputs(seed))
    spreads = {'L0_conv_b_proj': (0.0, 0.1),
     'L0_conv_ln1_g': (1.0, 0.2),
     'L0_conv_ln1_b': (0.0, 0.1),
     'L0_conv_ln2_g': (1.0, 0.2),
     'L0_conv_ln2_b': (0.0, 0.1),
     'L0_ffn_router_b': (0.0, 0.1),
     'L0_ffn_expert_b': (0.0, 0.737),
     'L1_ffn_gamma': (1.0, 0.6),
     'L1_ffn_beta': (0.0, 0.8)}
    factors = {'L1_ffn_V': 3.852}
    for name, (base, spread) in spreads.items():
        noise = np.random.default_rng([zlib.crc32(name.encode()), seed]).standard_normal(out[name].shape)
        drawn = base * np.exp(spread * noise) if base else spread * noise
        out[name] = jnp.asarray(drawn.astype(out[name].dtype))
    for name, factor in factors.items():
        out[name] = (out[name] * factor).astype(out[name].dtype)
    return out
```

```python
from contextlib import ExitStack

import concourse.bass as bass
from concourse import mybir

F32 = mybir.dt.float32
BF16 = mybir.dt.bfloat16
ALU = mybir.AluOpType
ACT = mybir.ActivationFunctionType
AX = mybir.AxisListType

P = 128
IMGS, IMG = 8, 64
ROWS = 8
PIX = ROWS * IMG
TILES = PIX // P
CHUNKS = IMGS * IMG // ROWS
HALO = 2
HROWS = ROWS + 2 * HALO
HPIX = HROWS * IMG
HTILES = HPIX // P
HALF = HPIX // 2
PADW = IMG + 2 * HALO
HEADS, HD = 8, 16
KW = 3
NB = 2 * KW - 1
OFFS = NB * NB
WINS = KW * KW
EXPERTS = 8
PARTS = 3
STEPS = IMG * IMG
CONV_STEPS = 20
ROUTE = 17
CONSTS = 35

SEQ = [4 * g + m for m in range(4) for g in range(4)] + [16, 20, 24, 17, 21, 18, 22, 19, 23]
BY_POOL = [k for k in range(OFFS) if k % 6 == 5]
BY_DVE = [k for k in range(OFFS) if k not in BY_POOL]
DVE_RING, POOL_RING = 6, 2

BLK = 128
HBLK = BLK // 2
PIECES = 8


def program(nc, x_halo, valid, w_qkvT, w_projT, b_proj, ln1_g, ln1_b, ln2_g, ln2_b, router_w, router_b,
            expert_w, expert_b, conv, convT, w_T, v_T, gamma, beta, out, n_chunks=CHUNKS,
            n_blocks=STEPS // BLK):
    wx_dram = nc.dram_tensor("wx_scratch", (P, CHUNKS * PIX), F32, kind="Internal").ap()
    xb_dram = nc.dram_tensor("xb_scratch", (P, CHUNKS * PIX), F32, kind="Internal").ap()
    with ExitStack() as ctx:
        def sb(name, shape, dt=F32):
            return ctx.enter_context(nc.sbuf_tensor(name, shape, dt))

        def sem(name):
            return ctx.enter_context(nc.semaphore(name))

        ident = sb("ident", [P, P])
        ident_b = sb("ident_b", [P, P], BF16)
        mean_w = sb("mean_w", [P, P])
        head_sum = sb("head_sum", [P, 4, 32])
        spread = sb("spread", [P, NB, P], BF16)
        minus_half = sb("minus_half", [P, 4 * WINS])
        rank = sb("rank", [P, TILES, EXPERTS])
        wqkv = sb("wqkv", [P, 3, P])
        bqkv = sb("bqkv", [P, 3])
        wproj = sb("wproj", [P, P])
        wproj_g = sb("wproj_g", [P, P])
        prow = sb("prow", [P, 3, P])
        brow = sb("brow", [2, P])
        sel = sb("sel", [2, 2])
        bproj_c = sb("bproj_c", [P, 1])
        cols = sb("cols", [P, 6])
        rw = sb("rw", [P, EXPERTS])
        rb = sb("rb", [P, EXPERTS])
        ew = sb("ew", [P, EXPERTS, P])
        eb = sb("eb", [EXPERTS, P])
        conv_a = sb("conv_a", [P, P])
        conv_bT = sb("conv_bT", [P, P])
        conv_mT = sb("conv_mT", [P, P])
        w_in = sb("w_in", [P, P])
        v_rec = sb("v_rec", [P, P])
        tiny = sb("tiny", [P, 8])

        xh = sb("xh", [P, HPIX])
        xres = sb("xres", [P, PIX])
        xc0 = sb("xc0", [P, HPIX])
        sq0 = sb("sq0", [P, HPIX])
        var0 = sb("var0", [P, HTILES])
        rs0 = sb("rs0", [P, HTILES])
        q = sb("q", [P, PIX])
        k_pad = sb("k_pad", [P, HROWS, PADW])
        v_pad = sb("v_pad", [P, HROWS, PADW])
        prod_d = sb("prod_d", [P, DVE_RING, PIX])
        prod_p = sb("prod_p", [P, POOL_RING, PIX])
        s2 = sb("s2", [P, 2, PIX])
        smax = sb("smax", [P, TILES, HEADS])
        es = sb("es", [P, TILES, OFFS, HEADS])
        e32 = sb("e32", [P, TILES, OFFS, HEADS])
        erest = es
        e3 = sb("e3", [P, TILES, OFFS, PARTS, HEADS], BF16)
        dsum_a = sb("dsum_a", [P, TILES * NB, KW * HEADS])
        dsum_h = sb("dsum_h", [P, TILES, NB, KW * HEADS])
        dsum_b = sb("dsum_b", [P, TILES, KW * KW * HEADS])
        dsum = sb("dsum", [P, TILES, WINS * HEADS])
        rden = sb("rden", [P, TILES, WINS, HEADS])
        rrest = sb("rrest", [P, TILES, WINS, HEADS])
        r3 = sb("r3", [P, TILES, WINS, PARTS, HEADS], BF16)
        eT = sb("eT", [NB * PARTS * HEADS, NB, PIX], BF16)
        rT = sb("rT", [KW * PARTS * HEADS, KW, PIX], BF16)
        ev = sb("ev", [P, 2, NB, PIX])
        hs_a = sb("hs_a", [P, 2, 2, PIX])
        hs = sb("hs", [P, NB, KW, PIX])
        vs = sb("vs", [P, 2, KW, PIX])
        win = sb("win", [P, KW, KW, PIX])
        conv_s = win[:].rearrange("p a b n -> p (a b n)")[:, 0:(CONV_STEPS + 1) * P]\
            .rearrange("p (k n) -> p k n", n=P)
        sqy = sb("sqy", [P, 2, PIX])
        ok = sb("ok", [P, TILES, WINS + 1])
        vary = sb("vary", [P, TILES * WINS])
        rsy = sb("rsy", [P, TILES, WINS])
        rsv = sb("rsv", [P, TILES, WINS])
        rc = sb("rc", [P, TILES, 2])
        rcT = sb("rcT", [2, PIX])
        x1 = sb("x1", [P, PIX])
        xc = sb("xc", [P, PIX])
        sq = sb("sq", [P, PIX])
        xn = sb("xn", [P, PIX])
        var = sb("var", [P, TILES])
        rs = sb("rs", [P, TILES])
        logit = sb("logit", [P, TILES, EXPERTS])
        hot = sb("hot", [P, 2, TILES, EXPERTS])
        rt = sb("rt", [P, 4, TILES, EXPERTS])
        top = sb("top", [P, 8, TILES])
        gate = sb("gate", [P, TILES, EXPERTS])
        gT = sb("gT", [EXPERTS, PIX])
        xg = sb("xg", [P, 2, PIX])
        xa = sb("xa", [P, PIX])
        xb = sb("xb", [P, PIX])
        wx = sb("wx", [P, PIX])
        stats = sb("stats", [P, CHUNKS * 6])
        mv = sb("mv", [P, 2])
        n = IMGS * BLK
        wxr, xbr, outb = [hs[:].rearrange("p a b n -> p (a b n)")[:, k * n:(k + 1) * n]
                          .rearrange("p (b t) -> p b t", t=BLK) for k in range(3)]
        z, y = [hs[:].rearrange("p a b n -> p (a b n)")[:, k * n:(k + 1) * n]
                .rearrange("p (h t b) -> p h t b", h=2, b=IMGS) for k in (3, 4)]

        ps = ctx.enter_context(nc.psum_tensor("ps", [P, 8, 512], F32))
        psA = ps[:, 0:2, :]
        psS = ps[:, 2:4, :].rearrange("p b (t c) -> p (b t) c", c=256)
        psT = ps[:, 2:4, :].rearrange("p b c -> p (b c)").bitcast(BF16)
        psB = ps[:, 4:6, :]
        psY = ps[:, 6, :]
        psF = ps[:, 7, :]

        names = """consts weights w_scaled w_ready setup_pe setup_dve
            x_loaded ok_loaded xres_ready
            pre_mean pre_cent pre_sq pre_var pre_v pre_rs pre_bc pre_xn k_mm k_ready v_mm v_ready q_mm q_ready
            prod_dve prod_pool reduced s2_ready s_turned smax_ready es_ready e_ready e_hi e_rest e_mid e_lo
            dsum_step r_ready r_hi r_rest r_mid r_lo e_turned eT_ready e_spread ev_ready hsum_step vsum_step
            r_spread win_ready proj_mm sqy_ready vary_mm vary_ready rsy_ready rsv_ready rc_ready cnt_ready
            rc_turned rcT_ready rs_spread u_ready final_mm x1_ready
            lnA_mean lnA_cent lnA_sq lnA_var lnA_v lnA_rs lnA_bc lnA_xn
            lnB_mean lnB_cent lnB_sq lnB_var lnB_v lnB_rs lnB_bc lnB_xn
            lnC_mean lnC_cent lnC_sq lnC_var lnC_v lnC_rs lnC_bc lnC_xn
            logit_mm route_step gap_ready exp_ready g_ready g_turned gT_ready g_spread xg_ready moe_mm xa_ready
            conv_mm xb_ready wx_mm wx_ready stats_ready xb_stored wx_stored
            bn_step bn_v bn_rs z_loaded z_ready z_used step_mm y_ready res_loaded out_ready out_stored y_zero""".split()
        S = {n: sem(n) for n in names}
        block = ctx.enter_context(nc.Block())

        def head_shift(t, off):
            dy, dx = off // NB, off % NB
            return t[:, dy:dy + ROWS, dx:dx + IMG]

        def rows(a):
            return a.rearrange("p (r c) -> p r c", c=IMG)

        LOADS = 2 + 5 + 3 + 1 + 1 + 2 + 2 + 2

        def dram_block(a, at, ahead):
            a = a.rearrange("p (b t) -> p b t", b=IMGS)
            return (a[:, :, BLK:] if ahead else a)[:, :, bass.ds(at, BLK)]

        def scan_sp(sp):
            def load_wx(halves, at, ahead):
                sp.wait_ge(S["z_ready"], halves)
                sp.dma_start(wxr, dram_block(wx_dram, at, ahead)).then_inc(S["z_loaded"], 16)

            def load_res(halves, at, ahead):
                sp.wait_ge(S["out_ready"], halves)
                sp.dma_start(xbr, dram_block(xb_dram, at, ahead)).then_inc(S["res_loaded"], 16)

            def store(at):
                sp.dma_start(out.rearrange("b c t -> c b t")[:, :, bass.ds(at, BLK)], outb)\
                    .then_inc(S["out_stored"], 16)
            load_wx(0, 0, False)
            load_res(0, 0, False)
            if n_blocks > 1:
                with sp.Fori(0, n_blocks - 1) as n:
                    at = sp.snap(n * BLK)
                    halves = sp.snap(n * 2 + 2)
                    load_wx(halves, at, True)
                    load_res(halves, at, True)
                    store(at)
            sp.wait_ge(S["out_ready"], 2 * n_blocks)
            store((n_blocks - 1) * BLK)
            sp.wait_ge(S["out_stored"], 16 * n_blocks)

        def scan_dve(ve):
            def half(n, h):
                ve.wait_ge(S["z_loaded"], 16 * (n + 1))
                ve.tensor_scalar(z[:, h], wxr[:, :, HBLK * h:HBLK * (h + 1)].rearrange("p b t -> p t b"),
                                 tiny[:, 4:5], tiny[:, 5:6], ALU.mult, ALU.add).then_inc(S["z_ready"], 1)
            half(0, 0)
            half(0, 1)
            if n_blocks > 1:
                with ve.Fori(1, n_blocks) as n:
                    for h in range(2):
                        ve.wait_ge(S["z_used"], 2 * n + h - 1)
                        half(n, h)

        def scan_pe(pe):
            def preload(h, piece):
                c = piece * PIX // PIECES
                m = pe.matmul(ps[:, h, c:c + PIX // PIECES], ident[:],
                              z[:, h].rearrange("p t b -> p (t b)")[:, c:c + PIX // PIECES],
                              start=piece == 0, stop=True, skip_group_check=True)
                if piece == PIECES - 1:
                    m.then_inc(S["z_used"], 1)

            def steps(n, h, last):
                every = HBLK // PIECES
                for j in range(HBLK):
                    pe.wait_ge(S["y_ready"], (2 * n + h) * HBLK + j)
                    prev = y[:, h, j - 1, :] if j else y[:, 1 - h, HBLK - 1, :]
                    for g in range(4):
                        m = pe.matmul(ps[32 * g:32 * g + 32, h, IMGS * j:IMGS * (j + 1)], v_rec[:, 32 * g:32 * g + 32],
                                      prev, start=False, stop=True, skip_group_check=True)
                    m.then_inc(S["step_mm"], 1)
                    if j % every == every // 2 and not last:
                        if j == every // 2:
                            pe.wait_ge(S["z_ready"], 2 * n + h + 2)
                        preload(1 - h, j // every)
            pe.wait_ge(S["y_zero"], 1)
            pe.wait_ge(S["z_ready"], 1)
            for piece in range(PIECES):
                preload(0, piece)
            if n_blocks > 1:
                with pe.Fori(0, n_blocks - 1) as n:
                    steps(n, 0, False)
                    steps(n, 1, False)
            steps(n_blocks - 1, 0, False)
            steps(n_blocks - 1, 1, True)

        def scan_act(ac):
            def steps(n, h, first):
                if not first:
                    ac.wait_ge(S["out_ready"], 2 * n + h - 1)
                for j in range(HBLK):
                    ac.wait_ge(S["step_mm"], (2 * n + h) * HBLK + j + 1)
                    ac.activation(y[:, h, j, :], ps[:, h, IMGS * j:IMGS * (j + 1)], ACT.Sigmoid).then_inc(S["y_ready"], 1)
            steps(0, 0, True)
            steps(0, 1, True)
            if n_blocks > 1:
                with ac.Fori(1, n_blocks) as n:
                    steps(n, 0, False)
                    steps(n, 1, False)

        def scan_pool(pl):
            pl.memset(y[:, 1], 0.0).then_inc(S["y_zero"], 1)
            with pl.Fori(0, n_blocks) as n:
                pl.wait_ge(S["res_loaded"], 16 * (n + 1))
                pl.wait_ge(S["out_stored"], 16 * n)
                for h in range(2):
                    pl.wait_ge(S["y_ready"], (2 * n + h + 1) * HBLK)
                    pl.tensor_tensor(outb[:, :, HBLK * h:HBLK * (h + 1)], xbr[:, :, HBLK * h:HBLK * (h + 1)],
                                     y[:, h].rearrange("p t b -> p b t"), ALU.add).then_inc(S["out_ready"], 1)

        @block.sync
        def _(sp):
            sp.dma_start(wqkv[:], w_qkvT).then_inc(S["weights"], 16)
            sp.dma_start(wproj[:], w_projT).then_inc(S["weights"], 16)
            for n, v in enumerate((ln1_g, ln1_b, b_proj, gamma, beta)):
                sp.dma_start(cols[:, n:n + 1], v.rearrange("(p a) -> p a", a=1)).then_inc(S["weights"], 16)
            for n, v in enumerate((b_proj, ln2_g, ln2_b)):
                sp.dma_start(prow[:, n, :], v.partition_broadcast(P)).then_inc(S["weights"], 16)
            sp.dma_start(rb[:], router_b.partition_broadcast(P)).then_inc(S["weights"], 16)
            sp.dma_start(rw[:], router_w).then_inc(S["weights"], 16)
            sp.dma_start(ew[:], expert_w.rearrange("e d c -> d e c")).then_inc(S["weights"], 16)
            sp.dma_start(eb[:], expert_b).then_inc(S["weights"], 16)
            sp.dma_start(conv_a[:], conv).then_inc(S["weights"], 16)
            sp.dma_start(conv_mT[:], convT).then_inc(S["weights"], 16)
            sp.dma_start(w_in[:], w_T).then_inc(S["weights"], 16)
            sp.dma_start(v_rec[:], v_T).then_inc(S["weights"], 16)
            with sp.Fori(0, n_chunks) as i:
                at_x, at_ok = sp.snap(i * HPIX), sp.snap(i * (TILES * (WINS + 1)))
                sp.wait_ge(S["pre_cent"], i)
                sp.wait_ge(S["xres_ready"], i)
                sp.wait_ge(S["pre_mean"], i)
                sp.dma_start(xh[:], x_halo[:, bass.ds(at_x, HPIX)]).then_inc(S["x_loaded"], 16)
                sp.wait_ge(S["rsv_ready"], i)
                sp.wait_ge(S["cnt_ready"], i)
                sp.dma_start(ok[:].rearrange("p t w -> p (t w)"), valid[:, bass.ds(at_ok, TILES * (WINS + 1))])\
                    .then_inc(S["ok_loaded"], 16)
            sp.wait_ge(S["xb_stored"], 16 * n_chunks)
            sp.wait_ge(S["wx_stored"], 16 * n_chunks)
            scan_sp(sp)

        @block.gpsimd
        def _(pl):
            n = [0]

            def done(ins):
                n[0] += 1
                ins.then_inc(S["consts"], 1)
                pl.wait_ge(S["consts"], n[0])
            done(pl.memset(mean_w[:], 1.0 / P))
            done(pl.memset(minus_half[:], -0.5))
            done(pl.memset(k_pad[:], 0.0))
            done(pl.memset(v_pad[:], 0.0))
            for m in (ident, ident_b):
                done(pl.memset(m[:], 0.0))
                done(pl.affine_select(out=m[:], in_=m[:], compare_op=ALU.not_equal, fill=1.0, base=0,
                                      pattern=[[-1, P]], channel_multiplier=1))
            done(pl.memset(sel[:], 0.0))
            done(pl.affine_select(out=sel[:], in_=sel[:], compare_op=ALU.not_equal, fill=1.0, base=0,
                                  pattern=[[-1, 2]], channel_multiplier=1))
            done(pl.memset(head_sum[:], 0.0))
            for m in range(4):
                part = head_sum[:, m, 8 * m:8 * m + HEADS]
                done(pl.memset(part, 1.0))
                done(pl.affine_select(out=part, in_=part, compare_op=ALU.is_ge, fill=0.0, base=0,
                                      pattern=[[-HD, HEADS]], channel_multiplier=1))
                done(pl.affine_select(out=part, in_=part, compare_op=ALU.is_ge, fill=0.0, base=HD - 1,
                                      pattern=[[HD, HEADS]], channel_multiplier=-1))
            done(pl.memset(spread[:], 0.0))
            for s in range(PARTS):
                sp4 = spread[:].rearrange("p d (h c) -> p d h c", c=HD)
                done(pl.affine_select(out=sp4, in_=sp4, compare_op=ALU.not_equal, fill=1.0,
                                      base=-HEADS * s, pattern=[[-PARTS * HEADS, NB], [-1, HEADS], [0, HD]],
                                      channel_multiplier=1))
            for e in range(EXPERTS):
                done(pl.memset(rank[:, :, e:e + 1], float(e - EXPERTS)))
            assert n[0] == CONSTS

            def power(tag, out_, in_, i):
                pl.wait_ge(S[tag + "_v"], i + 1)
                pl.tensor_tensor(out_, in_, minus_half[:, 0:in_.shape[1]], ALU.pow).then_inc(S[tag + "_rs"], 1)

            with pl.Fori(0, n_chunks) as i:
                pl.wait_ge(S["pre_bc"], i)
                power("pre", rs0[:], var0[:], i)
                pl.wait_ge(S["k_ready"], i + 1)
                pl.wait_ge(S["q_ready"], i + 1)
                for n_, kk in enumerate(BY_POOL):
                    if n_ >= POOL_RING:
                        pl.wait_ge(S["reduced"], i * OFFS + BY_POOL[n_ - POOL_RING] + 1)
                    pl.tensor_tensor(rows(prod_p[:, n_ % POOL_RING, :]), rows(q[:]), head_shift(k_pad, SEQ[kk]),
                                     ALU.mult).then_inc(S["prod_pool"], 1)
                for dy in range(NB):
                    pl.wait_ge(S["ev_ready"], i * OFFS + NB * (dy + 1))
                    e, a, o = ev[:, dy % 2], hs_a[:, dy % 2], hs[:, dy]
                    c = i * 5 * NB + 5 * dy
                    if dy >= 2:
                        pl.wait_ge(S["hsum_step"], c - 5)
                    pl.tensor_tensor(a[:, 0, :], e[:, 1, :], e[:, 2, :], ALU.add).then_inc(S["hsum_step"], 1)
                    pl.tensor_tensor(a[:, 1, :], e[:, 3, :], e[:, 4, :], ALU.add).then_inc(S["hsum_step"], 1)
                    pl.wait_ge(S["hsum_step"], c + 1)
                    pl.tensor_tensor(o[:, 0, :], e[:, 0, :], a[:, 0, :], ALU.add).then_inc(S["hsum_step"], 1)
                    pl.tensor_tensor(o[:, 1, :], e[:, 3, :], a[:, 0, :], ALU.add).then_inc(S["hsum_step"], 1)
                    pl.wait_ge(S["hsum_step"], c + 2)
                    pl.tensor_tensor(o[:, 2, :], e[:, 2, :], a[:, 1, :], ALU.add).then_inc(S["hsum_step"], 1)
                pl.wait_ge(S["vary_ready"], i + 1)
                pl.tensor_tensor(rsy[:].rearrange("p t w -> p (t w)"), vary[:], minus_half[:], ALU.pow)\
                    .then_inc(S["rsy_ready"], 1)
                for tag in ("lnA", "lnB", "lnC"):
                    pl.wait_ge(S["lnC_bc" if tag == "lnA" else "lnA_bc" if tag == "lnB" else "lnB_bc"], i if tag == "lnA" else i + 1)
                    power(tag, rs[:], var[:], i)
            pl.wait_ge(S["bn_v"], 1)
            pl.tensor_tensor(tiny[:, 1:2], tiny[:, 0:1], minus_half[:, 0:1], ALU.pow).then_inc(S["bn_rs"], 1)
            scan_pool(pl)

        @block.tensor
        def _(pe):
            def turn(dst, src, idn):
                return pe.matmul(dst, src, idn, start=True, stop=True, is_transpose=True)

            def ln_pe(tag, x, ready, i):
                pe.wait_ge(S[ready], i + 1)
                pe.matmul(psA[:, 0, :], mean_w[:], x[:], start=True, stop=True).then_inc(S[tag + "_mean"], 1)
                pe.wait_ge(S[tag + "_cent"], i + 1)
                pe.wait_ge(S[tag + "_sq"], i + 1)
                for t in range(TILES):
                    m = pe.matmul(psA[:, 0, t:t + 1], sq[:, P * t:P * t + P], mean_w[:, 0:1], start=True, stop=True)
                m.then_inc(S[tag + "_var"], 1)
                pe.wait_ge(S[tag + "_v"], i + 1)
                pe.wait_ge(S[tag + "_rs"], i + 1)
                for t in range(TILES):
                    m = turn(psA[:, 0, P * t:P * t + P], rs[:, t:t + 1].to_broadcast([P, P]), ident[:])
                m.then_inc(S[tag + "_bc"], 1)

            pe.wait_ge(S["consts"], CONSTS)
            pe.wait_ge(S["weights"], 16 * LOADS)
            for n in range(3):
                pe.matmul(psA[:, 0, n:n + 1], wqkv[:, n, :], cols[:, 1:2], start=True, stop=True)
            pe.matmul(psA[:, 0, 4:5], mean_w[:], cols[:, 2:3], start=True, stop=True).then_inc(S["setup_pe"], 1)
            for n in range(CONV_STEPS):
                pe.wait_ge(S["setup_dve"], n + 1)
                pe.matmul(psB[:, n % 2, 0:P], conv_bT[:], conv_s[:, n, :], start=True, stop=True).then_inc(S["setup_pe"], 1)
            pe.wait_ge(S["setup_dve"], CONV_STEPS + 1)
            turn(psB[:, 0, 0:P], conv_s[:, CONV_STEPS, :], ident[:]).then_inc(S["setup_pe"], 1)
            pe.wait_ge(S["w_ready"], 1)

            with pe.Fori(0, n_chunks) as i:
                pe.wait_ge(S["x_loaded"], 16 * (i + 1))
                pe.wait_ge(S["stats_ready"], i)
                pe.wait_ge(S["wx_ready"], i)
                for h in range(2):
                    m = pe.matmul(psA[:, h, 0:HALF], mean_w[:], xh[:, h * HALF:(h + 1) * HALF], start=True, stop=True)
                m.then_inc(S["pre_mean"], 1)
                pe.wait_ge(S["pre_cent"], i + 1)
                pe.wait_ge(S["pre_sq"], i + 1)
                for t in range(HTILES):
                    m = pe.matmul(psA[:, 0, t:t + 1], sq0[:, P * t:P * t + P], mean_w[:, 0:1], start=True, stop=True)
                m.then_inc(S["pre_var"], 1)
                pe.wait_ge(S["pre_v"], i + 1)
                pe.wait_ge(S["pre_rs"], i + 1)
                for t in range(HTILES):
                    m = turn(psA[:, t // 3, P * (t % 3):P * (t % 3) + P], rs0[:, t:t + 1].to_broadcast([P, P]), ident[:])
                m.then_inc(S["pre_bc"], 1)
                pe.wait_ge(S["pre_xn"], i + 1)
                for h in range(2):
                    m = pe.matmul(psA[:, h, 0:HALF], wqkv[:, 1, :], xc0[:, h * HALF:(h + 1) * HALF], start=True, stop=True)
                m.then_inc(S["k_mm"], 1)
                pe.wait_ge(S["k_ready"], i + 1)
                pe.matmul(psA[:, 0, :], wqkv[:, 0, :], xc0[:, HALO * IMG:HALO * IMG + PIX], start=True, stop=True)\
                    .then_inc(S["q_mm"], 1)
                pe.wait_ge(S["q_ready"], i + 1)
                for h in range(2):
                    m = pe.matmul(psA[:, h, 0:HALF], wqkv[:, 2, :], xc0[:, h * HALF:(h + 1) * HALF], start=True, stop=True)
                m.then_inc(S["v_mm"], 1)

                pe.wait_ge(S["u_ready"], i * WINS)
                for kk, off in enumerate(SEQ):
                    if kk in BY_DVE:
                        n = BY_DVE.index(kk)
                        pe.wait_ge(S["prod_dve"], i * len(BY_DVE) + n + 1)
                        src = prod_d[:, n % DVE_RING, :]
                    else:
                        n = BY_POOL.index(kk)
                        pe.wait_ge(S["prod_pool"], i * len(BY_POOL) + n + 1)
                        src = prod_p[:, n % POOL_RING, :]
                    T, g, m4 = off // 16, off % 16 // 4, off % 4
                    last = m4 == 3 or off == OFFS - 1
                    pe.matmul(psB[32 * g:32 * g + 32, T, :], head_sum[:, m4, :], src, start=m4 == 0, stop=last)\
                        .then_inc(S["reduced"], 1)
                pe.wait_ge(S["eT_ready"], i * 4)
                for T in range(2):
                    n = P if T == 0 else OFFS * HEADS - P
                    pe.wait_ge(S["s2_ready"], 2 * i + T + 1)
                    for t in range(TILES):
                        m = turn(psS[:, t, P * T:P * T + n], s2[0:n, T, P * t:P * t + P], ident[0:n, 0:n])
                m.then_inc(S["s_turned"], 1)
                pe.wait_ge(S["es_ready"], i + 1)
                pe.wait_ge(S["e_hi"], i + 1)
                pe.wait_ge(S["e_mid"], i + 1)
                pe.wait_ge(S["e_lo"], i + 1)
                ge, gr = NB * PARTS * HEADS, KW * PARTS * HEADS
                for g in range(4):
                    for t in range(TILES):
                        c = PIX * g + P * t
                        m = turn(psT[0:ge, c:c + P], e3[:, t, NB * g:NB * g + NB].rearrange("p o s h -> p (o s h)"), ident_b[:])
                    if g % 2:
                        m.then_inc(S["e_turned"], 1)
                pe.wait_ge(S["eT_ready"], 4 * i + 1)
                for t in range(TILES):
                    m = turn(psT[0:ge, P * t:P * t + P], e3[:, t, NB * 4:NB * 5].rearrange("p o s h -> p (o s h)"), ident_b[:])
                m.then_inc(S["e_turned"], 1)
                pe.wait_ge(S["r_hi"], i + 1)
                pe.wait_ge(S["r_mid"], i + 1)
                pe.wait_ge(S["r_lo"], i + 1)
                for g in range(KW):
                    if g == 1:
                        pe.wait_ge(S["eT_ready"], 4 * i + 2)
                    for t in range(TILES):
                        c = PIX * (g + 1) + P * t
                        m = turn(psT[0:gr, c:c + P], r3[:, t, KW * g:KW * g + KW].rearrange("p o s h -> p (o s h)"), ident_b[:])
                m.then_inc(S["e_turned"], 1)
                pe.wait_ge(S["s2_ready"], 2 * i + 2)
                pe.wait_ge(S["eT_ready"], 4 * i + 3)
                for o in range(OFFS):
                    if o >= 2:
                        pe.wait_ge(S["ev_ready"], i * OFFS + o - 1)
                    pe.matmul(psB[:, o % 2, :], spread[0:ge, o % NB, :], eT[:, o // NB, :], start=True, stop=True)\
                        .then_inc(S["e_spread"], 1)
                pe.wait_ge(S["eT_ready"], 4 * i + 4)

                def r_spread(n):
                    b = (OFFS + n) % 2
                    if n < 2:
                        pe.wait_ge(S["ev_ready"], (i + 1) * OFFS - 1 + n)
                    else:
                        pe.wait_ge(S["win_ready"], i * WINS + n - 1)
                    pe.matmul(psB[:, b, :], spread[0:gr, n % KW, :], rT[:, n // KW, :], start=True, stop=True)\
                        .then_inc(S["r_spread"], 1)

                def var_y(n):
                    pe.wait_ge(S["sqy_ready"], i * WINS + n + 1)
                    for t in range(TILES):
                        m = pe.matmul(psF[:, t * WINS + n:t * WINS + n + 1], sqy[:, n % 2, P * t:P * t + P],
                                      mean_w[:, 0:1], start=True, stop=True)
                    m.then_inc(S["vary_mm"], 1)
                pe.wait_ge(S["x1_ready"], i)
                pe.wait_ge(S["rcT_ready"], i)
                r_spread(0)
                for n in range(WINS):
                    if n + 1 < WINS:
                        r_spread(n + 1)
                    pe.wait_ge(S["win_ready"], i * WINS + n + 1)
                    if n:
                        pe.wait_ge(S["sqy_ready"], i * WINS + n)
                    pe.matmul(psY, wproj[:], win[:, n // KW, n % KW, :], start=True, stop=True).then_inc(S["proj_mm"], 1)
                    if n:
                        var_y(n - 1)
                var_y(WINS - 1)
                pe.wait_ge(S["vary_ready"], i + 1)
                pe.wait_ge(S["rsv_ready"], i + 1)

                def rs_spread(n):
                    if n >= 2:
                        pe.wait_ge(S["u_ready"], i * WINS + n - 1)
                    for t in range(TILES):
                        m = turn(psB[:, n % 2, P * t:P * t + P], rsv[:, t, n:n + 1].to_broadcast([P, P]), ident[:])
                    m.then_inc(S["rs_spread"], 1)
                rs_spread(0)
                for n in range(WINS):
                    if n + 1 < WINS:
                        rs_spread(n + 1)
                    pe.wait_ge(S["u_ready"], i * WINS + n + 1)
                    pe.matmul(psF, wproj_g[:], win[:, n // KW, n % KW, :], start=n == 0, stop=False)
                pe.wait_ge(S["rc_ready"], i + 1)
                pe.wait_ge(S["cnt_ready"], i + 1)
                for t in range(TILES):
                    m = turn(psY[0:2, P * t:P * t + P], rc[:, t, :], ident[:])
                m.then_inc(S["rc_turned"], 1)
                pe.wait_ge(S["rcT_ready"], i + 1)
                pe.matmul(psF, brow[:], rcT[:], start=False, stop=True).then_inc(S["final_mm"], 1)

                pe.wait_ge(S["v_ready"], i + 1)
                ln_pe("lnA", x1, "x1_ready", i)
                pe.wait_ge(S["lnA_xn"], i + 1)
                for t in range(TILES):
                    m = pe.matmul(psA[:, 1, EXPERTS * t:EXPERTS * (t + 1)], xn[:, P * t:P * t + P], rw[:], start=True, stop=True)
                m.then_inc(S["logit_mm"], 1)
                pe.wait_ge(S["g_ready"], i + 1)
                for t in range(TILES):
                    m = turn(psA[0:EXPERTS, 0, P * t:P * t + P], gate[:, t, :], ident[:])
                m.then_inc(S["g_turned"], 1)
                pe.wait_ge(S["gT_ready"], i + 1)
                pe.matmul(psA[:, 1, :], eb[:], gT[:], start=True, stop=False)
                for e in range(EXPERTS):
                    if e:
                        pe.wait_ge(S["xg_ready"], i * EXPERTS + e)
                    for t in range(TILES):
                        m = turn(psA[:, 0, P * t:P * t + P], gate[:, t, e:e + 1].to_broadcast([P, P]), ident[:])
                    m.then_inc(S["g_spread"], 1)
                    if e:
                        pe.matmul(psA[:, 1, :], ew[:, e - 1, :], xg[:, (e - 1) % 2, :], start=False, stop=False)\
                            .then_inc(S["moe_mm"], 1)
                pe.wait_ge(S["xg_ready"], (i + 1) * EXPERTS)
                pe.matmul(psA[:, 1, :], ew[:, EXPERTS - 1, :], xg[:, (EXPERTS - 1) % 2, :], start=False, stop=True)\
                    .then_inc(S["moe_mm"], 1)
                ln_pe("lnB", xa, "xa_ready", i)
                pe.wait_ge(S["lnB_xn"], i + 1)
                pe.matmul(psA[:, 1, :], conv_mT[:], xn[:], start=True, stop=True).then_inc(S["conv_mm"], 1)
                ln_pe("lnC", xb, "xb_ready", i)
                pe.wait_ge(S["lnC_xn"], i + 1)
                pe.matmul(psA[:, 1, :], w_in[:], xn[:], start=True, stop=True).then_inc(S["wx_mm"], 1)
            scan_pe(pe)

        @block.scalar
        def _(ac):
            def ln_act(tag, i):
                ac.wait_ge(S[tag + "_cent"], i + 1)
                ac.activation(sq[:], xc[:], ACT.Square).then_inc(S[tag + "_sq"], 1)
            ac.wait_ge(S["w_ready"], 1)
            with ac.Fori(0, n_chunks) as i:
                ac.wait_ge(S["x_loaded"], 16 * (i + 1))
                ac.wait_ge(S["x1_ready"], i)
                ac.activation(xres[:], xh[:, HALO * IMG:HALO * IMG + PIX], ACT.Copy).then_inc(S["xres_ready"], 1)
                ac.wait_ge(S["pre_cent"], i + 1)
                ac.activation(sq0[:], xc0[:], ACT.Square).then_inc(S["pre_sq"], 1)
                ac.wait_ge(S["k_mm"], i + 1)
                ac.wait_ge(S["prod_pool"], i * len(BY_POOL))
                ac.wait_ge(S["prod_dve"], i * len(BY_DVE))
                halves = psA[:, :, 0:HALF].rearrange("p b (r c) -> p b r c", c=IMG)
                ac.activation(k_pad[:, :, HALO:HALO + IMG].rearrange("p (b r) c -> p b r c", b=2), halves,
                              ACT.Identity, bias=bqkv[:, 1:2]).then_inc(S["k_ready"], 1)
                ac.wait_ge(S["q_mm"], i + 1)
                ac.activation(q[:], psA[:, 0, :], ACT.Identity, bias=bqkv[:, 0:1]).then_inc(S["q_ready"], 1)
                ac.wait_ge(S["v_mm"], i + 1)
                ac.wait_ge(S["ev_ready"], i * OFFS)
                ac.activation(v_pad[:, :, HALO:HALO + IMG].rearrange("p (b r) c -> p b r c", b=2), halves,
                              ACT.Identity, bias=bqkv[:, 2:3]).then_inc(S["v_ready"], 1)
                ac.wait_ge(S["reduced"], i * OFFS + 16)
                ac.activation(s2[:, 0, :], psB[:, 0, :], ACT.Copy).then_inc(S["s2_ready"], 1)
                ac.wait_ge(S["reduced"], i * OFFS + OFFS)
                n = OFFS * HEADS - P
                ac.activation(s2[0:n, 1, :], psB[0:n, 1, :], ACT.Copy).then_inc(S["s2_ready"], 1)
                ac.wait_ge(S["es_ready"], i + 1)
                ac.activation(e32[:], es[:], ACT.Exp).then_inc(S["e_ready"], 1)
                ac.wait_ge(S["e_ready"], i + 1)
                to = e3[:].rearrange("p t o s h -> p (t o) s h")
                ac.activation(to[:, :, 0, :], e32[:].rearrange("p t o h -> p (t o) h"), ACT.Copy).then_inc(S["e_hi"], 1)
                ac.wait_ge(S["e_rest"], i + 1)
                ac.activation(to[:, :, 1, :], erest[:].rearrange("p t o h -> p (t o) h"), ACT.Copy).then_inc(S["e_mid"], 1)
                ac.wait_ge(S["r_ready"], i + 1)
                to = r3[:].rearrange("p t o s h -> p (t o) s h")
                ac.activation(to[:, :, 0, :], rden[:].rearrange("p t o h -> p (t o) h"), ACT.Copy).then_inc(S["r_hi"], 1)
                ac.wait_ge(S["r_rest"], i + 1)
                ac.activation(to[:, :, 1, :], rrest[:].rearrange("p t o h -> p (t o) h"), ACT.Copy).then_inc(S["r_mid"], 1)
                ge, gr = NB * PARTS * HEADS, KW * PARTS * HEADS
                ac.wait_ge(S["e_turned"], 4 * i + 1)
                ac.activation(eT[:, 0:2, :], psT[0:ge, 0:2 * PIX].rearrange("p (g n) -> p g n", n=PIX), ACT.Copy)\
                    .then_inc(S["eT_ready"], 1)
                ac.wait_ge(S["e_turned"], 4 * i + 2)
                ac.activation(eT[:, 2:4, :], psT[0:ge, 2 * PIX:4 * PIX].rearrange("p (g n) -> p g n", n=PIX), ACT.Copy)\
                    .then_inc(S["eT_ready"], 1)
                ac.wait_ge(S["e_turned"], 4 * i + 4)
                ac.activation(eT[:, 4, :], psT[0:ge, 0:PIX], ACT.Copy).then_inc(S["eT_ready"], 1)
                ac.activation(rT[:], psT[0:gr, PIX:4 * PIX].rearrange("p (g n) -> p g n", n=PIX), ACT.Copy)\
                    .then_inc(S["eT_ready"], 1)
                for n in range(WINS):
                    ac.wait_ge(S["proj_mm"], i * WINS + n + 1)
                    if n >= 2:
                        ac.wait_ge(S["vary_mm"], i * WINS + n - 1)
                    ac.activation(sqy[:, n % 2, :], psY, ACT.Square, bias=bproj_c[:]).then_inc(S["sqy_ready"], 1)
                ac.wait_ge(S["rc_turned"], i + 1)
                ac.activation(rcT[:], psY[0:2, :], ACT.Copy).then_inc(S["rcT_ready"], 1)
                ln_act("lnA", i)
                ac.wait_ge(S["gap_ready"], i + 1)
                ac.activation(top[:, 3, :], top[:, 2, :], ACT.Exp).then_inc(S["exp_ready"], 1)
                ac.wait_ge(S["g_turned"], i + 1)
                ac.activation(gT[:], psA[0:EXPERTS, 0, :], ACT.Copy).then_inc(S["gT_ready"], 1)
                ln_act("lnB", i)
                ln_act("lnC", i)
                ac.dma_start(xb_dram[:, bass.ds(i * PIX, PIX)], xb[:]).then_inc(S["xb_stored"], 16)
                ac.wait_ge(S["wx_mm"], i + 1)
                ac.wait_ge(S["stats_ready"], i + 1)
                ac.wait_ge(S["wx_stored"], 16 * i)
                ac.activation(wx[:], psA[:, 1, :], ACT.Copy).then_inc(S["wx_ready"], 1)
                ac.wait_ge(S["wx_ready"], i + 1)
                ac.dma_start(wx_dram[:, bass.ds(i * PIX, PIX)], wx[:]).then_inc(S["wx_stored"], 16)
            scan_act(ac)

        @block.vector
        def _(ve):
            n_setup = [0]

            def own(ins):
                n_setup[0] += 1
                ins.then_inc(S["w_scaled"], 1)
                ve.wait_ge(S["w_scaled"], n_setup[0])
            ve.wait_ge(S["weights"], 16 * LOADS)
            ve.wait_ge(S["consts"], CONSTS)
            own(ve.tensor_scalar(conv_bT[:], ident[:], 0.95, None, ALU.mult))
            own(ve.scalar_tensor_tensor(out=conv_bT[:], in0=conv_mT[:], scalar=0.025, in1=conv_bT[:], op0=ALU.mult, op1=ALU.add))
            ve.tensor_copy(conv_s[:, 0, :], conv_a[:]).then_inc(S["setup_dve"], 1)
            ve.wait_ge(S["setup_pe"], 1)
            own(ve.tensor_copy(bqkv[:], psA[:, 0, 0:3]))
            own(ve.tensor_scalar(bqkv[:, 0:1], bqkv[:, 0:1], HD ** -0.5, None, ALU.mult))
            own(ve.tensor_tensor(bproj_c[:], cols[:, 2:3], psA[:, 0, 4:5], ALU.subtract))
            own(ve.tensor_scalar(wqkv[:], wqkv[:], cols[:, 0:1], None, ALU.mult))
            own(ve.tensor_scalar(wqkv[:, 0, :], wqkv[:, 0, :], HD ** -0.5, None, ALU.mult))
            own(ve.tensor_reduce(tiny[:, 2:3], wproj[:], AX.X, ALU.add))
            own(ve.tensor_scalar(tiny[:, 2:3], tiny[:, 2:3], 1.0 / P, None, ALU.mult))
            own(ve.tensor_scalar(wproj[:], wproj[:], tiny[:, 2:3], None, ALU.subtract))
            own(ve.tensor_tensor(wproj_g[:], wproj[:], prow[:, 1, :], ALU.mult))
            own(ve.tensor_reduce(tiny[:, 3:4], prow[:, 0, :], AX.X, ALU.add))
            own(ve.tensor_scalar(tiny[:, 3:4], tiny[:, 3:4], 1.0 / P, None, ALU.mult))
            own(ve.tensor_scalar(prow[:, 0, :], prow[:, 0, :], tiny[:, 3:4], None, ALU.subtract))
            own(ve.tensor_tensor(prow[:, 0, :], prow[:, 0, :], prow[:, 1, :], ALU.mult))
            own(ve.tensor_scalar(brow[:], prow[0:2, 0, :], sel[:, 0:1], None, ALU.mult))
            own(ve.scalar_tensor_tensor(out=brow[:], in0=prow[0:2, 2, :], scalar=sel[:, 1:2], in1=brow[:], op0=ALU.mult, op1=ALU.add))
            for n in range(CONV_STEPS):
                ve.wait_ge(S["setup_pe"], n + 2)
                ve.scalar_tensor_tensor(out=conv_s[:, n + 1, :], in0=conv_a[:], scalar=0.025, in1=psB[:, n % 2, 0:P],
                                        op0=ALU.mult, op1=ALU.add).then_inc(S["setup_dve"], 1)
            ve.wait_ge(S["setup_pe"], CONV_STEPS + 2)
            ve.tensor_copy(conv_mT[:], psB[:, 0, 0:P]).then_inc(S["w_ready"], 1)

            def ln_dve(tag, x, i, eps):
                ve.wait_ge(S[tag + "_mean"], i + 1)
                ve.tensor_tensor(xc[:], x[:], psA[:, 0, :], ALU.subtract).then_inc(S[tag + "_cent"], 1)
                ve.wait_ge(S[tag + "_var"], i + 1)
                ve.tensor_scalar(var[:], psA[:, 0, 0:TILES], 1.0, eps, ALU.mult, ALU.add).then_inc(S[tag + "_v"], 1)
                ve.wait_ge(S[tag + "_bc"], i + 1)
                ve.tensor_tensor(xn[:], xc[:], psA[:, 0, :], ALU.mult).then_inc(S[tag + "_xn"], 1)

            with ve.Fori(0, n_chunks) as i:
                ve.wait_ge(S["pre_mean"], i + 1)
                ve.wait_ge(S["v_mm"], i)
                ve.wait_ge(S["q_mm"], i)
                xc2 = xc0[:].rearrange("p (b n) -> p b n", b=2)
                ve.tensor_tensor(xc2, xh[:].rearrange("p (b n) -> p b n", b=2), psA[:, :, 0:HALF], ALU.subtract)\
                    .then_inc(S["pre_cent"], 1)
                ve.wait_ge(S["pre_var"], i + 1)
                ve.tensor_scalar(var0[:], psA[:, 0, 0:HTILES], 1.0 + 1e-5, 1e-11, ALU.mult, ALU.add).then_inc(S["pre_v"], 1)
                ve.wait_ge(S["pre_bc"], i + 1)
                ve.wait_ge(S["pre_sq"], i + 1)
                ve.tensor_tensor(xc2, xc2, psA[:, :, 0:HALF], ALU.mult).then_inc(S["pre_xn"], 1)
                ve.wait_ge(S["k_ready"], i + 1)
                ve.wait_ge(S["q_ready"], i + 1)
                ve.wait_ge(S["reduced"], i * OFFS)
                for n, kk in enumerate(BY_DVE):
                    if n >= DVE_RING:
                        ve.wait_ge(S["reduced"], i * OFFS + BY_DVE[n - DVE_RING] + 1)
                    ve.tensor_tensor(rows(prod_d[:, n % DVE_RING, :]), rows(q[:]), head_shift(k_pad, SEQ[kk]),
                                     ALU.mult).then_inc(S["prod_dve"], 1)
                ve.wait_ge(S["s_turned"], i + 1)
                sc = psS[:, :, 0:OFFS * HEADS].rearrange("p t (o h) -> p t o h", h=HEADS)
                ve.tensor_reduce(smax[:], psS[:, :, 0:OFFS * HEADS].rearrange("p t (o h) -> p t h o", h=HEADS), AX.X, ALU.max)\
                    .then_inc(S["smax_ready"], 1)
                ve.wait_ge(S["smax_ready"], i + 1)
                ve.tensor_tensor(es[:], sc, smax[:].unsqueeze(2).to_broadcast([P, TILES, OFFS, HEADS]), ALU.subtract)\
                    .then_inc(S["es_ready"], 1)
                ve.wait_ge(S["e_ready"], i + 1)
                ee = e32[:].rearrange("p t (y x) h -> p (t y) (x h)", x=NB)
                c, span = 4 * i, KW * HEADS
                ve.tensor_tensor(dsum_a[:], ee[:, :, 0:span], ee[:, :, HEADS:HEADS + span], ALU.add).then_inc(S["dsum_step"], 1)
                ve.wait_ge(S["e_hi"], i + 1)
                ve.tensor_tensor(erest[:].rearrange("p t o h -> p (t o) h"), e32[:].rearrange("p t o h -> p (t o) h"),
                                 e3[:].rearrange("p t o s h -> p (t o) s h")[:, :, 0, :], ALU.subtract).then_inc(S["e_rest"], 1)
                ve.wait_ge(S["dsum_step"], c + 1)
                ve.tensor_tensor(dsum_h[:].rearrange("p t y n -> p (t y) n"), dsum_a[:], ee[:, :, 2 * HEADS:2 * HEADS + span],
                                 ALU.add).then_inc(S["dsum_step"], 1)
                ve.wait_ge(S["dsum_step"], c + 2)
                dh = dsum_h[:].rearrange("p t y n -> p t (y n)")
                span *= KW
                row = KW * HEADS
                ve.tensor_tensor(dsum_b[:], dh[:, :, 0:span], dh[:, :, row:row + span], ALU.add).then_inc(S["dsum_step"], 1)
                ve.wait_ge(S["dsum_step"], c + 3)
                ve.tensor_tensor(dsum[:], dsum_b[:], dh[:, :, 2 * row:2 * row + span], ALU.add).then_inc(S["dsum_step"], 1)
                ve.wait_ge(S["dsum_step"], c + 4)
                ve.reciprocal(rden[:].rearrange("p t w h -> p (t w h)"), dsum[:].rearrange("p t n -> p (t n)"))\
                    .then_inc(S["r_ready"], 1)
                ve.wait_ge(S["e_mid"], i + 1)
                e3v = e3[:].rearrange("p t o s h -> p (t o) s h")
                ve.tensor_tensor(e3v[:, :, 2, :], erest[:].rearrange("p t o h -> p (t o) h"), e3v[:, :, 1, :], ALU.subtract)\
                    .then_inc(S["e_lo"], 1)
                ve.wait_ge(S["r_ready"], i + 1)
                ve.wait_ge(S["r_hi"], i + 1)
                r3v = r3[:].rearrange("p t o s h -> p (t o) s h")
                rd = rden[:].rearrange("p t o h -> p (t o) h")
                rr = rrest[:].rearrange("p t o h -> p (t o) h")
                ve.tensor_tensor(rr, rd, r3v[:, :, 0, :], ALU.subtract).then_inc(S["r_rest"], 1)
                ve.wait_ge(S["r_rest"], i + 1)
                ve.wait_ge(S["r_mid"], i + 1)
                ve.tensor_tensor(r3v[:, :, 2, :], rr, r3v[:, :, 1, :], ALU.subtract).then_inc(S["r_lo"], 1)
                ve.wait_ge(S["v_ready"], i + 1)
                for o in range(OFFS):
                    dy = o // NB
                    ve.wait_ge(S["e_spread"], i * OFFS + o + 1)
                    if o % NB == 0 and dy >= 2:
                        ve.wait_ge(S["hsum_step"], i * 5 * NB + 5 * (dy - 1))
                    ve.tensor_tensor(rows(ev[:, dy % 2, o % NB, :]), rows(psB[:, o % 2, :]), head_shift(v_pad, o), ALU.mult)\
                        .then_inc(S["ev_ready"], 1)
                c = 5 * i
                ve.wait_ge(S["hsum_step"], (i + 1) * 5 * NB)
                ve.wait_ge(S["final_mm"], i)
                ve.tensor_tensor(vs[:, 0], hs[:, 1], hs[:, 2], ALU.add).then_inc(S["vsum_step"], 1)
                ve.tensor_tensor(vs[:, 1], hs[:, 3], hs[:, 4], ALU.add).then_inc(S["vsum_step"], 1)
                ve.wait_ge(S["vsum_step"], c + 1)
                ve.tensor_tensor(win[:, 0], hs[:, 0], vs[:, 0], ALU.add).then_inc(S["vsum_step"], 1)
                ve.tensor_tensor(win[:, 1], hs[:, 3], vs[:, 0], ALU.add).then_inc(S["vsum_step"], 1)
                ve.wait_ge(S["vsum_step"], c + 2)
                ve.tensor_tensor(win[:, 2], hs[:, 2], vs[:, 1], ALU.add).then_inc(S["vsum_step"], 1)
                for n in range(WINS):
                    ve.wait_ge(S["r_spread"], i * WINS + n + 1)
                    if n % KW == 0:
                        ve.wait_ge(S["vsum_step"], c + 3 + n // KW)
                    o_w = win[:, n // KW, n % KW, :]
                    ve.tensor_tensor(o_w, o_w, psB[:, (OFFS + n) % 2, :], ALU.mult).then_inc(S["win_ready"], 1)
                ve.wait_ge(S["vary_mm"], (i + 1) * WINS)
                ve.tensor_scalar(vary[:], psF[:, 0:TILES * WINS], 1.0, 1e-5, ALU.mult, ALU.add).then_inc(S["vary_ready"], 1)
                ve.wait_ge(S["rsy_ready"], i + 1)
                ve.wait_ge(S["ok_loaded"], 16 * (i + 1))
                ve.tensor_tensor(rsv[:], rsy[:], ok[:, :, 0:WINS], ALU.mult).then_inc(S["rsv_ready"], 1)
                ve.wait_ge(S["rsv_ready"], i + 1)
                ve.wait_ge(S["rc_turned"], i)
                ve.tensor_reduce(rc[:, :, 0:1], rsv[:], AX.X, ALU.add).then_inc(S["rc_ready"], 1)
                ve.tensor_copy(rc[:, :, 1:2], ok[:, :, WINS:]).then_inc(S["cnt_ready"], 1)
                for n in range(WINS):
                    ve.wait_ge(S["rs_spread"], i * WINS + n + 1)
                    ve.wait_ge(S["proj_mm"], (i + 1) * WINS)
                    o_w = win[:, n // KW, n % KW, :]
                    ve.tensor_tensor(o_w, o_w, psB[:, n % 2, :], ALU.mult).then_inc(S["u_ready"], 1)
                ve.wait_ge(S["final_mm"], i + 1)
                ve.wait_ge(S["xres_ready"], i + 1)
                ve.tensor_tensor(x1[:], xres[:], psF, ALU.add).then_inc(S["x1_ready"], 1)

                ln_dve("lnA", x1, i, 1e-5)
                k = [0]

                def step(ins):
                    k[0] += 1
                    ins.then_inc(S["route_step"], 1)
                    ve.wait_ge(S["route_step"], ROUTE * i + k[0])

                def per_tile(a):
                    return a.unsqueeze(2).to_broadcast([P, TILES, EXPERTS])
                ve.wait_ge(S["logit_mm"], i + 1)
                step(ve.tensor_tensor(logit[:], psA[:, 1, 0:TILES * EXPERTS].rearrange("p (t e) -> p t e", e=EXPERTS),
                                      rb[:].unsqueeze(1).to_broadcast([P, TILES, EXPERTS]), ALU.add))
                for n in range(2):
                    src = logit[:] if n == 0 else rt[:, 2]
                    step(ve.tensor_reduce(top[:, n, :], src, AX.X, ALU.max))
                    step(ve.tensor_tensor(rt[:, 0], src, per_tile(top[:, n, :]), ALU.is_equal))
                    step(ve.tensor_tensor(rt[:, 1], rt[:, 0], rank[:], ALU.mult))
                    step(ve.tensor_reduce(top[:, 4, :], rt[:, 1], AX.X, ALU.min))
                    step(ve.tensor_tensor(hot[:, n], rt[:, 1], per_tile(top[:, 4, :]), ALU.is_equal))
                    if n == 0:
                        step(ve.scalar_tensor_tensor(out=rt[:, 2], in0=hot[:, 0], scalar=-3e38, in1=logit[:],
                                                     op0=ALU.mult, op1=ALU.add))
                ve.tensor_tensor(top[:, 2, :], top[:, 1, :], top[:, 0, :], ALU.subtract).then_inc(S["gap_ready"], 1)
                ve.wait_ge(S["exp_ready"], i + 1)
                step(ve.tensor_scalar(top[:, 5, :], top[:, 3, :], 1.0, None, ALU.add))
                step(ve.reciprocal(top[:, 6, :], top[:, 5, :]))
                step(ve.tensor_tensor(top[:, 7, :], top[:, 3, :], top[:, 6, :], ALU.mult))
                step(ve.tensor_tensor(rt[:, 0], hot[:, 0], per_tile(top[:, 6, :]), ALU.mult))
                step(ve.tensor_tensor(rt[:, 1], hot[:, 1], per_tile(top[:, 7, :]), ALU.mult))
                assert k[0] == ROUTE
                ve.tensor_tensor(gate[:], rt[:, 0], rt[:, 1], ALU.add).then_inc(S["g_ready"], 1)
                ve.wait_ge(S["moe_mm"], EXPERTS * i)
                for e in range(EXPERTS):
                    ve.wait_ge(S["g_spread"], EXPERTS * i + e + 1)
                    if e >= 2:
                        ve.wait_ge(S["moe_mm"], EXPERTS * i + e - 1)
                    ve.tensor_tensor(xg[:, e % 2, :], xn[:], psA[:, 0, :], ALU.mult).then_inc(S["xg_ready"], 1)
                ve.wait_ge(S["moe_mm"], EXPERTS * (i + 1))
                ve.tensor_tensor(xa[:], x1[:], psA[:, 1, :], ALU.add).then_inc(S["xa_ready"], 1)
                ve.wait_ge(S["xa_ready"], i + 1)
                ln_dve("lnB", xa, i, 1e-6)
                ve.wait_ge(S["conv_mm"], i + 1)
                ve.wait_ge(S["xb_stored"], 16 * i)
                ve.tensor_tensor(xb[:], xa[:], psA[:, 1, :], ALU.add).then_inc(S["xb_ready"], 1)
                ve.wait_ge(S["xb_ready"], i + 1)
                ln_dve("lnC", xb, i, 1e-5)
                ve.wait_ge(S["wx_mm"], i + 1)
                ve.bn_stats(stats[:, bass.ds(i * 6, 6)], psA[:, 1, :]).then_inc(S["stats_ready"], 1)
            ve.wait_ge(S["stats_ready"], n_chunks)
            ve.bn_aggr(mv[:], stats[:, 0:6 * n_chunks]).then_inc(S["bn_step"], 1)
            ve.wait_ge(S["bn_step"], 1)
            ve.tensor_scalar(tiny[:, 0:1], mv[:, 1:2], 1.0, 1e-5, ALU.mult, ALU.add).then_inc(S["bn_v"], 1)
            ve.wait_ge(S["bn_rs"], 1)
            ve.tensor_tensor(tiny[:, 4:5], tiny[:, 1:2], cols[:, 3:4], ALU.mult).then_inc(S["bn_step"], 1)
            ve.wait_ge(S["bn_step"], 2)
            ve.tensor_tensor(tiny[:, 6:7], mv[:, 0:1], tiny[:, 4:5], ALU.mult).then_inc(S["bn_step"], 1)
            ve.wait_ge(S["bn_step"], 3)
            ve.tensor_tensor(tiny[:, 5:6], cols[:, 4:5], tiny[:, 6:7], ALU.subtract).then_inc(S["bn_step"], 1)
            ve.wait_ge(S["bn_step"], 4)
            scan_dve(ve)


_INS = ["x_halo", "valid", "w_qkvT", "w_projT", "b_proj", "ln1_g", "ln1_b", "ln2_g", "ln2_b", "router_w", "router_b",
        "expert_w", "expert_b", "conv", "convT", "w_T", "v_T", "gamma", "beta"]


def layouts(inputs):
    import numpy as np
    x = np.asarray(inputs["x"])
    xp = np.zeros((IMGS, P, IMG + 2 * HALO, IMG), x.dtype)
    xp[:, :, HALO:HALO + IMG] = x
    halo = np.stack([xp[:, :, r:r + HROWS] for r in range(0, IMG, ROWS)], 1)
    rr, cc = np.meshgrid(np.arange(IMG), np.arange(IMG), indexing="ij")
    last = IMG - KW
    mask = np.stack([(rr - 2 + a >= 0) & (rr - 2 + a <= last) & (cc - 2 + b >= 0) & (cc - 2 + b <= last)
                     for a in range(KW) for b in range(KW)], -1).astype(np.float32)
    mask = np.concatenate([mask, mask.sum(-1, keepdims=True)], -1)
    mask = mask.reshape(IMG // ROWS, TILES, P, WINS + 1).transpose(0, 2, 1, 3).reshape(IMG // ROWS, P, TILES * (WINS + 1))
    taps = np.asarray(inputs["L1_conv_weight"]).reshape(-1)
    padded = np.zeros(2 * P + 1, taps.dtype)
    padded[P - taps.size // 2:P - taps.size // 2 + taps.size] = taps
    at = P + np.arange(P)[None, :] - np.arange(P)[:, None]
    conv = padded[at]
    got = {
        "x_halo": halo.transpose(2, 0, 1, 3, 4).reshape(P, CHUNKS * HPIX),
        "valid": np.tile(mask, (IMGS, 1, 1)).transpose(1, 0, 2).reshape(P, -1),
        "w_qkvT": inputs["L0_conv_w_qkv"].T, "w_projT": inputs["L0_conv_w_proj"].T,
        "b_proj": inputs["L0_conv_b_proj"], "ln1_g": inputs["L0_conv_ln1_g"], "ln1_b": inputs["L0_conv_ln1_b"],
        "ln2_g": inputs["L0_conv_ln2_g"], "ln2_b": inputs["L0_conv_ln2_b"],
        "router_w": inputs["L0_ffn_router_w"], "router_b": inputs["L0_ffn_router_b"],
        "expert_w": inputs["L0_ffn_expert_w"], "expert_b": inputs["L0_ffn_expert_b"],
        "conv": conv, "convT": conv.T,
        "w_T": inputs["L1_ffn_W"].T, "v_T": inputs["L1_ffn_V"].T,
        "gamma": inputs["L1_ffn_gamma"], "beta": inputs["L1_ffn_beta"],
    }
    return {n: np.ascontiguousarray(got[n]) for n in _INS}


def kernel(**inputs):
    import concourse.bacc as _bacc
    from concourse.bass_utils import run_bass_kernel_spmd as _run

    nc = _bacc.Bacc("TRN2", target_bir_lowering=False, num_devices=1)
    arrays = layouts(inputs)
    args = [nc.dram_tensor(n, a.shape, mybir.dt.from_np(a.dtype), kind="ExternalInput").ap() for n, a in arrays.items()]
    out = nc.dram_tensor("out", (IMGS, P, STEPS), F32, kind="ExternalOutput").ap()
    program(nc, *args, out)
    r = _run(nc, [arrays], core_ids=[0])
    return r.results[0]["out"].reshape(IMGS, P, IMG, IMG)
```

```python
from contextlib import ExitStack

import concourse.bass as bass
from concourse import mybir

F32 = mybir.dt.float32
BF16 = mybir.dt.bfloat16
ALU = mybir.AluOpType
ACT = mybir.ActivationFunctionType
AX = mybir.AxisListType

P = 128
IMGS, IMG = 8, 64
ROWS = 8
PIX = ROWS * IMG
TILES = PIX // P
CHUNKS = IMGS * IMG // ROWS
HALO = 2
HROWS = ROWS + 2 * HALO
HPIX = HROWS * IMG
HTILES = HPIX // P
HALF = HPIX // 2
PADW = IMG + 2 * HALO
HEADS, HD = 8, 16
KW = 3
NB = 2 * KW - 1
OFFS = NB * NB
WINS = KW * KW
EXPERTS = 8
PARTS = 3
STEPS = IMG * IMG
CONV_STEPS = 20
ROUTE = 17
CONSTS = 35

SEQ = [4 * g + m for m in range(4) for g in range(4)] + [16, 20, 24, 17, 21, 18, 22, 19, 23]
BY_POOL = list(range(1, OFFS, 2))
BY_DVE = list(range(0, OFFS, 2))
DVE_RING, POOL_RING = 4, 7
POOL_ROWS = 3
DVE_ROWS = NB - POOL_ROWS

BLK = 128
HBLK = BLK // 2
PIECES = 8


def program(nc, x_halo, valid, w_qkvT, w_projT, b_proj, ln1_g, ln1_b, ln2_g, ln2_b, router_w, router_b,
            expert_w, expert_b, conv, convT, w_T, v_T, gamma, beta, out, n_chunks=CHUNKS,
            n_blocks=STEPS // BLK):
    wx_dram = nc.dram_tensor("wx_scratch", (P, CHUNKS * PIX), F32, kind="Internal").ap()
    xb_dram = nc.dram_tensor("xb_scratch", (P, CHUNKS * PIX), F32, kind="Internal").ap()
    with ExitStack() as ctx:
        def sb(name, shape, dt=F32):
            return ctx.enter_context(nc.sbuf_tensor(name, shape, dt))

        def sem(name):
            return ctx.enter_context(nc.semaphore(name))

        ident = sb("ident", [P, P])
        ident_b = sb("ident_b", [P, P], BF16)
        mean_w = sb("mean_w", [P, P])
        head_sum = sb("head_sum", [P, 4, 32])
        spread = sb("spread", [P, NB, P], BF16)
        minus_half = sb("minus_half", [P, 4 * WINS])
        rank = sb("rank", [P, TILES, EXPERTS])
        wqkv = sb("wqkv", [P, 3, P])
        bqkv = sb("bqkv", [P, 3])
        wproj = sb("wproj", [P, P])
        wproj_g = sb("wproj_g", [P, P])
        prow = sb("prow", [P, 3, P])
        brow = sb("brow", [2, P])
        sel = sb("sel", [2, 2])
        bproj_c = sb("bproj_c", [P, 1])
        cols = sb("cols", [P, 6])
        rw = sb("rw", [P, EXPERTS])
        rb = sb("rb", [P, EXPERTS])
        ew = sb("ew", [P, EXPERTS, P])
        eb = sb("eb", [EXPERTS, P])
        conv_a = sb("conv_a", [P, P])
        conv_bT = sb("conv_bT", [P, P])
        conv_mT = sb("conv_mT", [P, P])
        w_in = sb("w_in", [P, P])
        v_rec = sb("v_rec", [P, P])
        tiny = sb("tiny", [P, 8])

        xh = sb("xh", [P, HPIX])
        xres = sb("xres", [P, PIX])
        xc0 = sb("xc0", [P, HPIX])
        var0 = sb("var0", [P, HTILES])
        rs0 = sb("rs0", [P, HTILES])
        q = sb("q", [P, PIX])
        k_pad = sb("k_pad", [P, HROWS, PADW])
        v_pad = sb("v_pad", [P, HROWS, PADW])
        prod_d = sb("prod_d", [P, DVE_RING, PIX])
        prod_p = sb("prod_p", [P, POOL_RING, PIX])
        s2 = sb("s2", [P, 2, PIX])
        sq0 = s2[:].rearrange("p b n -> p (b n)")[:, 0:HPIX]
        smax = sb("smax", [P, TILES, HEADS])
        es = sb("es", [P, TILES, OFFS, HEADS])
        e32 = sb("e32", [P, TILES, OFFS, HEADS])
        erest = es
        e3 = sb("e3", [P, TILES, OFFS, PARTS, HEADS], BF16)
        dsum_a = sb("dsum_a", [P, TILES * NB, KW * HEADS])
        dsum_h = sb("dsum_h", [P, TILES, NB, KW * HEADS])
        dsum_b = sb("dsum_b", [P, TILES, KW * KW * HEADS])
        dsum = sb("dsum", [P, TILES, WINS * HEADS])
        rden = sb("rden", [P, TILES, WINS, HEADS])
        rrest = sb("rrest", [P, TILES, WINS, HEADS])
        r3 = sb("r3", [P, TILES, WINS, PARTS, HEADS], BF16)
        eT = sb("eT", [NB * PARTS * HEADS, NB, PIX], BF16)
        rT = sb("rT", [KW * PARTS * HEADS, KW, PIX], BF16)
        ev = sb("ev", [P, 2, NB, PIX])
        hs_a = sb("hs_a", [P, 2, 2, PIX])
        hs_b = sb("hs_b", [P, 2, PIX])
        hs = sb("hs", [P, NB, KW, PIX])
        vs = sb("vs", [P, 2, KW, PIX])
        win = sb("win", [P, KW, KW, PIX])
        win9 = win[:].rearrange("p a b n -> p (a b) n")
        ev_row = [ev[:, 0], ev[:, 1], win9[:, 0:NB], ev[:, 0], ev[:, 1]]
        conv_s = win[:].rearrange("p a b n -> p (a b n)")[:, 0:(CONV_STEPS + 1) * P]\
            .rearrange("p (k n) -> p k n", n=P)
        sqy = sb("sqy", [P, 2, PIX])
        ok = sb("ok", [P, TILES, WINS + 1])
        vary = sb("vary", [P, TILES * WINS])
        rsy = sb("rsy", [P, WINS * TILES])
        rsv = sb("rsv", [P, TILES, WINS])
        rc = sb("rc", [P, TILES, 2])
        rcT = sb("rcT", [2, PIX])
        x1 = sb("x1", [P, PIX])
        xc = sb("xc", [P, PIX])
        sq = sb("sq", [P, PIX])
        xn = sb("xn", [P, PIX])
        var = sb("var", [P, TILES])
        rs = sb("rs", [P, TILES])
        logit = sb("logit", [P, TILES, EXPERTS])
        hot = sb("hot", [P, 2, TILES, EXPERTS])
        rt = sb("rt", [P, 4, TILES, EXPERTS])
        top = sb("top", [P, 8, TILES])
        gate = sb("gate", [P, TILES, EXPERTS])
        gT = sb("gT", [EXPERTS, PIX])
        xg = sb("xg", [P, 2, PIX])
        xa = sb("xa", [P, PIX])
        xb = sb("xb", [P, PIX])
        wx = sb("wx", [P, PIX])
        stats = sb("stats", [P, CHUNKS * 6])
        mv = sb("mv", [P, 2])
        n = IMGS * BLK
        wxr, xbr, outb = [hs[:].rearrange("p a b n -> p (a b n)")[:, k * n:(k + 1) * n]
                          .rearrange("p (b t) -> p b t", t=BLK) for k in range(3)]
        z, y = [hs[:].rearrange("p a b n -> p (a b n)")[:, k * n:(k + 1) * n]
                .rearrange("p (h t b) -> p h t b", h=2, b=IMGS) for k in (3, 4)]

        ps = ctx.enter_context(nc.psum_tensor("ps", [P, 8, 512], F32))
        psA = ps[:, 0:2, :]
        psP = ps[:, 2:4, :]
        psS = ps[:, 2:4, :].rearrange("p b (t c) -> p (b t) c", c=256)
        psT = ps[:, 2:4, :].rearrange("p b c -> p (b c)").bitcast(BF16)
        psB = ps[:, 4:6, :]
        psE = ps[:, 4:8, :]
        psR = ps[:, 4:7, :]
        psY = ps[:, 6, :]
        psF = ps[:, 7, :]

        names = """consts weights w_scaled w_ready setup_pe setup_dve
            x_loaded ok_loaded xres_ready
            pre_mean pre_cent pre_sq pre_var pre_v pre_rs pre_bc pre_xn k_mm k_ready v_mm v_ready q_mm q_ready
            prod_dve prod_pool reduced s2_ready s_turned smax_ready es_ready e_ready e_hi e_rest e_mid e_lo
            dsum_step r_ready r_hi r_rest r_mid r_lo e_turned eT_ready e_spread ev_ready hsum_step hsum_dve vsum_step
            r_spread win_ready proj_mm sqy_ready vary_mm vary_ready rsy_ready rsv_ready rc_ready cnt_ready
            rc_turned rcT_ready rs_spread u_ready final_mm x1_ready
            lnA_mean lnA_cent lnA_sq lnA_var lnA_v lnA_rs lnA_bc lnA_xn
            lnB_mean lnB_cent lnB_sq lnB_var lnB_v lnB_rs lnB_bc lnB_xn
            lnC_mean lnC_cent lnC_sq lnC_var lnC_v lnC_rs lnC_bc lnC_xn
            logit_mm route_step gap_ready exp_ready g_ready g_turned gT_ready g_spread xg_ready moe_mm xa_ready
            conv_mm xb_ready wx_mm wx_ready stats_ready xb_stored wx_stored
            bn_step bn_v bn_rs z_loaded z_ready z_used step_mm y_ready res_loaded out_ready out_stored""".split()
        S = {n: sem(n) for n in names}
        block = ctx.enter_context(nc.Block())

        def head_shift(t, off):
            dy, dx = off // NB, off % NB
            return t[:, dy:dy + ROWS, dx:dx + IMG]

        def rows(a):
            return a.rearrange("p (r c) -> p r c", c=IMG)

        LOADS = 2 + 5 + 3 + 1 + 1 + 2 + 2 + 2

        MIX = 0
        COLS = MIX + OFFS
        VERT = COLS + 1
        NORM = VERT + 2
        SOFT = NORM + WINS
        SUM = SOFT + 1
        END = SUM + WINS
        F_MEAN, F_CENT, F_VAR, F_V, F_BC, F_XN, F_K, F_Q, F_VAL = 4, 7, 9, 11, 17, 18, 20, 22, COLS
        GROUPS = [range(4 * n, 4 * n + 4) for n in range(4)] + [range(16, 19), range(19, 21), range(21, 23), range(23, 25), []]
        A_SLOTS, B_SLOTS, C_SLOTS = (0, 1, 3, 4, 6, 7), (28, 29, 30, 31, 33, 34), (36, 38, 39, 40, 43, 44)
        LOGIT, ROUTE1, ROUTE2, G_TURN = 8, 10, 12, 13
        XG = [15, 17, 19, 21, 23, 24, 25, 26]
        AHEAD = 3
        VARY = [(0, 6), (6, WINS)]
        XA, XB, STATS = 27, 35, 46

        def rounds(eng, body):
            body(-1, False, True, False)
            body(0, True, n_chunks > 1, False)
            if n_chunks > 2:
                body(1, True, True, True)
            if n_chunks > 3:
                with eng.Fori(2, n_chunks - 1) as i:
                    body(i, True, True, True)
            if n_chunks > 1:
                body(n_chunks - 1, True, False, True)
            body(n_chunks, False, False, True)

        def dram_block(a, at, ahead):
            a = a.rearrange("p (b t) -> p b t", b=IMGS)
            return (a[:, :, BLK:] if ahead else a)[:, :, bass.ds(at, BLK)]

        def scan_sp(sp):
            def load_wx(halves, at, ahead):
                sp.wait_ge(S["z_ready"], halves)
                sp.dma_start(wxr, dram_block(wx_dram, at, ahead)).then_inc(S["z_loaded"], 16)

            def load_res(halves, at, ahead):
                sp.wait_ge(S["out_ready"], halves)
                sp.dma_start(xbr, dram_block(xb_dram, at, ahead)).then_inc(S["res_loaded"], 16)

            def store(at):
                sp.dma_start(out.rearrange("b c t -> c b t")[:, :, bass.ds(at, BLK)], outb)\
                    .then_inc(S["out_stored"], 16)
            load_wx(0, 0, False)
            load_res(0, 0, False)
            if n_blocks > 1:
                with sp.Fori(0, n_blocks - 1) as n:
                    at = sp.snap(n * BLK)
                    halves = sp.snap(n * 2 + 2)
                    load_wx(halves, at, True)
                    load_res(halves, at, True)
                    store(at)
            sp.wait_ge(S["out_ready"], 2 * n_blocks)
            store((n_blocks - 1) * BLK)
            sp.wait_ge(S["out_stored"], 16 * n_blocks)

        def scan_dve(ve):
            def half(n, h):
                ve.wait_ge(S["z_loaded"], 16 * (n + 1))
                ve.tensor_scalar(z[:, h], wxr[:, :, HBLK * h:HBLK * (h + 1)].rearrange("p b t -> p t b"),
                                 tiny[:, 4:5], tiny[:, 5:6], ALU.mult, ALU.add).then_inc(S["z_ready"], 1)
            half(0, 0)
            half(0, 1)
            if n_blocks > 1:
                with ve.Fori(1, n_blocks) as n:
                    for h in range(2):
                        ve.wait_ge(S["z_used"], 2 * n + h - 1)
                        half(n, h)

        def scan_pe(pe):
            def preload(h, piece):
                c = piece * PIX // PIECES
                m = pe.matmul(ps[:, h, c:c + PIX // PIECES], ident[:],
                              z[:, h].rearrange("p t b -> p (t b)")[:, c:c + PIX // PIECES],
                              start=piece == 0, stop=True, skip_group_check=True)
                if piece == PIECES - 1:
                    m.then_inc(S["z_used"], 1)

            def steps(n, h, last):
                every = HBLK // PIECES
                for j in range(HBLK):
                    pe.wait_ge(S["y_ready"], (2 * n + h) * HBLK + j + 1)
                    prev = y[:, h, j - 1, :] if j else y[:, 1 - h, HBLK - 1, :]
                    for g in range(4):
                        m = pe.matmul(ps[32 * g:32 * g + 32, h, IMGS * j:IMGS * (j + 1)], v_rec[:, 32 * g:32 * g + 32],
                                      prev, start=False, stop=True, skip_group_check=True)
                    m.then_inc(S["step_mm"], 1)
                    if j % every == every // 2 and not last:
                        if j == every // 2:
                            pe.wait_ge(S["z_ready"], 2 * n + h + 2)
                        preload(1 - h, j // every)
            pe.wait_ge(S["y_ready"], 1)
            pe.wait_ge(S["z_ready"], 1)
            for piece in range(PIECES):
                preload(0, piece)
            if n_blocks > 1:
                with pe.Fori(0, n_blocks - 1) as n:
                    steps(n, 0, False)
                    steps(n, 1, False)
            steps(n_blocks - 1, 0, False)
            steps(n_blocks - 1, 1, True)

        def scan_act(ac):
            def steps(n, h, first):
                if not first:
                    ac.wait_ge(S["out_ready"], 2 * n + h - 1)
                for j in range(HBLK):
                    ac.wait_ge(S["step_mm"], (2 * n + h) * HBLK + j + 1)
                    ac.activation(y[:, h, j, :], ps[:, h, IMGS * j:IMGS * (j + 1)], ACT.Sigmoid).then_inc(S["y_ready"], 1)
            steps(0, 0, True)
            steps(0, 1, True)
            if n_blocks > 1:
                with ac.Fori(1, n_blocks) as n:
                    steps(n, 0, False)
                    steps(n, 1, False)

        def scan_pool(pl):
            pl.memset(y[:, 1], 0.0).then_inc(S["y_ready"], 1)

            def add(n):
                pl.wait_ge(S["res_loaded"], 16 * (n + 1))
                for h in range(2):
                    pl.wait_ge(S["y_ready"], (2 * n + h + 1) * HBLK + 1)
                    pl.tensor_tensor(outb[:, :, HBLK * h:HBLK * (h + 1)], xbr[:, :, HBLK * h:HBLK * (h + 1)],
                                     y[:, h].rearrange("p t b -> p b t"), ALU.add).then_inc(S["out_ready"], 1)
            add(0)
            if n_blocks > 1:
                with pl.Fori(1, n_blocks) as n:
                    pl.wait_ge(S["out_stored"], 16 * n)
                    add(n)

        @block.sync
        def _(sp):
            sp.dma_start(wqkv[:], w_qkvT).then_inc(S["weights"], 16)
            sp.dma_start(wproj[:], w_projT).then_inc(S["weights"], 16)
            for n, v in enumerate((ln1_g, ln1_b, b_proj, gamma, beta)):
                sp.dma_start(cols[:, n:n + 1], v.rearrange("(p a) -> p a", a=1)).then_inc(S["weights"], 16)
            for n, v in enumerate((b_proj, ln2_g, ln2_b)):
                sp.dma_start(prow[:, n, :], v.partition_broadcast(P)).then_inc(S["weights"], 16)
            sp.dma_start(rb[:], router_b.partition_broadcast(P)).then_inc(S["weights"], 16)
            sp.dma_start(rw[:], router_w).then_inc(S["weights"], 16)
            sp.dma_start(ew[:], expert_w.rearrange("e d c -> d e c")).then_inc(S["weights"], 16)
            sp.dma_start(eb[:], expert_b).then_inc(S["weights"], 16)
            sp.dma_start(conv_a[:], conv).then_inc(S["weights"], 16)
            sp.dma_start(conv_mT[:], convT).then_inc(S["weights"], 16)
            sp.dma_start(w_in[:], w_T).then_inc(S["weights"], 16)
            sp.dma_start(v_rec[:], v_T).then_inc(S["weights"], 16)
            def load(i, at_x):
                if not isinstance(i, int) or i:
                    sp.wait_ge(S["pre_cent"], i)
                    sp.wait_ge(S["xres_ready"], i)
                    sp.wait_ge(S["pre_mean"], i)
                sp.dma_start(xh[:], x_halo[:, bass.ds(at_x, HPIX)]).then_inc(S["x_loaded"], 16)

            def load_mask(i, at_ok):
                if not isinstance(i, int) or i:
                    sp.wait_ge(S["rsv_ready"], i)
                    sp.wait_ge(S["cnt_ready"], i)
                sp.dma_start(ok[:].rearrange("p t w -> p (t w)"), valid[:, bass.ds(at_ok, TILES * (WINS + 1))])\
                    .then_inc(S["ok_loaded"], 16)

            def store(i, at):
                sp.wait_ge(S["xb_ready"], i + 1)
                sp.dma_start(xb_dram[:, bass.ds(at, PIX)], xb[:]).then_inc(S["xb_stored"], 16)
                sp.wait_ge(S["wx_ready"], i + 1)
                sp.dma_start(wx_dram[:, bass.ds(at, PIX)], wx[:]).then_inc(S["wx_stored"], 16)
            mask = TILES * (WINS + 1)
            load(0, 0)
            load_mask(0, 0)
            for i in (1, 2):
                if i < n_chunks:
                    load(i, i * HPIX)
                    load_mask(i, i * mask)
            if n_chunks > 3:
                with sp.Fori(3, n_chunks) as i:
                    at_x, at_ok, at = sp.snap(i * HPIX), sp.snap(i * mask), sp.snap(i * PIX - 3 * PIX)
                    before = sp.snap(i - 2)
                    load(i, at_x)
                    sp.wait_ge(S["xb_ready"], before)
                    sp.dma_start(xb_dram[:, bass.ds(at, PIX)], xb[:]).then_inc(S["xb_stored"], 16)
                    sp.wait_ge(S["wx_ready"], before)
                    sp.dma_start(wx_dram[:, bass.ds(at, PIX)], wx[:]).then_inc(S["wx_stored"], 16)
                    load_mask(i, at_ok)
            for i in range(max(n_chunks - 3, 0), n_chunks):
                store(i, i * PIX)
            sp.wait_ge(S["xb_stored"], 16 * n_chunks)
            sp.wait_ge(S["wx_stored"], 16 * n_chunks)
            scan_sp(sp)

        @block.gpsimd
        def _(pl):
            n = [0]

            def done(ins):
                n[0] += 1
                ins.then_inc(S["consts"], 1)
                pl.wait_ge(S["consts"], n[0])
            done(pl.memset(mean_w[:], 1.0 / P))
            done(pl.memset(minus_half[:], -0.5))
            done(pl.memset(k_pad[:], 0.0))
            done(pl.memset(v_pad[:], 0.0))
            for m in (ident, ident_b):
                done(pl.memset(m[:], 0.0))
                done(pl.affine_select(out=m[:], in_=m[:], compare_op=ALU.not_equal, fill=1.0, base=0,
                                      pattern=[[-1, P]], channel_multiplier=1))
            done(pl.memset(sel[:], 0.0))
            done(pl.affine_select(out=sel[:], in_=sel[:], compare_op=ALU.not_equal, fill=1.0, base=0,
                                  pattern=[[-1, 2]], channel_multiplier=1))
            done(pl.memset(head_sum[:], 0.0))
            for m in range(4):
                part = head_sum[:, m, 8 * m:8 * m + HEADS]
                done(pl.memset(part, 1.0))
                done(pl.affine_select(out=part, in_=part, compare_op=ALU.is_ge, fill=0.0, base=0,
                                      pattern=[[-HD, HEADS]], channel_multiplier=1))
                done(pl.affine_select(out=part, in_=part, compare_op=ALU.is_ge, fill=0.0, base=HD - 1,
                                      pattern=[[HD, HEADS]], channel_multiplier=-1))
            done(pl.memset(spread[:], 0.0))
            for s in range(PARTS):
                sp4 = spread[:].rearrange("p d (h c) -> p d h c", c=HD)
                done(pl.affine_select(out=sp4, in_=sp4, compare_op=ALU.not_equal, fill=1.0,
                                      base=-HEADS * s, pattern=[[-PARTS * HEADS, NB], [-1, HEADS], [0, HD]],
                                      channel_multiplier=1))
            for e in range(EXPERTS):
                done(pl.memset(rank[:, :, e:e + 1], float(e - EXPERTS)))
            assert n[0] == CONSTS

            def power(tag, out_, in_, i):
                pl.wait_ge(S[tag + "_v"], i + 1)
                pl.tensor_tensor(out_, in_, minus_half[:, 0:in_.shape[1]], ALU.pow).then_inc(S[tag + "_rs"], 1)

            def products(i, which):
                for n in which:
                    pl.wait_ge(S["k_ready"], i + 1)
                    pl.wait_ge(S["q_ready"], i + 1)
                    if n >= POOL_RING:
                        pl.wait_ge(S["reduced"], i * OFFS + BY_POOL[n - POOL_RING] + 1)
                    elif n == 0:
                        pl.wait_ge(S["reduced"], i * OFFS)
                    pl.tensor_tensor(rows(prod_p[:, n % POOL_RING, :]), rows(q[:]), head_shift(k_pad, SEQ[BY_POOL[n]]),
                                     ALU.mult).then_inc(S["prod_pool"], 1)

            def column_sums(i, dy):
                pl.wait_ge(S["ev_ready"], i * OFFS + NB * (dy + 1))
                e, a, o = ev_row[dy], hs_a[:, dy % 2], hs[:, dy]
                c = i * 5 * POOL_ROWS + 5 * dy
                if dy >= 2:
                    pl.wait_ge(S["hsum_step"], c - 5)
                pl.tensor_tensor(a[:, 0, :], e[:, 1, :], e[:, 2, :], ALU.add).then_inc(S["hsum_step"], 1)
                pl.tensor_tensor(a[:, 1, :], e[:, 3, :], e[:, 4, :], ALU.add).then_inc(S["hsum_step"], 1)
                pl.wait_ge(S["hsum_step"], c + 1)
                pl.tensor_tensor(o[:, 0, :], e[:, 0, :], a[:, 0, :], ALU.add).then_inc(S["hsum_step"], 1)
                pl.tensor_tensor(o[:, 1, :], e[:, 3, :], a[:, 0, :], ALU.add).then_inc(S["hsum_step"], 1)
                pl.wait_ge(S["hsum_step"], c + 2)
                pl.tensor_tensor(o[:, 2, :], e[:, 2, :], a[:, 1, :], ALU.add).then_inc(S["hsum_step"], 1)

            def round_pool(i, main, front, back):
                j, m = i - 1, i + 1
                if back:
                    pl.wait_ge(S["lnC_bc"], j)
                    power("lnA", rs[:], var[:], j)
                if main:
                    column_sums(i, 0)
                if front:
                    pl.wait_ge(S["pre_bc"], m)
                    power("pre", rs0[:], var0[:], m)
                if main:
                    for dy in range(1, POOL_ROWS):
                        column_sums(i, dy)
                if front:
                    products(m, range(len(BY_POOL)))
                if back:
                    pl.wait_ge(S["lnA_bc"], j + 1)
                    power("lnB", rs[:], var[:], j)
                if main:
                    for part, (w0, w1) in enumerate(VARY):
                        pl.wait_ge(S["vary_ready"], 2 * i + part + 1)
                        pl.tensor_tensor(rsy[:, w0 * TILES:w1 * TILES], vary[:, w0 * TILES:w1 * TILES],
                                         minus_half[:, 0:(w1 - w0) * TILES], ALU.pow).then_inc(S["rsy_ready"], 1)
                if back:
                    pl.wait_ge(S["lnB_bc"], j + 1)
                    power("lnC", rs[:], var[:], j)
            rounds(pl, round_pool)
            pl.wait_ge(S["bn_v"], 1)
            pl.tensor_tensor(tiny[:, 1:2], tiny[:, 0:1], minus_half[:, 0:1], ALU.pow).then_inc(S["bn_rs"], 1)
            scan_pool(pl)

        @block.tensor
        def _(pe):
            def turn(dst, src, idn):
                return pe.matmul(dst, src, idn, start=True, stop=True, is_transpose=True)

            def ln_pe(tag, slots, s, x, ready, i):
                if s == slots[0]:
                    pe.wait_ge(S[ready], i + 1)
                    pe.matmul(psA[:, 0, :], mean_w[:], x[:], start=True, stop=True).then_inc(S[tag + "_mean"], 1)
                if s == slots[2]:
                    pe.wait_ge(S[tag + "_cent"], i + 1)
                    pe.wait_ge(S[tag + "_sq"], i + 1)
                    for t in range(TILES):
                        m = pe.matmul(psA[:, 0, t:t + 1], sq[:, P * t:P * t + P], mean_w[:, 0:1], start=True, stop=True)
                    m.then_inc(S[tag + "_var"], 1)
                if s == slots[4]:
                    pe.wait_ge(S[tag + "_v"], i + 1)
                    pe.wait_ge(S[tag + "_rs"], i + 1)
                    for t in range(TILES):
                        m = turn(psA[:, 0, P * t:P * t + P], rs[:, t:t + 1].to_broadcast([P, P]), ident[:])
                    m.then_inc(S[tag + "_bc"], 1)

            pe.wait_ge(S["consts"], CONSTS)
            pe.wait_ge(S["weights"], 16 * LOADS)
            for n in range(3):
                pe.matmul(psA[:, 0, n:n + 1], wqkv[:, n, :], cols[:, 1:2], start=True, stop=True)
            pe.matmul(psA[:, 0, 4:5], mean_w[:], cols[:, 2:3], start=True, stop=True).then_inc(S["setup_pe"], 1)
            for n in range(CONV_STEPS):
                pe.wait_ge(S["setup_dve"], n + 1)
                pe.matmul(psB[:, n % 2, 0:P], conv_bT[:], conv_s[:, n, :], start=True, stop=True).then_inc(S["setup_pe"], 1)
            pe.wait_ge(S["setup_dve"], CONV_STEPS + 1)
            turn(psB[:, 0, 0:P], conv_s[:, CONV_STEPS, :], ident[:]).then_inc(S["setup_pe"], 1)
            pe.wait_ge(S["w_ready"], 1)

            ge, gr = NB * PARTS * HEADS, KW * PARTS * HEADS

            def front_pe(s, i):
                if s == F_MEAN:
                    pe.wait_ge(S["x_loaded"], 16 * (i + 1))
                    pe.wait_ge(S["eT_ready"], 4 * i)
                    for h in range(2):
                        m = pe.matmul(psP[:, h, 0:HALF], mean_w[:], xh[:, h * HALF:(h + 1) * HALF], start=True, stop=True)
                    m.then_inc(S["pre_mean"], 1)
                if s == F_VAR:
                    pe.wait_ge(S["pre_cent"], i + 1)
                    pe.wait_ge(S["pre_sq"], i + 1)
                    for t in range(HTILES):
                        m = pe.matmul(psP[:, 0, t:t + 1], sq0[:, P * t:P * t + P], mean_w[:, 0:1], start=True, stop=True)
                    m.then_inc(S["pre_var"], 1)
                if s == F_BC:
                    pe.wait_ge(S["pre_v"], i + 1)
                    pe.wait_ge(S["pre_rs"], i + 1)
                    for t in range(HTILES):
                        m = turn(psP[:, t // 3, P * (t % 3):P * (t % 3) + P], rs0[:, t:t + 1].to_broadcast([P, P]), ident[:])
                    m.then_inc(S["pre_bc"], 1)
                if s == F_K:
                    pe.wait_ge(S["pre_xn"], i + 1)
                    for h in range(2):
                        m = pe.matmul(psP[:, h, 0:HALF], wqkv[:, 1, :], xc0[:, h * HALF:(h + 1) * HALF], start=True, stop=True)
                    m.then_inc(S["k_mm"], 1)
                if s == F_Q:
                    pe.wait_ge(S["k_ready"], i + 1)
                    pe.matmul(psP[:, 0, :], wqkv[:, 0, :], xc0[:, HALO * IMG:HALO * IMG + PIX], start=True, stop=True)\
                        .then_inc(S["q_mm"], 1)
                if s == F_VAL:
                    pe.wait_ge(S["q_ready"], i + 1)
                    for h in range(2):
                        m = pe.matmul(psP[:, h, 0:HALF], wqkv[:, 2, :], xc0[:, h * HALF:(h + 1) * HALF], start=True, stop=True)
                    m.then_inc(S["v_mm"], 1)

            def reduce_scores(i, group):
                if 0 in group:
                    pe.wait_ge(S["v_ready"], i + 1)
                for kk in reversed(group):
                    if kk in BY_DVE:
                        pe.wait_ge(S["prod_dve"], i * len(BY_DVE) + BY_DVE.index(kk) + 1)
                        break
                for kk in reversed(group):
                    if kk in BY_POOL:
                        pe.wait_ge(S["prod_pool"], i * len(BY_POOL) + BY_POOL.index(kk) + 1)
                        break
                for kk in group:
                    off = SEQ[kk]
                    src = prod_d[:, BY_DVE.index(kk) % DVE_RING, :] if kk in BY_DVE else prod_p[:, BY_POOL.index(kk) % POOL_RING, :]
                    T, g, m4 = off // 16, off % 16 // 4, off % 4
                    last = m4 == 3 or off == OFFS - 1
                    pe.matmul(psP[32 * g:32 * g + 32, T, :], head_sum[:, m4, :], src, start=m4 == 0, stop=last)\
                        .then_inc(S["reduced"], 1)

            def turn_scores(i):
                for T in range(2):
                    n = P if T == 0 else OFFS * HEADS - P
                    pe.wait_ge(S["s2_ready"], 2 * i + 2)
                    for t in range(TILES):
                        m = turn(psS[:, t, P * T:P * T + n], s2[0:n, T, P * t:P * t + P], ident[0:n, 0:n])
                m.then_inc(S["s_turned"], 1)

            def turn_e(i, part):
                if part == 0:
                    pe.wait_ge(S["es_ready"], i + 1)
                    pe.wait_ge(S["e_hi"], i + 1)
                    pe.wait_ge(S["e_mid"], i + 1)
                    pe.wait_ge(S["e_lo"], i + 1)
                    for g in range(4):
                        for t in range(TILES):
                            c = PIX * g + P * t
                            m = turn(psT[0:ge, c:c + P], e3[:, t, NB * g:NB * g + NB].rearrange("p o s h -> p (o s h)"), ident_b[:])
                        if g % 2:
                            m.then_inc(S["e_turned"], 1)
                else:
                    pe.wait_ge(S["eT_ready"], 4 * i + 1)
                    for t in range(TILES):
                        m = turn(psT[0:ge, P * t:P * t + P], e3[:, t, NB * 4:NB * 5].rearrange("p o s h -> p (o s h)"), ident_b[:])
                    m.then_inc(S["e_turned"], 1)

            def turn_r(i):
                pe.wait_ge(S["r_hi"], i + 1)
                pe.wait_ge(S["r_mid"], i + 1)
                pe.wait_ge(S["r_lo"], i + 1)
                for g in range(KW):
                    if g == 1:
                        pe.wait_ge(S["eT_ready"], 4 * i + 2)
                    for t in range(TILES):
                        c = PIX * (g + 1) + P * t
                        m = turn(psT[0:gr, c:c + P], r3[:, t, KW * g:KW * g + KW].rearrange("p o s h -> p (o s h)"), ident_b[:])
                m.then_inc(S["e_turned"], 1)

            def r_spread(i, n):
                b = n % 2
                if n < 2:
                    pe.wait_ge(S["ev_ready"], (i + 1) * OFFS)
                else:
                    pe.wait_ge(S["win_ready"], i * WINS + n - 1)
                pe.matmul(psB[:, b, :], spread[0:gr, n % KW, :], rT[:, n // KW, :], start=True, stop=True)\
                    .then_inc(S["r_spread"], 1)

            def var_y(i, n):
                pe.wait_ge(S["sqy_ready"], i * WINS + n + 1)
                for t in range(TILES):
                    m = pe.matmul(psF[:, n * TILES + t:n * TILES + t + 1], sqy[:, n % 2, P * t:P * t + P],
                                  mean_w[:, 0:1], start=True, stop=True)
                m.then_inc(S["vary_mm"], 1)

            def e_spread(o):
                pe.matmul(psE[:, o % 4, :], spread[0:ge, o % NB, :], eT[:, o // NB, :], start=True, stop=True)\
                    .then_inc(S["e_spread"], 1)

            def rs_spread(i, n):
                if n >= 3:
                    pe.wait_ge(S["u_ready"], i * WINS + n - 2)
                for t in range(TILES):
                    m = turn(psR[:, n % 3, P * t:P * t + P], rsv[:, t, n:n + 1].to_broadcast([P, P]), ident[:])
                m.then_inc(S["rs_spread"], 1)

            def back_pe(s, i):
                ln_pe("lnA", A_SLOTS, s, x1, "x1_ready", i)
                if s == LOGIT:
                    pe.wait_ge(S["lnA_xn"], i + 1)
                    for t in range(TILES):
                        m = pe.matmul(psA[:, 1, EXPERTS * t:EXPERTS * (t + 1)], xn[:, P * t:P * t + P], rw[:], start=True, stop=True)
                    m.then_inc(S["logit_mm"], 1)
                if s == G_TURN:
                    pe.wait_ge(S["g_ready"], i + 1)
                    for t in range(TILES):
                        m = turn(psA[0:EXPERTS, 0, P * t:P * t + P], gate[:, t, :], ident[:])
                    m.then_inc(S["g_turned"], 1)
                if s == G_TURN + 1:
                    pe.wait_ge(S["gT_ready"], i + 1)
                    pe.matmul(psA[:, 1, :], eb[:], gT[:], start=True, stop=False)
                if s in [G_TURN + 1] + XG[:-1]:
                    e = ([G_TURN + 1] + XG).index(s)
                    if e:
                        pe.wait_ge(S["xg_ready"], i * EXPERTS + e)
                    for t in range(TILES):
                        m = turn(psA[:, 0, P * t:P * t + P], gate[:, t, e:e + 1].to_broadcast([P, P]), ident[:])
                    m.then_inc(S["g_spread"], 1)
                if s in XG:
                    e = XG.index(s)
                    pe.wait_ge(S["xg_ready"], i * EXPERTS + e + 1)
                    pe.matmul(psA[:, 1, :], ew[:, e, :], xg[:, e % 2, :], start=False, stop=e == EXPERTS - 1)\
                        .then_inc(S["moe_mm"], 1)
                ln_pe("lnB", B_SLOTS, s, xa, "xa_ready", i)
                if s == B_SLOTS[5]:
                    pe.wait_ge(S["lnB_xn"], i + 1)
                    pe.matmul(psA[:, 1, :], conv_mT[:], xn[:], start=True, stop=True).then_inc(S["conv_mm"], 1)
                ln_pe("lnC", C_SLOTS, s, xb, "xb_ready", i)
                if s == C_SLOTS[5]:
                    pe.wait_ge(S["lnC_xn"], i + 1)
                    pe.matmul(psA[:, 1, :], w_in[:], xn[:], start=True, stop=True).then_inc(S["wx_mm"], 1)

            def round_pe(i, main, front, back):
                j, m = i - 1, i + 1
                for s in range(END):
                    if main and MIX <= s < MIX + OFFS:
                        o = s - MIX
                        if o == 0:
                            pe.wait_ge(S["u_ready"], i * WINS)
                            pe.wait_ge(S["eT_ready"], 4 * i + 3)
                            for ahead in range(AHEAD):
                                e_spread(ahead)
                            pe.wait_ge(S["x1_ready"], i)
                        else:
                            pe.wait_ge(S["ev_ready"], i * OFFS + o)
                        if o + AHEAD < OFFS:
                            e_spread(o + AHEAD)
                    if NORM <= s < NORM + WINS:
                        n = s - NORM
                        if main:
                            if n == 0:
                                pe.wait_ge(S["eT_ready"], 4 * i + 4)
                                r_spread(i, 0)
                            if n + 1 < WINS:
                                r_spread(i, n + 1)
                            pe.wait_ge(S["win_ready"], i * WINS + n + 1)
                            if n:
                                pe.wait_ge(S["sqy_ready"], i * WINS + n)
                            pe.matmul(psY, wproj[:], win[:, n // KW, n % KW, :], start=True, stop=True).then_inc(S["proj_mm"], 1)
                            if n:
                                var_y(i, n - 1)
                        if front:
                            reduce_scores(m, GROUPS[n])
                    if s == SOFT:
                        if main:
                            var_y(i, WINS - 1)
                        if front:
                            turn_scores(m)
                        if main:
                            pe.wait_ge(S["vary_ready"], 2 * i + 2)
                            pe.wait_ge(S["rsv_ready"], i + 1)
                            rs_spread(i, 0)
                            rs_spread(i, 1)
                            pe.wait_ge(S["rc_ready"], i + 1)
                            pe.wait_ge(S["cnt_ready"], i + 1)
                            for t in range(TILES):
                                mm = turn(psY[0:2, P * t:P * t + P], rc[:, t, :], ident[:])
                            mm.then_inc(S["rc_turned"], 1)
                    if SUM <= s < SUM + WINS:
                        n = s - SUM
                        if main:
                            if n == 0:
                                pe.wait_ge(S["rcT_ready"], i + 1)
                                pe.matmul(psF, brow[:], rcT[:], start=True, stop=False)
                            if n + 2 < WINS:
                                rs_spread(i, n + 2)
                            pe.wait_ge(S["u_ready"], i * WINS + n + 1)
                            mm = pe.matmul(psF, wproj_g[:], win[:, n // KW, n % KW, :], start=False, stop=n == WINS - 1)
                            if n == WINS - 1:
                                mm.then_inc(S["final_mm"], 1)
                        if front and n == 3:
                            turn_e(m, 0)
                        if front and n == 5:
                            turn_e(m, 1)
                        if front and n == 7:
                            turn_r(m)
                    if back:
                        back_pe(s, j)
                    if front:
                        front_pe(s, m)
            rounds(pe, round_pe)
            scan_pe(pe)

        @block.scalar
        def _(ac):
            halves = psP[:, :, 0:HALF].rearrange("p b (r c) -> p b r c", c=IMG)

            def ln_act(tag, slots, s, i):
                if s == slots[1]:
                    ac.wait_ge(S[tag + "_cent"], i + 1)
                    ac.activation(sq[:], xc[:], ACT.Square).then_inc(S[tag + "_sq"], 1)

            def front_act(s, i):
                if s == F_CENT:
                    ac.wait_ge(S["pre_cent"], i + 1)
                    ac.activation(sq0, xc0[:], ACT.Square).then_inc(S["pre_sq"], 1)
                if s == F_K:
                    ac.wait_ge(S["k_mm"], i + 1)
                    ac.wait_ge(S["prod_pool"], i * len(BY_POOL))
                    ac.wait_ge(S["prod_dve"], i * len(BY_DVE))
                    ac.activation(k_pad[:, :, HALO:HALO + IMG].rearrange("p (b r) c -> p b r c", b=2), halves,
                                  ACT.Identity, bias=bqkv[:, 1:2]).then_inc(S["k_ready"], 1)
                if s == F_Q:
                    ac.wait_ge(S["q_mm"], i + 1)
                    ac.activation(q[:], psP[:, 0, :], ACT.Identity, bias=bqkv[:, 0:1]).then_inc(S["q_ready"], 1)
                if s == F_VAL:
                    ac.wait_ge(S["v_mm"], i + 1)
                    ac.wait_ge(S["ev_ready"], i * OFFS)
                    ac.activation(v_pad[:, :, HALO:HALO + IMG].rearrange("p (b r) c -> p b r c", b=2), halves,
                                  ACT.Identity, bias=bqkv[:, 2:3]).then_inc(S["v_ready"], 1)

            def soft_act(i):
                ac.wait_ge(S["es_ready"], i + 1)
                ac.activation(e32[:], es[:], ACT.Exp).then_inc(S["e_ready"], 1)
                ac.wait_ge(S["e_ready"], i + 1)
                to = e3[:].rearrange("p t o s h -> p (t o) s h")
                ac.activation(to[:, :, 0, :], e32[:].rearrange("p t o h -> p (t o) h"), ACT.Copy).then_inc(S["e_hi"], 1)

            def mid_act(i):
                to = e3[:].rearrange("p t o s h -> p (t o) s h")
                ac.wait_ge(S["e_rest"], i + 1)
                ac.activation(to[:, :, 1, :], erest[:].rearrange("p t o h -> p (t o) h"), ACT.Copy).then_inc(S["e_mid"], 1)

            def parts_act(i, part):
                to = r3[:].rearrange("p t o s h -> p (t o) s h")
                if part == 0:
                    ac.wait_ge(S["r_ready"], i + 1)
                    ac.activation(to[:, :, 0, :], rden[:].rearrange("p t o h -> p (t o) h"), ACT.Copy).then_inc(S["r_hi"], 1)
                else:
                    ac.wait_ge(S["r_rest"], i + 1)
                    ac.activation(to[:, :, 1, :], rrest[:].rearrange("p t o h -> p (t o) h"), ACT.Copy).then_inc(S["r_mid"], 1)

            def turned_act(i, part):
                ge, gr = NB * PARTS * HEADS, KW * PARTS * HEADS
                if part == 0:
                    ac.wait_ge(S["e_turned"], 4 * i + 1)
                    ac.activation(eT[:, 0:2, :], psT[0:ge, 0:2 * PIX].rearrange("p (g n) -> p g n", n=PIX), ACT.Copy)\
                        .then_inc(S["eT_ready"], 1)
                    ac.wait_ge(S["e_turned"], 4 * i + 2)
                    ac.activation(eT[:, 2:4, :], psT[0:ge, 2 * PIX:4 * PIX].rearrange("p (g n) -> p g n", n=PIX), ACT.Copy)\
                        .then_inc(S["eT_ready"], 1)
                else:
                    ac.wait_ge(S["e_turned"], 4 * i + 3)
                    ac.wait_ge(S["e_turned"], 4 * i + 4)
                    ac.activation(eT[:, 4, :], psT[0:ge, 0:PIX], ACT.Copy).then_inc(S["eT_ready"], 1)
                    ac.activation(rT[:], psT[0:gr, PIX:4 * PIX].rearrange("p (g n) -> p g n", n=PIX), ACT.Copy)\
                        .then_inc(S["eT_ready"], 1)

            def back_act(s, i):
                ln_act("lnA", A_SLOTS, s, i)
                if s == ROUTE1:
                    ac.wait_ge(S["gap_ready"], i + 1)
                    ac.activation(top[:, 3, :], top[:, 2, :], ACT.Exp).then_inc(S["exp_ready"], 1)
                if s == G_TURN:
                    ac.wait_ge(S["g_turned"], i + 1)
                    ac.activation(gT[:], psA[0:EXPERTS, 0, :], ACT.Copy).then_inc(S["gT_ready"], 1)
                ln_act("lnB", B_SLOTS, s, i)
                ln_act("lnC", C_SLOTS, s, i)
                if s == STATS:
                    ac.wait_ge(S["stats_ready"], i + 1)
                    ac.wait_ge(S["wx_stored"], 16 * i)
                    ac.activation(wx[:], psA[:, 1, :], ACT.Copy).then_inc(S["wx_ready"], 1)

            def round_act(i, main, front, back):
                j, m = i - 1, i + 1
                if main:
                    ac.wait_ge(S["x_loaded"], 16 * (i + 1))
                    ac.wait_ge(S["x1_ready"], i)
                    ac.activation(xres[:], xh[:, HALO * IMG:HALO * IMG + PIX], ACT.Copy).then_inc(S["xres_ready"], 1)
                for s in range(END):
                    if NORM <= s < NORM + WINS:
                        n = s - NORM
                        if main:
                            ac.wait_ge(S["proj_mm"], i * WINS + n + 1)
                            if n >= 2:
                                ac.wait_ge(S["vary_mm"], i * WINS + n - 1)
                            ac.activation(sqy[:, n % 2, :], psY, ACT.Square, bias=bproj_c[:]).then_inc(S["sqy_ready"], 1)
                        if front and n == 5:
                            ac.wait_ge(S["reduced"], m * OFFS + 16)
                            ac.activation(s2[:, 0, :], psP[:, 0, :], ACT.Copy).then_inc(S["s2_ready"], 1)
                    if s == SOFT and front:
                        n = OFFS * HEADS - P
                        ac.wait_ge(S["reduced"], m * OFFS + OFFS)
                        ac.activation(s2[0:n, 1, :], psP[0:n, 1, :], ACT.Copy).then_inc(S["s2_ready"], 1)
                        soft_act(m)
                    if s == SOFT and main:
                        ac.wait_ge(S["rc_turned"], i + 1)
                        ac.activation(rcT[:], psY[0:2, :], ACT.Copy).then_inc(S["rcT_ready"], 1)
                    if s == SOFT and front:
                        mid_act(m)
                    if s == SUM + 3 and front:
                        parts_act(m, 0)
                        turned_act(m, 0)
                    if s == SUM + 5 and front:
                        parts_act(m, 1)
                    if s == SUM + 7 and front:
                        turned_act(m, 1)
                    if back:
                        back_act(s, j)
                    if front:
                        front_act(s, m)
            rounds(ac, round_act)
            scan_act(ac)

        @block.vector
        def _(ve):
            n_setup = [0]

            def own(ins):
                n_setup[0] += 1
                ins.then_inc(S["w_scaled"], 1)
                ve.wait_ge(S["w_scaled"], n_setup[0])
            ve.wait_ge(S["weights"], 16 * LOADS)
            ve.wait_ge(S["consts"], CONSTS)
            own(ve.tensor_scalar(conv_bT[:], ident[:], 0.95, None, ALU.mult))
            own(ve.scalar_tensor_tensor(out=conv_bT[:], in0=conv_mT[:], scalar=0.025, in1=conv_bT[:], op0=ALU.mult, op1=ALU.add))
            ve.tensor_copy(conv_s[:, 0, :], conv_a[:]).then_inc(S["setup_dve"], 1)
            ve.wait_ge(S["setup_pe"], 1)
            own(ve.tensor_copy(bqkv[:], psA[:, 0, 0:3]))
            own(ve.tensor_scalar(bqkv[:, 0:1], bqkv[:, 0:1], HD ** -0.5, None, ALU.mult))
            own(ve.tensor_tensor(bproj_c[:], cols[:, 2:3], psA[:, 0, 4:5], ALU.subtract))
            own(ve.tensor_scalar(wqkv[:], wqkv[:], cols[:, 0:1], None, ALU.mult))
            own(ve.tensor_scalar(wqkv[:, 0, :], wqkv[:, 0, :], HD ** -0.5, None, ALU.mult))
            own(ve.tensor_reduce(tiny[:, 2:3], wproj[:], AX.X, ALU.add))
            own(ve.tensor_scalar(tiny[:, 2:3], tiny[:, 2:3], 1.0 / P, None, ALU.mult))
            own(ve.tensor_scalar(wproj[:], wproj[:], tiny[:, 2:3], None, ALU.subtract))
            own(ve.tensor_tensor(wproj_g[:], wproj[:], prow[:, 1, :], ALU.mult))
            own(ve.tensor_reduce(tiny[:, 3:4], prow[:, 0, :], AX.X, ALU.add))
            own(ve.tensor_scalar(tiny[:, 3:4], tiny[:, 3:4], 1.0 / P, None, ALU.mult))
            own(ve.tensor_scalar(prow[:, 0, :], prow[:, 0, :], tiny[:, 3:4], None, ALU.subtract))
            own(ve.tensor_tensor(prow[:, 0, :], prow[:, 0, :], prow[:, 1, :], ALU.mult))
            own(ve.tensor_scalar(brow[:], prow[0:2, 0, :], sel[:, 0:1], None, ALU.mult))
            own(ve.scalar_tensor_tensor(out=brow[:], in0=prow[0:2, 2, :], scalar=sel[:, 1:2], in1=brow[:], op0=ALU.mult, op1=ALU.add))
            for n in range(CONV_STEPS):
                ve.wait_ge(S["setup_pe"], n + 2)
                ve.scalar_tensor_tensor(out=conv_s[:, n + 1, :], in0=conv_a[:], scalar=0.025, in1=psB[:, n % 2, 0:P],
                                        op0=ALU.mult, op1=ALU.add).then_inc(S["setup_dve"], 1)
            ve.wait_ge(S["setup_pe"], CONV_STEPS + 2)
            ve.tensor_copy(conv_mT[:], psB[:, 0, 0:P]).then_inc(S["w_ready"], 1)

            def ln_dve(tag, slots, s, x, ready, i, eps):
                if s == slots[1]:
                    ve.wait_ge(S[ready], i + 1)
                    ve.wait_ge(S[tag + "_mean"], i + 1)
                    ve.tensor_tensor(xc[:], x[:], psA[:, 0, :], ALU.subtract).then_inc(S[tag + "_cent"], 1)
                if s == slots[3]:
                    ve.wait_ge(S[tag + "_var"], i + 1)
                    ve.tensor_scalar(var[:], psA[:, 0, 0:TILES], 1.0, eps, ALU.mult, ALU.add).then_inc(S[tag + "_v"], 1)
                if s == slots[5]:
                    ve.wait_ge(S[tag + "_bc"], i + 1)
                    ve.tensor_tensor(xn[:], xc[:], psA[:, 0, :], ALU.mult).then_inc(S[tag + "_xn"], 1)

            def front_dve(s, i):
                xc2 = xc0[:].rearrange("p (b n) -> p b n", b=2)
                if s == F_CENT:
                    ve.wait_ge(S["pre_mean"], i + 1)
                    ve.wait_ge(S["v_mm"], i)
                    ve.tensor_tensor(xc2, xh[:].rearrange("p (b n) -> p b n", b=2), psP[:, :, 0:HALF], ALU.subtract)\
                        .then_inc(S["pre_cent"], 1)
                if s == F_V:
                    ve.wait_ge(S["pre_var"], i + 1)
                    ve.tensor_scalar(var0[:], psP[:, 0, 0:HTILES], 1.0 + 1e-5, 1e-11, ALU.mult, ALU.add).then_inc(S["pre_v"], 1)
                if s == F_XN:
                    ve.wait_ge(S["pre_bc"], i + 1)
                    ve.wait_ge(S["pre_sq"], i + 1)
                    ve.tensor_tensor(xc2, xc2, psP[:, :, 0:HALF], ALU.mult).then_inc(S["pre_xn"], 1)

            def products(i, group):
                for kk in group:
                    if kk not in BY_DVE:
                        continue
                    n = BY_DVE.index(kk)
                    if n == 0:
                        ve.wait_ge(S["k_ready"], i + 1)
                        ve.wait_ge(S["q_ready"], i + 1)
                        ve.wait_ge(S["reduced"], i * OFFS)
                    if n >= DVE_RING:
                        ve.wait_ge(S["reduced"], i * OFFS + BY_DVE[n - DVE_RING] + 1)
                    ve.tensor_tensor(rows(prod_d[:, n % DVE_RING, :]), rows(q[:]), head_shift(k_pad, SEQ[kk]),
                                     ALU.mult).then_inc(S["prod_dve"], 1)

            def soft_shift(i):
                ve.wait_ge(S["s_turned"], i + 1)
                sc = psS[:, :, 0:OFFS * HEADS].rearrange("p t (o h) -> p t o h", h=HEADS)
                ve.tensor_reduce(smax[:], psS[:, :, 0:OFFS * HEADS].rearrange("p t (o h) -> p t h o", h=HEADS), AX.X, ALU.max)\
                    .then_inc(S["smax_ready"], 1)
                ve.wait_ge(S["smax_ready"], i + 1)
                ve.tensor_tensor(es[:], sc, smax[:].unsqueeze(2).to_broadcast([P, TILES, OFFS, HEADS]), ALU.subtract)\
                    .then_inc(S["es_ready"], 1)

            def soft_sums(i, part):
                ee = e32[:].rearrange("p t (y x) h -> p (t y) (x h)", x=NB)
                e3v = e3[:].rearrange("p t o s h -> p (t o) s h")
                er = erest[:].rearrange("p t o h -> p (t o) h")
                dh = dsum_h[:].rearrange("p t y n -> p t (y n)")
                c, row = 4 * i, KW * HEADS
                if part == 0:
                    ve.wait_ge(S["e_ready"], i + 1)
                    ve.tensor_tensor(dsum_a[:], ee[:, :, 0:row], ee[:, :, HEADS:HEADS + row], ALU.add).then_inc(S["dsum_step"], 1)
                    ve.wait_ge(S["e_hi"], i + 1)
                    ve.tensor_tensor(er, e32[:].rearrange("p t o h -> p (t o) h"), e3v[:, :, 0, :], ALU.subtract)\
                        .then_inc(S["e_rest"], 1)
                if part == 1:
                    ve.wait_ge(S["dsum_step"], c + 1)
                    ve.tensor_tensor(dsum_h[:].rearrange("p t y n -> p (t y) n"), dsum_a[:], ee[:, :, 2 * HEADS:2 * HEADS + row],
                                     ALU.add).then_inc(S["dsum_step"], 1)
                    ve.wait_ge(S["dsum_step"], c + 2)
                    ve.tensor_tensor(dsum_b[:], dh[:, :, 0:KW * row], dh[:, :, row:row + KW * row], ALU.add)\
                        .then_inc(S["dsum_step"], 1)
                if part == 2:
                    ve.wait_ge(S["e_rest"], i + 1)
                    ve.wait_ge(S["e_mid"], i + 1)
                    ve.tensor_tensor(e3v[:, :, 2, :], er, e3v[:, :, 1, :], ALU.subtract).then_inc(S["e_lo"], 1)
                    ve.wait_ge(S["dsum_step"], c + 3)
                    ve.tensor_tensor(dsum[:], dsum_b[:], dh[:, :, 2 * row:2 * row + KW * row], ALU.add)\
                        .then_inc(S["dsum_step"], 1)
                if part == 3:
                    ve.wait_ge(S["dsum_step"], c + 4)
                    ve.reciprocal(rden[:].rearrange("p t w h -> p (t w h)"), dsum[:].rearrange("p t n -> p (t n)"))\
                        .then_inc(S["r_ready"], 1)

            def soft_parts(i, part):
                r3v = r3[:].rearrange("p t o s h -> p (t o) s h")
                rr = rrest[:].rearrange("p t o h -> p (t o) h")
                if part == 0:
                    ve.wait_ge(S["r_ready"], i + 1)
                    ve.wait_ge(S["r_hi"], i + 1)
                    ve.tensor_tensor(rr, rden[:].rearrange("p t o h -> p (t o) h"), r3v[:, :, 0, :], ALU.subtract)\
                        .then_inc(S["r_rest"], 1)
                else:
                    ve.wait_ge(S["r_rest"], i + 1)
                    ve.wait_ge(S["r_mid"], i + 1)
                    ve.tensor_tensor(r3v[:, :, 2, :], rr, r3v[:, :, 1, :], ALU.subtract).then_inc(S["r_lo"], 1)

            def vary_part(i, part):
                w0, w1 = VARY[part]
                ve.wait_ge(S["vary_mm"], i * WINS + w1)
                ve.tensor_scalar(vary[:, w0 * TILES:w1 * TILES], psF[:, w0 * TILES:w1 * TILES], 1.0, 1e-5, ALU.mult, ALU.add)\
                    .then_inc(S["vary_ready"], 1)

            def dve_column_sums(i, dy):
                e, o, c = ev_row[dy], hs[:, dy], 5 * (i * DVE_ROWS + dy - POOL_ROWS)
                ve.wait_ge(S["ev_ready"], i * OFFS + NB * (dy + 1))
                if dy > POOL_ROWS or not isinstance(i, int) or i:
                    ve.wait_ge(S["hsum_dve"], c)
                ve.tensor_tensor(hs_b[:, 0, :], e[:, 1, :], e[:, 2, :], ALU.add).then_inc(S["hsum_dve"], 1)
                ve.tensor_tensor(hs_b[:, 1, :], e[:, 3, :], e[:, 4, :], ALU.add).then_inc(S["hsum_dve"], 1)
                ve.wait_ge(S["hsum_dve"], c + 1)
                ve.tensor_tensor(o[:, 0, :], e[:, 0, :], hs_b[:, 0, :], ALU.add).then_inc(S["hsum_dve"], 1)
                ve.tensor_tensor(o[:, 1, :], e[:, 3, :], hs_b[:, 0, :], ALU.add).then_inc(S["hsum_dve"], 1)
                ve.wait_ge(S["hsum_dve"], c + 2)
                ve.tensor_tensor(o[:, 2, :], e[:, 2, :], hs_b[:, 1, :], ALU.add).then_inc(S["hsum_dve"], 1)

            def row_sums(i, n):
                c = 5 * i
                if n == 0:
                    ve.wait_ge(S["hsum_step"], (i + 1) * 5 * POOL_ROWS)
                    ve.wait_ge(S["final_mm"], i)
                    ve.tensor_tensor(vs[:, 0], hs[:, 1], hs[:, 2], ALU.add).then_inc(S["vsum_step"], 1)
                if n == 1:
                    ve.wait_ge(S["vsum_step"], c + 1)
                    ve.tensor_tensor(win[:, 0], hs[:, 0], vs[:, 0], ALU.add).then_inc(S["vsum_step"], 1)
                if n == 2:
                    ve.wait_ge(S["hsum_dve"], 5 * DVE_ROWS * (i + 1))
                    ve.tensor_tensor(vs[:, 1], hs[:, 3], hs[:, 4], ALU.add).then_inc(S["vsum_step"], 1)
                if n == 3:
                    ve.tensor_tensor(win[:, 1], hs[:, 3], vs[:, 0], ALU.add).then_inc(S["vsum_step"], 1)
                if n == 4:
                    ve.wait_ge(S["vsum_step"], c + 3)
                    ve.tensor_tensor(win[:, 2], hs[:, 2], vs[:, 1], ALU.add).then_inc(S["vsum_step"], 1)

            def route(i, part):
                k = [0 if part == 0 else 12]

                def step(ins):
                    k[0] += 1
                    ins.then_inc(S["route_step"], 1)
                    ve.wait_ge(S["route_step"], ROUTE * i + k[0])

                def per_tile(a):
                    return a.unsqueeze(2).to_broadcast([P, TILES, EXPERTS])
                if part == 0:
                    ve.wait_ge(S["logit_mm"], i + 1)
                    step(ve.tensor_tensor(logit[:], psA[:, 1, 0:TILES * EXPERTS].rearrange("p (t e) -> p t e", e=EXPERTS),
                                          rb[:].unsqueeze(1).to_broadcast([P, TILES, EXPERTS]), ALU.add))
                    for n in range(2):
                        src = logit[:] if n == 0 else rt[:, 2]
                        step(ve.tensor_reduce(top[:, n, :], src, AX.X, ALU.max))
                        step(ve.tensor_tensor(rt[:, 0], src, per_tile(top[:, n, :]), ALU.is_equal))
                        step(ve.tensor_tensor(rt[:, 1], rt[:, 0], rank[:], ALU.mult))
                        step(ve.tensor_reduce(top[:, 4, :], rt[:, 1], AX.X, ALU.min))
                        step(ve.tensor_tensor(hot[:, n], rt[:, 1], per_tile(top[:, 4, :]), ALU.is_equal))
                        if n == 0:
                            step(ve.scalar_tensor_tensor(out=rt[:, 2], in0=hot[:, 0], scalar=-3e38, in1=logit[:],
                                                         op0=ALU.mult, op1=ALU.add))
                    assert k[0] == 12
                    ve.tensor_tensor(top[:, 2, :], top[:, 1, :], top[:, 0, :], ALU.subtract).then_inc(S["gap_ready"], 1)
                else:
                    ve.wait_ge(S["exp_ready"], i + 1)
                    step(ve.tensor_scalar(top[:, 5, :], top[:, 3, :], 1.0, None, ALU.add))
                    step(ve.reciprocal(top[:, 6, :], top[:, 5, :]))
                    step(ve.tensor_tensor(top[:, 7, :], top[:, 3, :], top[:, 6, :], ALU.mult))
                    step(ve.tensor_tensor(rt[:, 0], hot[:, 0], per_tile(top[:, 6, :]), ALU.mult))
                    step(ve.tensor_tensor(rt[:, 1], hot[:, 1], per_tile(top[:, 7, :]), ALU.mult))
                    assert k[0] == ROUTE
                    ve.tensor_tensor(gate[:], rt[:, 0], rt[:, 1], ALU.add).then_inc(S["g_ready"], 1)

            def back_dve(s, i):
                ln_dve("lnA", A_SLOTS, s, x1, "x1_ready", i, 1e-5)
                if s == ROUTE1:
                    route(i, 0)
                if s == ROUTE2:
                    route(i, 1)
                if s in XG:
                    e = XG.index(s)
                    ve.wait_ge(S["g_spread"], EXPERTS * i + e + 1)
                    if e >= 2:
                        ve.wait_ge(S["moe_mm"], EXPERTS * i + e - 1)
                    ve.tensor_tensor(xg[:, e % 2, :], xn[:], psA[:, 0, :], ALU.mult).then_inc(S["xg_ready"], 1)
                if s == XA:
                    ve.wait_ge(S["moe_mm"], EXPERTS * (i + 1))
                    ve.tensor_tensor(xa[:], x1[:], psA[:, 1, :], ALU.add).then_inc(S["xa_ready"], 1)
                ln_dve("lnB", B_SLOTS, s, xa, "xa_ready", i, 1e-6)
                if s == XB:
                    ve.wait_ge(S["conv_mm"], i + 1)
                    ve.wait_ge(S["xb_stored"], 16 * i)
                    ve.tensor_tensor(xb[:], xa[:], psA[:, 1, :], ALU.add).then_inc(S["xb_ready"], 1)
                ln_dve("lnC", C_SLOTS, s, xb, "xb_ready", i, 1e-5)
                if s == STATS:
                    ve.wait_ge(S["wx_mm"], i + 1)
                    ve.bn_stats(stats[:, bass.ds(i * 6, 6)] if n_chunks > 3 and not isinstance(i, int)
                                else stats[:, i * 6:i * 6 + 6], psA[:, 1, :]).then_inc(S["stats_ready"], 1)

            def round_dve(i, main, front, back):
                j, m = i - 1, i + 1
                for s in range(END):
                    if main and MIX <= s < MIX + OFFS:
                        o = s - MIX
                        dy = o // NB
                        if o == 0:
                            ve.wait_ge(S["v_ready"], i + 1)
                        ve.wait_ge(S["e_spread"], i * OFFS + o + 1)
                        if o == 4 * NB:
                            dve_column_sums(i, POOL_ROWS)
                        if o == 2 * NB:
                            ve.wait_ge(S["final_mm"], i)
                        if o == 3 * NB:
                            ve.wait_ge(S["hsum_step"], i * 5 * POOL_ROWS + 5)
                        if o == 4 * NB:
                            ve.wait_ge(S["hsum_step"], i * 5 * POOL_ROWS + 10)
                        ve.tensor_tensor(rows(ev_row[dy][:, o % NB, :]), rows(psE[:, o % 4, :]), head_shift(v_pad, o), ALU.mult)\
                            .then_inc(S["ev_ready"], 1)
                    if main and s == COLS:
                        dve_column_sums(i, NB - 1)
                    if main and VERT <= s < VERT + 2:
                        row_sums(i, s - VERT)
                    if NORM <= s < NORM + WINS:
                        n = s - NORM
                        if main:
                            ve.wait_ge(S["r_spread"], i * WINS + n + 1)
                            if n % KW == 0:
                                ve.wait_ge(S["vsum_step"], 5 * i + (2, 4, 5)[n // KW])
                            o_w = win[:, n // KW, n % KW, :]
                            ve.tensor_tensor(o_w, o_w, psB[:, n % 2, :], ALU.mult).then_inc(S["win_ready"], 1)
                        if front:
                            products(m, GROUPS[n])
                        if main and n < 3:
                            row_sums(i, n + 2)
                        if main and n == VARY[0][1]:
                            vary_part(i, 0)
                    if s == SOFT:
                        if main:
                            vary_part(i, 1)
                        if front:
                            soft_shift(m)
                        if main:
                            ve.wait_ge(S["rsy_ready"], 2 * i + 2)
                            ve.wait_ge(S["ok_loaded"], 16 * (i + 1))
                            ve.tensor_tensor(rsv[:], rsy[:].rearrange("p (w t) -> p t w", t=TILES), ok[:, :, 0:WINS], ALU.mult).then_inc(S["rsv_ready"], 1)
                            ve.wait_ge(S["rsv_ready"], i + 1)
                            ve.wait_ge(S["rc_turned"], i)
                            ve.tensor_reduce(rc[:, :, 0:1], rsv[:], AX.X, ALU.add).then_inc(S["rc_ready"], 1)
                            ve.tensor_copy(rc[:, :, 1:2], ok[:, :, WINS:]).then_inc(S["cnt_ready"], 1)
                    if SUM <= s < SUM + WINS:
                        n = s - SUM
                        if main:
                            ve.wait_ge(S["rs_spread"], i * WINS + n + 1)
                            ve.wait_ge(S["proj_mm"], (i + 1) * WINS)
                            o_w = win[:, n // KW, n % KW, :]
                            ve.tensor_tensor(o_w, o_w, psR[:, n % 3, :], ALU.mult).then_inc(S["u_ready"], 1)
                        if front and n < 4:
                            soft_sums(m, n)
                        if front and n in (4, 6):
                            soft_parts(m, n // 2 - 2)
                    if back:
                        back_dve(s, j)
                    if front:
                        front_dve(s, m)
                if main:
                    ve.wait_ge(S["final_mm"], i + 1)
                    ve.wait_ge(S["xres_ready"], i + 1)
                    ve.tensor_tensor(x1[:], xres[:], psF, ALU.add).then_inc(S["x1_ready"], 1)
            rounds(ve, round_dve)
            ve.wait_ge(S["stats_ready"], n_chunks)
            ve.bn_aggr(mv[:], stats[:, 0:6 * n_chunks]).then_inc(S["bn_step"], 1)
            ve.wait_ge(S["bn_step"], 1)
            ve.tensor_scalar(tiny[:, 0:1], mv[:, 1:2], 1.0, 1e-5, ALU.mult, ALU.add).then_inc(S["bn_v"], 1)
            ve.wait_ge(S["bn_rs"], 1)
            ve.tensor_tensor(tiny[:, 4:5], tiny[:, 1:2], cols[:, 3:4], ALU.mult).then_inc(S["bn_step"], 1)
            ve.wait_ge(S["bn_step"], 2)
            ve.tensor_tensor(tiny[:, 6:7], mv[:, 0:1], tiny[:, 4:5], ALU.mult).then_inc(S["bn_step"], 1)
            ve.wait_ge(S["bn_step"], 3)
            ve.tensor_tensor(tiny[:, 5:6], cols[:, 4:5], tiny[:, 6:7], ALU.subtract).then_inc(S["bn_step"], 1)
            ve.wait_ge(S["bn_step"], 4)
            scan_dve(ve)


_INS = ["x_halo", "valid", "w_qkvT", "w_projT", "b_proj", "ln1_g", "ln1_b", "ln2_g", "ln2_b", "router_w", "router_b",
        "expert_w", "expert_b", "conv", "convT", "w_T", "v_T", "gamma", "beta"]


def layouts(inputs):
    import numpy as np
    x = np.asarray(inputs["x"])
    xp = np.zeros((IMGS, P, IMG + 2 * HALO, IMG), x.dtype)
    xp[:, :, HALO:HALO + IMG] = x
    halo = np.stack([xp[:, :, r:r + HROWS] for r in range(0, IMG, ROWS)], 1)
    rr, cc = np.meshgrid(np.arange(IMG), np.arange(IMG), indexing="ij")
    last = IMG - KW
    mask = np.stack([(rr - 2 + a >= 0) & (rr - 2 + a <= last) & (cc - 2 + b >= 0) & (cc - 2 + b <= last)
                     for a in range(KW) for b in range(KW)], -1).astype(np.float32)
    mask = np.concatenate([mask, mask.sum(-1, keepdims=True)], -1)
    mask = mask.reshape(IMG // ROWS, TILES, P, WINS + 1).transpose(0, 2, 1, 3).reshape(IMG // ROWS, P, TILES * (WINS + 1))
    taps = np.asarray(inputs["L1_conv_weight"]).reshape(-1)
    padded = np.zeros(2 * P + 1, taps.dtype)
    padded[P - taps.size // 2:P - taps.size // 2 + taps.size] = taps
    at = P + np.arange(P)[None, :] - np.arange(P)[:, None]
    conv = padded[at]
    got = {
        "x_halo": halo.transpose(2, 0, 1, 3, 4).reshape(P, CHUNKS * HPIX),
        "valid": np.tile(mask, (IMGS, 1, 1)).transpose(1, 0, 2).reshape(P, -1),
        "w_qkvT": inputs["L0_conv_w_qkv"].T, "w_projT": inputs["L0_conv_w_proj"].T,
        "b_proj": inputs["L0_conv_b_proj"], "ln1_g": inputs["L0_conv_ln1_g"], "ln1_b": inputs["L0_conv_ln1_b"],
        "ln2_g": inputs["L0_conv_ln2_g"], "ln2_b": inputs["L0_conv_ln2_b"],
        "router_w": inputs["L0_ffn_router_w"], "router_b": inputs["L0_ffn_router_b"],
        "expert_w": inputs["L0_ffn_expert_w"], "expert_b": inputs["L0_ffn_expert_b"],
        "conv": conv, "convT": conv.T,
        "w_T": inputs["L1_ffn_W"].T, "v_T": inputs["L1_ffn_V"].T,
        "gamma": inputs["L1_ffn_gamma"], "beta": inputs["L1_ffn_beta"],
    }
    return {n: np.ascontiguousarray(got[n]) for n in _INS}


def kernel(**inputs):
    import concourse.bacc as _bacc
    from concourse.bass_utils import run_bass_kernel_spmd as _run

    nc = _bacc.Bacc("TRN2", target_bir_lowering=False, num_devices=1)
    arrays = layouts(inputs)
    args = [nc.dram_tensor(n, a.shape, mybir.dt.from_np(a.dtype), kind="ExternalInput").ap() for n, a in arrays.items()]
    out = nc.dram_tensor("out", (IMGS, P, STEPS), F32, kind="ExternalOutput").ap()
    program(nc, *args, out)
    r = _run(nc, [arrays], core_ids=[0])
    return r.results[0]["out"].reshape(IMGS, P, IMG, IMG)
```

```python
from contextlib import ExitStack

import concourse.bass as bass
from concourse import mybir

F32 = mybir.dt.float32
BF16 = mybir.dt.bfloat16
ALU = mybir.AluOpType
ACT = mybir.ActivationFunctionType
AX = mybir.AxisListType

P = 128
IMGS, IMG = 8, 64
ROWS = 8
PIX = ROWS * IMG
TILES = PIX // P
CHUNKS = IMGS * IMG // ROWS
HALO = 2
HROWS = ROWS + 2 * HALO
HPIX = HROWS * IMG
HTILES = HPIX // P
HALF = HPIX // 2
PADW = IMG + 2 * HALO
HEADS, HD = 8, 16
KW = 3
NB = 2 * KW - 1
OFFS = NB * NB
WINS = KW * KW
EXPERTS = 8
PARTS = 3
STEPS = IMG * IMG
CONV_STEPS = 20
ROUTE = 17
CONSTS = 37

SEQ = [4 * g + m for m in range(4) for g in range(4)] + [16, 20, 24, 17, 21, 18, 22, 19, 23]
BY_POOL = list(range(1, OFFS, 2))
BY_DVE = list(range(0, OFFS, 2))
DVE_RING, POOL_RING = 4, 7
POOL_ROWS = 4
DVE_ROWS = NB - POOL_ROWS

BLK = 128
HBLK = BLK // 2
PIECES = 8


def program(nc, x_halo, valid, w_qkvT, w_projT, b_proj, ln1_g, ln1_b, ln2_g, ln2_b, router_w, router_b,
            expert_w, expert_b, conv, convT, w_T, v_T, gamma, beta, out, n_chunks=CHUNKS,
            n_blocks=STEPS // BLK):
    wx_dram = nc.dram_tensor("wx_scratch", (P, CHUNKS * PIX), F32, kind="Internal").ap()
    xb_dram = nc.dram_tensor("xb_scratch", (P, CHUNKS * PIX), F32, kind="Internal").ap()
    with ExitStack() as ctx:
        def sb(name, shape, dt=F32):
            return ctx.enter_context(nc.sbuf_tensor(name, shape, dt))

        def sem(name):
            return ctx.enter_context(nc.semaphore(name))

        ident = sb("ident", [P, P])
        ident_b = sb("ident_b", [P, P], BF16)
        mean_w = sb("mean_w", [P, 32])
        cent_w = sb("cent_w", [P, P])
        head_sum = sb("head_sum", [P, 4, 32])
        spread = sb("spread", [P, NB, P], BF16)
        minus_half = sb("minus_half", [P, 4 * WINS])
        rank = sb("rank", [P, TILES, EXPERTS])
        wqkv = sb("wqkv", [P, 3, P])
        bqkv = sb("bqkv", [P, 3])
        wproj = sb("wproj", [P, P])
        wproj_g = sb("wproj_g", [P, P])
        prow = sb("prow", [P, 3, P])
        brow = sb("brow", [2, P])
        sel = sb("sel", [2, 2])
        bproj_c = sb("bproj_c", [P, 1])
        cols = sb("cols", [P, 6])
        rw = sb("rw", [P, EXPERTS])
        rb = sb("rb", [P, EXPERTS])
        ew = sb("ew", [P, EXPERTS, P])
        eb = sb("eb", [EXPERTS, P])
        conv_a = sb("conv_a", [P, P])
        conv_mT = sb("conv_mT", [P, P])
        w_in = sb("w_in", [P, P])
        v_rec = sb("v_rec", [P, P])
        tiny = sb("tiny", [P, 8])

        xh = sb("xh", [P, HPIX])
        xres = sb("xres", [P, PIX])
        xc0 = sb("xc0", [P, HPIX])
        var0 = sb("var0", [P, HTILES])
        rs0 = sb("rs0", [P, HTILES])
        q = sb("q", [P, PIX])
        k_pad = sb("k_pad", [P, HROWS, PADW])
        v_pad = sb("v_pad", [P, HROWS, PADW])
        prod_d = sb("prod_d", [P, DVE_RING, PIX])
        prod_p = sb("prod_p", [P, POOL_RING, PIX])
        s2 = sb("s2", [P, 2, PIX])
        sq0 = s2[:].rearrange("p b n -> p (b n)")[:, 0:HPIX]
        smax = sb("smax", [P, TILES, HEADS])
        es = sb("es", [P, TILES, OFFS, HEADS])
        e32 = sb("e32", [P, TILES, OFFS, HEADS])
        erest = es
        e3 = sb("e3", [P, TILES, OFFS, PARTS, HEADS], BF16)
        dsum_a = sb("dsum_a", [P, TILES * NB, KW * HEADS])
        dsum_h = sb("dsum_h", [P, TILES, NB, KW * HEADS])
        dsum_b = sb("dsum_b", [P, TILES, KW * KW * HEADS])
        dsum = sb("dsum", [P, TILES, WINS * HEADS])
        rden = sb("rden", [P, TILES, WINS, HEADS])
        rrest = sb("rrest", [P, TILES, WINS, HEADS])
        r3 = sb("r3", [P, TILES, WINS, PARTS, HEADS], BF16)
        eT = sb("eT", [NB * PARTS * HEADS, NB, PIX], BF16)
        rT = sb("rT", [KW * PARTS * HEADS, KW, PIX], BF16)
        ev = sb("ev", [P, 2, NB, PIX])
        hs_a = sb("hs_a", [P, 2, 2, PIX])
        hs_b = sb("hs_b", [P, 2, PIX])
        hs = sb("hs", [P, NB, KW, PIX])
        vs = sb("vs", [P, 2, KW, PIX])
        win = sb("win", [P, KW, KW, PIX])
        conv_bT = hs[:, 0, 0, 0:P]
        win9 = win[:].rearrange("p a b n -> p (a b) n")
        ev_row = [ev[:, 0], ev[:, 1], win9[:, 0:NB], ev[:, 0], ev[:, 1]]
        conv_s = win[:].rearrange("p a b n -> p (a b n)")[:, 0:(CONV_STEPS + 1) * P]\
            .rearrange("p (k n) -> p k n", n=P)
        sqy = sb("sqy", [P, 2, PIX])
        ok = sb("ok", [P, TILES, WINS + 1])
        vary = sb("vary", [P, TILES * WINS])
        rsy = sb("rsy", [P, WINS * TILES])
        rsv = sb("rsv", [P, TILES, WINS])
        rc = sb("rc", [P, TILES, 2])
        rcT = sb("rcT", [2, PIX])
        x1 = sb("x1", [P, PIX])
        xc = sb("xc", [P, PIX])
        sq = sb("sq", [P, PIX])
        xn = sb("xn", [P, PIX])
        var = sb("var", [P, TILES])
        rs = sb("rs", [P, TILES])
        logit = sb("logit", [P, TILES, EXPERTS])
        hot = sb("hot", [P, 2, TILES, EXPERTS])
        rt = sb("rt", [P, 4, TILES, EXPERTS])
        top = sb("top", [P, 8, TILES])
        gate = sb("gate", [P, TILES, EXPERTS])
        gT = sb("gT", [EXPERTS, PIX])
        xg = sb("xg", [P, 2, PIX])
        xa = sb("xa", [P, PIX])
        xb = sb("xb", [P, PIX])
        wx = sb("wx", [P, PIX])
        stats = sb("stats", [P, CHUNKS * 6])
        mv = sb("mv", [P, 2])
        n = IMGS * BLK
        wxr, xbr, outb = [hs[:].rearrange("p a b n -> p (a b n)")[:, k * n:(k + 1) * n]
                          .rearrange("p (b t) -> p b t", t=BLK) for k in range(3)]
        z, y = [hs[:].rearrange("p a b n -> p (a b n)")[:, k * n:(k + 1) * n]
                .rearrange("p (h t b) -> p h t b", h=2, b=IMGS) for k in (3, 4)]

        ps = ctx.enter_context(nc.psum_tensor("ps", [P, 8, 512], F32))
        psA = ps[:, 0:2, :]
        psP = ps[:, 2:4, :]
        psS = ps[:, 2:4, :].rearrange("p b (t c) -> p (b t) c", c=256)
        psT = ps[:, 2:4, :].rearrange("p b c -> p (b c)").bitcast(BF16)
        psB = ps[:, 4:6, :]
        psE = ps[:, 4:8, :]
        sqy_slot = [sqy[:, 0], sqy[:, 1], hs_a[:, 0, 0], hs_a[:, 0, 1], hs_a[:, 1, 0], hs_a[:, 1, 1], hs_b[:, 0], hs_b[:, 1], sqy[:, 0]]
        var_row = hs[:, 0, 0, :]
        psR = ps[:, 4:7, :]
        psY = ps[:, 6, :]
        psF = ps[:, 7, :]

        names = """consts weights w_scaled w_ready setup_pe setup_dve
            x_loaded ok_loaded xres_loaded
            pre_mean pre_cent pre_sq pre_var pre_v pre_rs pre_bc pre_xn k_mm k_ready v_mm v_ready q_mm q_ready
            prod_dve prod_pool reduced s2_ready s_turned smax_ready es_ready e_ready e_hi e_rest e_mid e_lo
            dsum_step r_ready r_hi r_rest r_mid r_lo e_turned eT_ready e_spread ev_ready hsum_step hsum_dve vsum_step
            r_spread win_ready proj_mm sqy_ready vary_mm var_row var_turned vary_ready rsy_ready rsv_ready rc_ready cnt_ready
            rc_turned rcT_ready rs_spread u_ready final_mm x1_ready
            lnA_mean lnA_cent lnA_sq lnA_var lnA_v lnA_rs lnA_bc lnA_xn
            lnB_mean lnB_cent lnB_sq lnB_var lnB_v lnB_rs lnB_bc lnB_xn
            lnC_mean lnC_cent lnC_sq lnC_var lnC_v lnC_rs lnC_bc lnC_xn
            logit_mm route_step gap_ready exp_ready g_ready g_turned gT_ready g_spread xg_ready moe_mm xa_ready
            conv_mm xb_ready wx_mm wx_ready stats_ready xb_stored wx_stored
            bn_step bn_v bn_rs z_loaded z_ready z_used step_mm y_ready res_loaded out_ready out_stored""".split()
        S = {n: sem(n) for n in names}
        block = ctx.enter_context(nc.Block())

        def head_shift(t, off):
            dy, dx = off // NB, off % NB
            return t[:, dy:dy + ROWS, dx:dx + IMG]

        def rows(a):
            return a.rearrange("p (r c) -> p r c", c=IMG)

        LOADS = 2 + 5 + 3 + 1 + 1 + 2 + 2 + 2

        MIX = 0
        COLS = MIX + OFFS
        VERT = COLS + 1
        NORM = VERT + 2
        SOFT = NORM + WINS
        SUM = SOFT + 1
        END = SUM + WINS
        F_MEAN, F_CENT, F_VAR, F_V, F_BC, F_XN, F_K, F_Q, F_VAL = 3, 5, 7, 9, 12, 14, 16, 18, COLS
        GROUPS = [[]] + [range(4 * n, 4 * n + 4) for n in range(4)] + [range(16, 19), range(19, 21), range(21, 23), range(23, 25)]
        X1 = 1
        A_SLOTS, B_SLOTS, C_SLOTS = (0, 1, 3, 4, 6, 7), (28, 29, 30, 31, 33, 34), (36, 36, 38, 39, 42, 43)
        LOGIT, ROUTE1, ROUTE2, G_TURN = 8, 10, 12, 13
        XG = [15, 17, 19, 21, 23, 24, 25, 26]
        AHEAD = 3
        VARY = [(0, 4), (4, 8), (8, WINS)]
        XA, XB, STATS = 27, 35, 45

        def rounds(eng, body):
            body(-1, False, True, False)
            body(0, True, n_chunks > 1, False)
            if n_chunks > 2:
                body(1, True, True, True)
            if n_chunks > 3:
                with eng.Fori(2, n_chunks - 1) as i:
                    body(i, True, True, True)
            if n_chunks > 1:
                body(n_chunks - 1, True, False, True)
            body(n_chunks, False, False, True)

        def dram_block(a, at, ahead):
            a = a.rearrange("p (b t) -> p b t", b=IMGS)
            return (a[:, :, BLK:] if ahead else a)[:, :, bass.ds(at, BLK)]

        def scan_sp(sp):
            def load_wx(halves, at, ahead):
                sp.wait_ge(S["z_ready"], halves)
                sp.dma_start(wxr, dram_block(wx_dram, at, ahead)).then_inc(S["z_loaded"], 16)

            def load_res(halves, at, ahead):
                sp.wait_ge(S["out_ready"], halves)
                sp.dma_start(xbr, dram_block(xb_dram, at, ahead)).then_inc(S["res_loaded"], 16)

            def store(at):
                sp.dma_start(out.rearrange("b c t -> c b t")[:, :, bass.ds(at, BLK)], outb)\
                    .then_inc(S["out_stored"], 16)
            load_wx(0, 0, False)
            load_res(0, 0, False)
            if n_blocks > 1:
                with sp.Fori(0, n_blocks - 1) as n:
                    at = sp.snap(n * BLK)
                    halves = sp.snap(n * 2 + 2)
                    load_wx(halves, at, True)
                    load_res(halves, at, True)
                    store(at)
            sp.wait_ge(S["out_ready"], 2 * n_blocks)
            store((n_blocks - 1) * BLK)
            sp.wait_ge(S["out_stored"], 16 * n_blocks)

        def scan_dve(ve):
            def half(n, h):
                ve.wait_ge(S["z_loaded"], 16 * (n + 1))
                ve.tensor_scalar(z[:, h], wxr[:, :, HBLK * h:HBLK * (h + 1)].rearrange("p b t -> p t b"),
                                 tiny[:, 4:5], tiny[:, 5:6], ALU.mult, ALU.add).then_inc(S["z_ready"], 1)
            half(0, 0)
            half(0, 1)
            if n_blocks > 1:
                with ve.Fori(1, n_blocks) as n:
                    for h in range(2):
                        ve.wait_ge(S["z_used"], 2 * n + h - 1)
                        half(n, h)

        def scan_pe(pe):
            def preload(h, piece):
                c = piece * PIX // PIECES
                m = pe.matmul(ps[:, h, c:c + PIX // PIECES], ident[:],
                              z[:, h].rearrange("p t b -> p (t b)")[:, c:c + PIX // PIECES],
                              start=piece == 0, stop=True, skip_group_check=True)
                if piece == PIECES - 1:
                    m.then_inc(S["z_used"], 1)

            def steps(n, h, last):
                every = HBLK // PIECES
                for j in range(HBLK):
                    pe.wait_ge(S["y_ready"], (2 * n + h) * HBLK + j + 1)
                    prev = y[:, h, j - 1, :] if j else y[:, 1 - h, HBLK - 1, :]
                    for g in range(4):
                        m = pe.matmul(ps[32 * g:32 * g + 32, h, IMGS * j:IMGS * (j + 1)], v_rec[:, 32 * g:32 * g + 32],
                                      prev, start=False, stop=True, skip_group_check=True)
                    m.then_inc(S["step_mm"], 1)
                    if j % every == every // 2 and not last:
                        if j == every // 2:
                            pe.wait_ge(S["z_ready"], 2 * n + h + 2)
                        preload(1 - h, j // every)
            pe.wait_ge(S["y_ready"], 1)
            pe.wait_ge(S["z_ready"], 1)
            for piece in range(PIECES):
                preload(0, piece)
            if n_blocks > 1:
                with pe.Fori(0, n_blocks - 1) as n:
                    steps(n, 0, False)
                    steps(n, 1, False)
            steps(n_blocks - 1, 0, False)
            steps(n_blocks - 1, 1, True)

        def scan_act(ac):
            def steps(n, h, first):
                if not first:
                    ac.wait_ge(S["out_ready"], 2 * n + h - 1)
                for j in range(HBLK):
                    ac.wait_ge(S["step_mm"], (2 * n + h) * HBLK + j + 1)
                    ac.activation(y[:, h, j, :], ps[:, h, IMGS * j:IMGS * (j + 1)], ACT.Sigmoid).then_inc(S["y_ready"], 1)
            steps(0, 0, True)
            steps(0, 1, True)
            if n_blocks > 1:
                with ac.Fori(1, n_blocks) as n:
                    steps(n, 0, False)
                    steps(n, 1, False)

        def scan_pool(pl):
            pl.memset(y[:, 1], 0.0).then_inc(S["y_ready"], 1)

            def add(n):
                pl.wait_ge(S["res_loaded"], 16 * (n + 1))
                for h in range(2):
                    pl.wait_ge(S["y_ready"], (2 * n + h + 1) * HBLK + 1)
                    pl.tensor_tensor(outb[:, :, HBLK * h:HBLK * (h + 1)], xbr[:, :, HBLK * h:HBLK * (h + 1)],
                                     y[:, h].rearrange("p t b -> p b t"), ALU.add).then_inc(S["out_ready"], 1)
            add(0)
            if n_blocks > 1:
                with pl.Fori(1, n_blocks) as n:
                    pl.wait_ge(S["out_stored"], 16 * n)
                    add(n)

        @block.sync
        def _(sp):
            sp.dma_start(wqkv[:], w_qkvT).then_inc(S["weights"], 16)
            sp.dma_start(wproj[:], w_projT).then_inc(S["weights"], 16)
            for n, v in enumerate((ln1_g, ln1_b, b_proj, gamma, beta)):
                sp.dma_start(cols[:, n:n + 1], v.rearrange("(p a) -> p a", a=1)).then_inc(S["weights"], 16)
            for n, v in enumerate((b_proj, ln2_g, ln2_b)):
                sp.dma_start(prow[:, n, :], v.partition_broadcast(P)).then_inc(S["weights"], 16)
            sp.dma_start(rb[:], router_b.partition_broadcast(P)).then_inc(S["weights"], 16)
            sp.dma_start(rw[:], router_w).then_inc(S["weights"], 16)
            sp.dma_start(ew[:], expert_w.rearrange("e d c -> d e c")).then_inc(S["weights"], 16)
            sp.dma_start(eb[:], expert_b).then_inc(S["weights"], 16)
            sp.dma_start(conv_a[:], conv).then_inc(S["weights"], 16)
            sp.dma_start(conv_mT[:], convT).then_inc(S["weights"], 16)
            sp.dma_start(w_in[:], w_T).then_inc(S["weights"], 16)
            sp.dma_start(v_rec[:], v_T).then_inc(S["weights"], 16)
            def load(i, at_x):
                if not isinstance(i, int) or i:
                    sp.wait_ge(S["pre_mean"], i)
                sp.dma_start(xh[:], x_halo[:, bass.ds(at_x, HPIX)]).then_inc(S["x_loaded"], 16)

            def load_res(i, at_res):
                if not isinstance(i, int) or i:
                    sp.wait_ge(S["x1_ready"], i)
                sp.dma_start(xres[:], x_halo[:, bass.ds(at_res, PIX)]).then_inc(S["xres_loaded"], 16)

            def load_mask(i, at_ok):
                if not isinstance(i, int) or i:
                    sp.wait_ge(S["cnt_ready"], i)
                sp.dma_start(ok[:].rearrange("p t w -> p (t w)"), valid[:, bass.ds(at_ok, TILES * (WINS + 1))])\
                    .then_inc(S["ok_loaded"], 16)

            def store(i, at):
                sp.wait_ge(S["xb_ready"], i + 1)
                sp.dma_start(xb_dram[:, bass.ds(at, PIX)], xb[:]).then_inc(S["xb_stored"], 16)
                sp.wait_ge(S["wx_ready"], i + 1)
                sp.dma_start(wx_dram[:, bass.ds(at, PIX)], wx[:]).then_inc(S["wx_stored"], 16)
            mask = TILES * (WINS + 1)
            inner = HALO * IMG
            load(0, 0)
            load_mask(0, 0)
            load_res(0, inner)
            for i in (1, 2):
                if i < n_chunks:
                    load(i, i * HPIX)
                    load_mask(i, i * mask)
            if n_chunks > 3:
                with sp.Fori(3, n_chunks) as i:
                    at_x, at_ok, at = sp.snap(i * HPIX), sp.snap(i * mask), sp.snap(i * PIX - 3 * PIX)
                    before, at_res = sp.snap(i - 2), sp.snap(i * HPIX - 2 * HPIX + inner)
                    load(i, at_x)
                    load_res(before, at_res)
                    sp.wait_ge(S["xb_ready"], before)
                    sp.dma_start(xb_dram[:, bass.ds(at, PIX)], xb[:]).then_inc(S["xb_stored"], 16)
                    sp.wait_ge(S["wx_ready"], before)
                    sp.dma_start(wx_dram[:, bass.ds(at, PIX)], wx[:]).then_inc(S["wx_stored"], 16)
                    load_mask(i, at_ok)
            for i in range(max(n_chunks - 3, 0), n_chunks):
                if 0 < i + 1 < n_chunks:
                    load_res(i + 1, (i + 1) * HPIX + inner)
                store(i, i * PIX)
            sp.wait_ge(S["xb_stored"], 16 * n_chunks)
            sp.wait_ge(S["wx_stored"], 16 * n_chunks)
            scan_sp(sp)

        @block.gpsimd
        def _(pl):
            n = [0]

            def done(ins):
                n[0] += 1
                ins.then_inc(S["consts"], 1)
                pl.wait_ge(S["consts"], n[0])
            done(pl.memset(mean_w[:], 1.0 / P))
            done(pl.memset(cent_w[:], -1.0 / P))
            done(pl.affine_select(out=cent_w[:], in_=cent_w[:], compare_op=ALU.not_equal, fill=1.0 - 1.0 / P, base=0,
                                  pattern=[[-1, P]], channel_multiplier=1))
            done(pl.memset(minus_half[:], -0.5))
            done(pl.memset(k_pad[:], 0.0))
            done(pl.memset(v_pad[:], 0.0))
            for m in (ident, ident_b):
                done(pl.memset(m[:], 0.0))
                done(pl.affine_select(out=m[:], in_=m[:], compare_op=ALU.not_equal, fill=1.0, base=0,
                                      pattern=[[-1, P]], channel_multiplier=1))
            done(pl.memset(sel[:], 0.0))
            done(pl.affine_select(out=sel[:], in_=sel[:], compare_op=ALU.not_equal, fill=1.0, base=0,
                                  pattern=[[-1, 2]], channel_multiplier=1))
            done(pl.memset(head_sum[:], 0.0))
            for m in range(4):
                part = head_sum[:, m, 8 * m:8 * m + HEADS]
                done(pl.memset(part, 1.0))
                done(pl.affine_select(out=part, in_=part, compare_op=ALU.is_ge, fill=0.0, base=0,
                                      pattern=[[-HD, HEADS]], channel_multiplier=1))
                done(pl.affine_select(out=part, in_=part, compare_op=ALU.is_ge, fill=0.0, base=HD - 1,
                                      pattern=[[HD, HEADS]], channel_multiplier=-1))
            done(pl.memset(spread[:], 0.0))
            for s in range(PARTS):
                sp4 = spread[:].rearrange("p d (h c) -> p d h c", c=HD)
                done(pl.affine_select(out=sp4, in_=sp4, compare_op=ALU.not_equal, fill=1.0,
                                      base=-HEADS * s, pattern=[[-PARTS * HEADS, NB], [-1, HEADS], [0, HD]],
                                      channel_multiplier=1))
            for e in range(EXPERTS):
                done(pl.memset(rank[:, :, e:e + 1], float(e - EXPERTS)))
            assert n[0] == CONSTS

            def power(tag, out_, in_, i):
                pl.wait_ge(S[tag + "_v"], i + 1)
                pl.tensor_tensor(out_, in_, minus_half[:, 0:in_.shape[1]], ALU.pow).then_inc(S[tag + "_rs"], 1)

            def products(i, which):
                for n in which:
                    pl.wait_ge(S["k_ready"], i + 1)
                    pl.wait_ge(S["q_ready"], i + 1)
                    if n >= POOL_RING:
                        pl.wait_ge(S["reduced"], i * OFFS + BY_POOL[n - POOL_RING] + 1)
                    elif n == 0:
                        pl.wait_ge(S["reduced"], i * OFFS)
                    pl.tensor_tensor(rows(prod_p[:, n % POOL_RING, :]), rows(q[:]), head_shift(k_pad, SEQ[BY_POOL[n]]),
                                     ALU.mult).then_inc(S["prod_pool"], 1)

            def column_sums(i, dy):
                pl.wait_ge(S["ev_ready"], i * OFFS + NB * (dy + 1))
                e, a, o = ev_row[dy], hs_a[:, dy % 2], hs[:, dy]
                c = i * 5 * POOL_ROWS + 5 * dy
                if dy >= 2:
                    pl.wait_ge(S["hsum_step"], c - 5)
                pl.tensor_tensor(a[:, 0, :], e[:, 1, :], e[:, 2, :], ALU.add).then_inc(S["hsum_step"], 1)
                pl.tensor_tensor(a[:, 1, :], e[:, 3, :], e[:, 4, :], ALU.add).then_inc(S["hsum_step"], 1)
                pl.wait_ge(S["hsum_step"], c + 1)
                pl.tensor_tensor(o[:, 0, :], e[:, 0, :], a[:, 0, :], ALU.add).then_inc(S["hsum_step"], 1)
                pl.tensor_tensor(o[:, 1, :], e[:, 3, :], a[:, 0, :], ALU.add).then_inc(S["hsum_step"], 1)
                pl.wait_ge(S["hsum_step"], c + 2)
                pl.tensor_tensor(o[:, 2, :], e[:, 2, :], a[:, 1, :], ALU.add).then_inc(S["hsum_step"], 1)

            def round_pool(i, main, front, back):
                j, m = i - 1, i + 1
                if back:
                    pl.wait_ge(S["lnC_bc"], j)
                    power("lnA", rs[:], var[:], j)
                if main:
                    column_sums(i, 0)
                if front:
                    pl.wait_ge(S["pre_bc"], m)
                    power("pre", rs0[:], var0[:], m)
                if main:
                    for dy in range(1, POOL_ROWS):
                        column_sums(i, dy)
                if front:
                    products(m, range(len(BY_POOL)))
                if back:
                    pl.wait_ge(S["lnA_bc"], j + 1)
                    power("lnB", rs[:], var[:], j)
                if main:
                    for part, (w0, w1) in enumerate(VARY):
                        pl.wait_ge(S["vary_ready"], 3 * i + part + 1)
                        pl.tensor_tensor(rsy[:, w0 * TILES:w1 * TILES], vary[:, w0 * TILES:w1 * TILES],
                                         minus_half[:, 0:(w1 - w0) * TILES], ALU.pow).then_inc(S["rsy_ready"], 1)
                if back:
                    pl.wait_ge(S["lnB_bc"], j + 1)
                    power("lnC", rs[:], var[:], j)
            rounds(pl, round_pool)
            pl.wait_ge(S["bn_v"], 1)
            pl.tensor_tensor(tiny[:, 1:2], tiny[:, 0:1], minus_half[:, 0:1], ALU.pow).then_inc(S["bn_rs"], 1)
            scan_pool(pl)

        @block.tensor
        def _(pe):
            def turn(dst, src, idn):
                return pe.matmul(dst, src, idn, start=True, stop=True, is_transpose=True)

            def ln_pe(tag, slots, s, x, ready, i):
                if s == slots[0]:
                    pe.wait_ge(S[ready], i + 1)
                    pe.matmul(psA[:, 0, :], cent_w[:], x[:], start=True, stop=True).then_inc(S[tag + "_mean"], 1)
                if s == slots[2]:
                    pe.wait_ge(S[tag + "_cent"], i + 1)
                    pe.wait_ge(S[tag + "_sq"], i + 1)
                    for t in range(TILES):
                        m = pe.matmul(psA[:, 0, t:t + 1], sq[:, P * t:P * t + P], mean_w[:, 0:1], start=True, stop=True)
                    m.then_inc(S[tag + "_var"], 1)
                if s == slots[4]:
                    pe.wait_ge(S[tag + "_v"], i + 1)
                    pe.wait_ge(S[tag + "_rs"], i + 1)
                    for t in range(TILES):
                        m = turn(psA[:, 0, P * t:P * t + P], rs[:, t:t + 1].to_broadcast([P, P]), ident[:])
                    m.then_inc(S[tag + "_bc"], 1)

            pe.wait_ge(S["consts"], CONSTS)
            pe.wait_ge(S["weights"], 16 * LOADS)
            for n in range(3):
                pe.matmul(psA[:, 0, n:n + 1], wqkv[:, n, :], cols[:, 1:2], start=True, stop=True)
            pe.matmul(psA[:, 0, 4:5], cent_w[:], cols[:, 2:3], start=True, stop=True).then_inc(S["setup_pe"], 1)
            for n in range(CONV_STEPS):
                pe.wait_ge(S["setup_dve"], n + 1)
                pe.matmul(psB[:, n % 2, 0:P], conv_bT, conv_s[:, n, :], start=True, stop=True).then_inc(S["setup_pe"], 1)
            pe.wait_ge(S["setup_dve"], CONV_STEPS + 1)
            turn(psB[:, 0, 0:P], conv_s[:, CONV_STEPS, :], ident[:]).then_inc(S["setup_pe"], 1)
            pe.wait_ge(S["w_ready"], 1)

            ge, gr = NB * PARTS * HEADS, KW * PARTS * HEADS

            def front_pe(s, i):
                if s == F_MEAN:
                    pe.wait_ge(S["x_loaded"], 16 * (i + 1))
                    pe.wait_ge(S["eT_ready"], 4 * i)
                    for h in range(2):
                        m = pe.matmul(psP[:, h, 0:HALF], cent_w[:], xh[:, h * HALF:(h + 1) * HALF], start=True, stop=True)
                    m.then_inc(S["pre_mean"], 1)
                if s == F_VAR:
                    pe.wait_ge(S["pre_cent"], i + 1)
                    pe.wait_ge(S["pre_sq"], i + 1)
                    for t in range(HTILES):
                        m = pe.matmul(psP[:, 0, t:t + 1], sq0[:, P * t:P * t + P], mean_w[:, 0:1], start=True, stop=True)
                    m.then_inc(S["pre_var"], 1)
                if s == F_BC:
                    pe.wait_ge(S["pre_v"], i + 1)
                    pe.wait_ge(S["pre_rs"], i + 1)
                    for t in range(HTILES):
                        m = turn(psP[:, t // 3, P * (t % 3):P * (t % 3) + P], rs0[:, t:t + 1].to_broadcast([P, P]), ident[:])
                    m.then_inc(S["pre_bc"], 1)
                if s == F_K:
                    pe.wait_ge(S["pre_xn"], i + 1)
                    for h in range(2):
                        m = pe.matmul(psP[:, h, 0:HALF], wqkv[:, 1, :], xc0[:, h * HALF:(h + 1) * HALF], start=True, stop=True)
                    m.then_inc(S["k_mm"], 1)
                if s == F_Q:
                    pe.wait_ge(S["k_ready"], i + 1)
                    pe.matmul(psP[:, 0, :], wqkv[:, 0, :], xc0[:, HALO * IMG:HALO * IMG + PIX], start=True, stop=True)\
                        .then_inc(S["q_mm"], 1)
                if s == F_VAL:
                    pe.wait_ge(S["q_ready"], i + 1)
                    for h in range(2):
                        m = pe.matmul(psP[:, h, 0:HALF], wqkv[:, 2, :], xc0[:, h * HALF:(h + 1) * HALF], start=True, stop=True)
                    m.then_inc(S["v_mm"], 1)

            def reduce_scores(i, group):
                if 0 in group:
                    pe.wait_ge(S["v_ready"], i + 1)
                for kk in reversed(group):
                    if kk in BY_DVE:
                        pe.wait_ge(S["prod_dve"], i * len(BY_DVE) + BY_DVE.index(kk) + 1)
                        break
                for kk in reversed(group):
                    if kk in BY_POOL:
                        pe.wait_ge(S["prod_pool"], i * len(BY_POOL) + BY_POOL.index(kk) + 1)
                        break
                for kk in group:
                    off = SEQ[kk]
                    src = prod_d[:, BY_DVE.index(kk) % DVE_RING, :] if kk in BY_DVE else prod_p[:, BY_POOL.index(kk) % POOL_RING, :]
                    T, g, m4 = off // 16, off % 16 // 4, off % 4
                    last = m4 == 3 or off == OFFS - 1
                    pe.matmul(psP[32 * g:32 * g + 32, T, :], head_sum[:, m4, :], src, start=m4 == 0, stop=last)\
                        .then_inc(S["reduced"], 1)

            def turn_scores(i):
                for T in range(2):
                    n = P if T == 0 else OFFS * HEADS - P
                    pe.wait_ge(S["s2_ready"], 2 * i + 2)
                    for t in range(TILES):
                        m = turn(psS[:, t, P * T:P * T + n], s2[0:n, T, P * t:P * t + P], ident[0:n, 0:n])
                m.then_inc(S["s_turned"], 1)

            def turn_e(i, part):
                if part == 0:
                    pe.wait_ge(S["es_ready"], i + 1)
                    pe.wait_ge(S["e_hi"], i + 1)
                    pe.wait_ge(S["e_mid"], i + 1)
                    pe.wait_ge(S["e_lo"], i + 1)
                    for g in range(4):
                        for t in range(TILES):
                            c = PIX * g + P * t
                            m = turn(psT[0:ge, c:c + P], e3[:, t, NB * g:NB * g + NB].rearrange("p o s h -> p (o s h)"), ident_b[:])
                        if g % 2:
                            m.then_inc(S["e_turned"], 1)
                else:
                    pe.wait_ge(S["eT_ready"], 4 * i + 1)
                    for t in range(TILES):
                        m = turn(psT[0:ge, P * t:P * t + P], e3[:, t, NB * 4:NB * 5].rearrange("p o s h -> p (o s h)"), ident_b[:])
                    m.then_inc(S["e_turned"], 1)

            def turn_r(i):
                pe.wait_ge(S["r_hi"], i + 1)
                pe.wait_ge(S["r_mid"], i + 1)
                pe.wait_ge(S["r_lo"], i + 1)
                for g in range(KW):
                    if g == 1:
                        pe.wait_ge(S["eT_ready"], 4 * i + 2)
                    for t in range(TILES):
                        c = PIX * (g + 1) + P * t
                        m = turn(psT[0:gr, c:c + P], r3[:, t, KW * g:KW * g + KW].rearrange("p o s h -> p (o s h)"), ident_b[:])
                m.then_inc(S["e_turned"], 1)

            def r_spread(i, n):
                b = n % 2
                if n < 2:
                    pe.wait_ge(S["ev_ready"], (i + 1) * OFFS)
                else:
                    pe.wait_ge(S["win_ready"], i * WINS + n - 1)
                pe.matmul(psB[:, b, :], spread[0:gr, n % KW, :], rT[:, n // KW, :], start=True, stop=True)\
                    .then_inc(S["r_spread"], 1)

            def var_y(i, n):
                pe.wait_ge(S["sqy_ready"], i * WINS + n + 1)
                if n < WINS - 1:
                    if n == 7:
                        pe.wait_ge(S["vary_ready"], 3 * i + 1)
                    for g in range(4):
                        m = pe.matmul(psF[32 * g:32 * g + 32, :], mean_w[:], sqy_slot[n - 3 + g], start=True, stop=True)
                else:
                    pe.wait_ge(S["vary_ready"], 3 * i + 2)
                    for t in range(TILES):
                        m = pe.matmul(psF[:, t:t + 1], sqy_slot[n][:, P * t:P * t + P], mean_w[:, 0:1], start=True, stop=True)
                m.then_inc(S["vary_mm"], 1)

            def turn_var(i, batch):
                pe.wait_ge(S["var_row"], 2 * i + batch + 1)
                for t in range(TILES):
                    m = turn(psF[:, P * t:P * t + P], var_row[:, P * t:P * t + P], ident[:])
                m.then_inc(S["var_turned"], 1)

            def e_spread(o):
                pe.matmul(psE[:, o % 4, :], spread[0:ge, o % NB, :], eT[:, o // NB, :], start=True, stop=True)\
                    .then_inc(S["e_spread"], 1)

            def rs_spread(i, n):
                if n < 2:
                    pe.wait_ge(S["rsv_ready"], 2 * i + 1)
                    pe.wait_ge(S["win_ready"], (i + 1) * WINS)
                elif n == 2:
                    pe.wait_ge(S["sqy_ready"], (i + 1) * WINS)
                else:
                    pe.wait_ge(S["u_ready"], i * WINS + n - 2)
                if n >= 4:
                    pe.wait_ge(S["rsv_ready"], 2 * i + 2)
                for t in range(TILES):
                    m = turn(psR[:, n % 3, P * t:P * t + P], rsv[:, t, n:n + 1].to_broadcast([P, P]), ident[:])
                m.then_inc(S["rs_spread"], 1)

            def back_pe(s, i, main):
                ln_pe("lnA", A_SLOTS, s, x1, "x1_ready", i)
                if s == LOGIT:
                    pe.wait_ge(S["lnA_xn"], i + 1)
                    for t in range(TILES):
                        m = pe.matmul(psA[:, 1, EXPERTS * t:EXPERTS * (t + 1)], xn[:, P * t:P * t + P], rw[:], start=True, stop=True)
                    m.then_inc(S["logit_mm"], 1)
                if s == G_TURN:
                    pe.wait_ge(S["g_ready"], i + 1)
                    for t in range(TILES):
                        m = turn(psA[0:EXPERTS, 1, P * t:P * t + P], gate[:, t, :], ident[:])
                    m.then_inc(S["g_turned"], 1)
                if s in [G_TURN + 1] + XG[:-1]:
                    e = ([G_TURN + 1] + XG).index(s)
                    if e:
                        pe.wait_ge(S["xg_ready"], i * EXPERTS + e)
                    for t in range(TILES):
                        m = turn(psA[:, 0, P * t:P * t + P], gate[:, t, e:e + 1].to_broadcast([P, P]), ident[:])
                    m.then_inc(S["g_spread"], 1)
                if s in XG:
                    e = XG.index(s)
                    pe.wait_ge(S["xg_ready"], i * EXPERTS + e + 1)
                    if e == 0:
                        pe.wait_ge(S["gT_ready"], i + 1)
                        pe.matmul(psA[:, 1, :], eb[:], gT[:], start=True, stop=False)
                    pe.matmul(psA[:, 1, :], ew[:, e, :], xg[:, e % 2, :], start=False, stop=e == EXPERTS - 1)\
                        .then_inc(S["moe_mm"], 1)
                ln_pe("lnB", B_SLOTS, s, xa, "xa_ready", i)
                if s == B_SLOTS[5]:
                    pe.wait_ge(S["lnB_xn"], i + 1)
                    pe.matmul(psA[:, 1, :], conv_mT[:], xn[:], start=True, stop=True).then_inc(S["conv_mm"], 1)
                ln_pe("lnC", C_SLOTS, s, xb, "xb_ready", i)
                if s == C_SLOTS[5]:
                    pe.wait_ge(S["lnC_xn"], i + 1)
                    if main:
                        pe.wait_ge(S["rcT_ready"], i + 2)
                    pe.matmul(psA[:, 1, :], w_in[:], xn[:], start=True, stop=True).then_inc(S["wx_mm"], 1)

            def round_pe(i, main, front, back):
                j, m = i - 1, i + 1
                for s in range(END):
                    if main and MIX <= s < MIX + OFFS:
                        o = s - MIX
                        if o == 0:
                            pe.wait_ge(S["x1_ready"], i)
                        else:
                            pe.wait_ge(S["ev_ready"], i * OFFS + o)
                        if o + AHEAD == 4 * NB:
                            pe.wait_ge(S["eT_ready"], 4 * i + 3)
                        if o + AHEAD < OFFS:
                            e_spread(o + AHEAD)
                    if NORM <= s < NORM + WINS:
                        n = s - NORM
                        if main:
                            if n == 0:
                                pe.wait_ge(S["eT_ready"], 4 * i + 4)
                                r_spread(i, 0)
                            if n + 1 < WINS:
                                r_spread(i, n + 1)
                            pe.wait_ge(S["win_ready"], i * WINS + n + 1)
                            if n:
                                pe.wait_ge(S["sqy_ready"], i * WINS + n)
                            pe.matmul(psY, wproj[:], win[:, n // KW, n % KW, :], start=True, stop=True).then_inc(S["proj_mm"], 1)
                            if n in (4, 8):
                                var_y(i, n - 1)
                            if n == 5:
                                turn_var(i, 0)
                        if front:
                            reduce_scores(m, GROUPS[n])
                    if s == SOFT:
                        if main:
                            rs_spread(i, 0)
                            rs_spread(i, 1)
                            turn_var(i, 1)
                            rs_spread(i, 2)
                            var_y(i, WINS - 1)
                        if front:
                            turn_scores(m)
                    if SUM <= s < SUM + WINS:
                        n = s - SUM
                        if main:
                            if n == 0:
                                pe.wait_ge(S["vary_ready"], 3 * i + 3)
                            pe.wait_ge(S["u_ready"], i * WINS + n + 1)
                            if n + 3 < WINS:
                                rs_spread(i, n + 3)
                        if front and n == WINS - 1:
                            pe.wait_ge(S["eT_ready"], 4 * m + 2)
                            for ahead in range(AHEAD):
                                e_spread(ahead)
                        if main:
                            mm = pe.matmul(psF, wproj_g[:], win[:, n // KW, n % KW, :], start=n == 0, stop=n == WINS - 1)
                            if n == WINS - 1:
                                mm.then_inc(S["final_mm"], 1)
                            if n == 2:
                                pe.wait_ge(S["rc_ready"], i + 1)
                                pe.wait_ge(S["cnt_ready"], i + 1)
                                if back:
                                    pe.wait_ge(S["xb_ready"], j + 1)
                                for t in range(TILES):
                                    mm = turn(psA[0:2, 1, P * t:P * t + P], rc[:, t, :], ident[:])
                                mm.then_inc(S["rc_turned"], 1)
                            if n == WINS - 2:
                                pe.wait_ge(S["rcT_ready"], i + 1)
                                pe.matmul(psF, brow[:], rcT[:], start=False, stop=False)
                        if front and n == 3:
                            turn_e(m, 0)
                        if front and n == 5:
                            turn_e(m, 1)
                        if front and n == 8:
                            turn_r(m)
                    if back:
                        back_pe(s, j, main)
                    if front:
                        front_pe(s, m)
            rounds(pe, round_pe)
            scan_pe(pe)

        @block.scalar
        def _(ac):
            halves = psP[:, :, 0:HALF].rearrange("p b (r c) -> p b r c", c=IMG)

            def ln_act(tag, slots, s, i):
                if s == slots[1]:
                    ac.wait_ge(S[tag + "_mean"], i + 1)
                    ac.activation(sq[:], psA[:, 0, :], ACT.Square).then_inc(S[tag + "_sq"], 1)
                    if tag == "lnA":
                        ac.wait_ge(S["lnC_xn"], i)
                    if tag == "lnB":
                        ac.wait_ge(S["lnA_xn"], i + 1)
                    if tag == "lnC":
                        ac.wait_ge(S["lnB_xn"], i + 1)
                    ac.activation(xc[:], psA[:, 0, :], ACT.Copy).then_inc(S[tag + "_cent"], 1)

            def front_act(s, i):
                if s == F_CENT:
                    ac.wait_ge(S["pre_mean"], i + 1)
                    ac.activation(sq0.rearrange("p (b n) -> p b n", b=2), psP[:, :, 0:HALF], ACT.Square).then_inc(S["pre_sq"], 1)
                    ac.wait_ge(S["v_mm"], i)
                    ac.activation(xc0[:].rearrange("p (b n) -> p b n", b=2), psP[:, :, 0:HALF], ACT.Copy)\
                        .then_inc(S["pre_cent"], 1)
                if s == F_K:
                    ac.wait_ge(S["k_mm"], i + 1)
                    ac.wait_ge(S["prod_pool"], i * len(BY_POOL))
                    ac.wait_ge(S["prod_dve"], i * len(BY_DVE))
                    ac.activation(k_pad[:, :, HALO:HALO + IMG].rearrange("p (b r) c -> p b r c", b=2), halves,
                                  ACT.Identity, bias=bqkv[:, 1:2]).then_inc(S["k_ready"], 1)
                if s == F_Q:
                    ac.wait_ge(S["q_mm"], i + 1)
                    ac.activation(q[:], psP[:, 0, :], ACT.Identity, bias=bqkv[:, 0:1]).then_inc(S["q_ready"], 1)
                if s == F_VAL:
                    ac.wait_ge(S["v_mm"], i + 1)
                    ac.wait_ge(S["ev_ready"], i * OFFS)
                    ac.activation(v_pad[:, :, HALO:HALO + IMG].rearrange("p (b r) c -> p b r c", b=2), halves,
                                  ACT.Identity, bias=bqkv[:, 2:3]).then_inc(S["v_ready"], 1)

            def soft_act(i):
                ac.wait_ge(S["es_ready"], i + 1)
                ac.activation(e32[:], es[:], ACT.Exp).then_inc(S["e_ready"], 1)
                ac.wait_ge(S["e_ready"], i + 1)
                to = e3[:].rearrange("p t o s h -> p (t o) s h")
                ac.activation(to[:, :, 0, :], e32[:].rearrange("p t o h -> p (t o) h"), ACT.Copy).then_inc(S["e_hi"], 1)

            def mid_act(i):
                to = e3[:].rearrange("p t o s h -> p (t o) s h")
                ac.wait_ge(S["e_rest"], i + 1)
                ac.activation(to[:, :, 1, :], erest[:].rearrange("p t o h -> p (t o) h"), ACT.Copy).then_inc(S["e_mid"], 1)

            def parts_act(i, part):
                to = r3[:].rearrange("p t o s h -> p (t o) s h")
                if part == 0:
                    ac.wait_ge(S["r_ready"], i + 1)
                    ac.activation(to[:, :, 0, :], rden[:].rearrange("p t o h -> p (t o) h"), ACT.Copy).then_inc(S["r_hi"], 1)
                else:
                    ac.wait_ge(S["r_rest"], i + 1)
                    ac.activation(to[:, :, 1, :], rrest[:].rearrange("p t o h -> p (t o) h"), ACT.Copy).then_inc(S["r_mid"], 1)

            def turned_act(i, part):
                ge, gr = NB * PARTS * HEADS, KW * PARTS * HEADS
                if part == 0:
                    ac.wait_ge(S["e_turned"], 4 * i + 1)
                    ac.activation(eT[:, 0:2, :], psT[0:ge, 0:2 * PIX].rearrange("p (g n) -> p g n", n=PIX), ACT.Copy)\
                        .then_inc(S["eT_ready"], 1)
                    ac.wait_ge(S["e_turned"], 4 * i + 2)
                    ac.activation(eT[:, 2:4, :], psT[0:ge, 2 * PIX:4 * PIX].rearrange("p (g n) -> p g n", n=PIX), ACT.Copy)\
                        .then_inc(S["eT_ready"], 1)
                else:
                    ac.wait_ge(S["e_turned"], 4 * i + 3)
                    ac.wait_ge(S["e_turned"], 4 * i + 4)
                    ac.activation(eT[:, 4, :], psT[0:ge, 0:PIX], ACT.Copy).then_inc(S["eT_ready"], 1)
                    ac.activation(rT[:], psT[0:gr, PIX:4 * PIX].rearrange("p (g n) -> p g n", n=PIX), ACT.Copy)\
                        .then_inc(S["eT_ready"], 1)

            def back_act(s, i):
                ln_act("lnA", A_SLOTS, s, i)
                if s == ROUTE1:
                    ac.wait_ge(S["gap_ready"], i + 1)
                    ac.activation(top[:, 3, :], top[:, 2, :], ACT.Exp).then_inc(S["exp_ready"], 1)
                if s == G_TURN:
                    ac.wait_ge(S["g_turned"], i + 1)
                    ac.activation(gT[:], psA[0:EXPERTS, 1, :], ACT.Copy).then_inc(S["gT_ready"], 1)
                ln_act("lnB", B_SLOTS, s, i)
                ln_act("lnC", C_SLOTS, s, i)
                if s == STATS:
                    ac.wait_ge(S["stats_ready"], i + 1)
                    ac.wait_ge(S["wx_stored"], 16 * i)
                    ac.activation(wx[:], psA[:, 1, :], ACT.Copy).then_inc(S["wx_ready"], 1)

            def round_act(i, main, front, back):
                j, m = i - 1, i + 1
                for s in range(END):
                    if NORM <= s < NORM + WINS:
                        n = s - NORM
                        if main:
                            ac.wait_ge(S["proj_mm"], i * WINS + n + 1)
                            if n == 2:
                                ac.wait_ge(S["hsum_step"], (i + 1) * 5 * POOL_ROWS)
                            if n == 6:
                                ac.wait_ge(S["hsum_dve"], 5 * DVE_ROWS * (i + 1))
                            if n == 8:
                                ac.wait_ge(S["vary_mm"], 3 * i + 1)
                            ac.activation(sqy_slot[n], psY, ACT.Square, bias=bproj_c[:]).then_inc(S["sqy_ready"], 1)
                            if n in (4, 8):
                                ac.wait_ge(S["vary_mm"], 3 * i + n // 4)
                                ac.wait_ge(S["vsum_step"], 5 * i + 2)
                                if n == 8:
                                    ac.wait_ge(S["var_turned"], 2 * i + 1)
                                ac.activation(var_row, psF, ACT.Copy).then_inc(S["var_row"], 1)
                        if front and n == 5:
                            ac.wait_ge(S["reduced"], m * OFFS + 16)
                            ac.activation(s2[:, 0, :], psP[:, 0, :], ACT.Copy).then_inc(S["s2_ready"], 1)
                    if s == SOFT and front:
                        n = OFFS * HEADS - P
                        ac.wait_ge(S["reduced"], m * OFFS + OFFS)
                        ac.activation(s2[0:n, 1, :], psP[0:n, 1, :], ACT.Copy).then_inc(S["s2_ready"], 1)
                        soft_act(m)
                    if s == SOFT and front:
                        mid_act(m)
                    if s == SUM + 2 and main:
                        ac.wait_ge(S["rc_turned"], i + 1)
                        ac.activation(rcT[:], psA[0:2, 1, :], ACT.Copy).then_inc(S["rcT_ready"], 1)
                    if s == SUM + 3 and front:
                        parts_act(m, 0)
                        turned_act(m, 0)
                    if s == SUM + 5 and front:
                        parts_act(m, 1)
                    if s == SUM + 8 and front:
                        turned_act(m, 1)
                    if back:
                        back_act(s, j)
                    if front:
                        front_act(s, m)
            rounds(ac, round_act)
            scan_act(ac)

        @block.vector
        def _(ve):
            n_setup = [0]

            def own(ins):
                n_setup[0] += 1
                ins.then_inc(S["w_scaled"], 1)
                ve.wait_ge(S["w_scaled"], n_setup[0])
            ve.wait_ge(S["weights"], 16 * LOADS)
            ve.wait_ge(S["consts"], CONSTS)
            own(ve.tensor_scalar(conv_bT, ident[:], 0.95, None, ALU.mult))
            own(ve.scalar_tensor_tensor(out=conv_bT, in0=conv_mT[:], scalar=0.025, in1=conv_bT, op0=ALU.mult, op1=ALU.add))
            ve.tensor_copy(conv_s[:, 0, :], conv_a[:]).then_inc(S["setup_dve"], 1)
            ve.wait_ge(S["setup_pe"], 1)
            own(ve.tensor_copy(bqkv[:], psA[:, 0, 0:3]))
            own(ve.tensor_scalar(bqkv[:, 0:1], bqkv[:, 0:1], HD ** -0.5, None, ALU.mult))
            own(ve.tensor_copy(bproj_c[:], psA[:, 0, 4:5]))
            own(ve.tensor_scalar(wqkv[:], wqkv[:], cols[:, 0:1], None, ALU.mult))
            own(ve.tensor_scalar(wqkv[:, 0, :], wqkv[:, 0, :], HD ** -0.5, None, ALU.mult))
            own(ve.tensor_reduce(tiny[:, 2:3], wproj[:], AX.X, ALU.add))
            own(ve.tensor_scalar(tiny[:, 2:3], tiny[:, 2:3], 1.0 / P, None, ALU.mult))
            own(ve.tensor_scalar(wproj[:], wproj[:], tiny[:, 2:3], None, ALU.subtract))
            own(ve.tensor_tensor(wproj_g[:], wproj[:], prow[:, 1, :], ALU.mult))
            own(ve.tensor_reduce(tiny[:, 3:4], prow[:, 0, :], AX.X, ALU.add))
            own(ve.tensor_scalar(tiny[:, 3:4], tiny[:, 3:4], 1.0 / P, None, ALU.mult))
            own(ve.tensor_scalar(prow[:, 0, :], prow[:, 0, :], tiny[:, 3:4], None, ALU.subtract))
            own(ve.tensor_tensor(prow[:, 0, :], prow[:, 0, :], prow[:, 1, :], ALU.mult))
            own(ve.tensor_scalar(brow[:], prow[0:2, 0, :], sel[:, 0:1], None, ALU.mult))
            own(ve.scalar_tensor_tensor(out=brow[:], in0=prow[0:2, 2, :], scalar=sel[:, 1:2], in1=brow[:], op0=ALU.mult, op1=ALU.add))
            for n in range(CONV_STEPS):
                ve.wait_ge(S["setup_pe"], n + 2)
                ve.scalar_tensor_tensor(out=conv_s[:, n + 1, :], in0=conv_a[:], scalar=0.025, in1=psB[:, n % 2, 0:P],
                                        op0=ALU.mult, op1=ALU.add).then_inc(S["setup_dve"], 1)
            ve.wait_ge(S["setup_pe"], CONV_STEPS + 2)
            ve.tensor_copy(conv_mT[:], psB[:, 0, 0:P]).then_inc(S["w_ready"], 1)

            def ln_dve(tag, slots, s, i, eps):
                if s == slots[3]:
                    ve.wait_ge(S[tag + "_var"], i + 1)
                    ve.tensor_scalar(var[:], psA[:, 0, 0:TILES], 1.0, eps, ALU.mult, ALU.add).then_inc(S[tag + "_v"], 1)
                if s == slots[5]:
                    ve.wait_ge(S[tag + "_cent"], i + 1)
                    ve.wait_ge(S[tag + "_bc"], i + 1)
                    ve.tensor_tensor(xn[:], xc[:], psA[:, 0, :], ALU.mult).then_inc(S[tag + "_xn"], 1)

            def front_dve(s, i):
                xc2 = xc0[:].rearrange("p (b n) -> p b n", b=2)
                if s == F_V:
                    ve.wait_ge(S["pre_var"], i + 1)
                    ve.tensor_scalar(var0[:], psP[:, 0, 0:HTILES], 1.0 + 1e-5, 1e-11, ALU.mult, ALU.add).then_inc(S["pre_v"], 1)
                if s == F_XN:
                    ve.wait_ge(S["pre_bc"], i + 1)
                    ve.wait_ge(S["pre_cent"], i + 1)
                    ve.tensor_tensor(xc2, xc2, psP[:, :, 0:HALF], ALU.mult).then_inc(S["pre_xn"], 1)

            def products(i, group):
                for kk in group:
                    if kk not in BY_DVE:
                        continue
                    n = BY_DVE.index(kk)
                    if n == 0:
                        ve.wait_ge(S["k_ready"], i + 1)
                        ve.wait_ge(S["q_ready"], i + 1)
                        ve.wait_ge(S["reduced"], i * OFFS)
                    if n >= DVE_RING:
                        ve.wait_ge(S["reduced"], i * OFFS + BY_DVE[n - DVE_RING] + 1)
                    ve.tensor_tensor(rows(prod_d[:, n % DVE_RING, :]), rows(q[:]), head_shift(k_pad, SEQ[kk]),
                                     ALU.mult).then_inc(S["prod_dve"], 1)

            def soft_shift(i):
                ve.wait_ge(S["s_turned"], i + 1)
                sc = psS[:, :, 0:OFFS * HEADS].rearrange("p t (o h) -> p t o h", h=HEADS)
                ve.tensor_reduce(smax[:], psS[:, :, 0:OFFS * HEADS].rearrange("p t (o h) -> p t h o", h=HEADS), AX.X, ALU.max)\
                    .then_inc(S["smax_ready"], 1)
                ve.wait_ge(S["smax_ready"], i + 1)
                ve.tensor_tensor(es[:], sc, smax[:].unsqueeze(2).to_broadcast([P, TILES, OFFS, HEADS]), ALU.subtract)\
                    .then_inc(S["es_ready"], 1)

            def soft_sums(i, part):
                ee = e32[:].rearrange("p t (y x) h -> p (t y) (x h)", x=NB)
                e3v = e3[:].rearrange("p t o s h -> p (t o) s h")
                er = erest[:].rearrange("p t o h -> p (t o) h")
                dh = dsum_h[:].rearrange("p t y n -> p t (y n)")
                c, row = 4 * i, KW * HEADS
                if part == 0:
                    ve.wait_ge(S["e_ready"], i + 1)
                    ve.tensor_tensor(dsum_a[:], ee[:, :, 0:row], ee[:, :, HEADS:HEADS + row], ALU.add).then_inc(S["dsum_step"], 1)
                    ve.wait_ge(S["e_hi"], i + 1)
                    ve.tensor_tensor(er, e32[:].rearrange("p t o h -> p (t o) h"), e3v[:, :, 0, :], ALU.subtract)\
                        .then_inc(S["e_rest"], 1)
                if part == 1:
                    ve.wait_ge(S["dsum_step"], c + 1)
                    ve.tensor_tensor(dsum_h[:].rearrange("p t y n -> p (t y) n"), dsum_a[:], ee[:, :, 2 * HEADS:2 * HEADS + row],
                                     ALU.add).then_inc(S["dsum_step"], 1)
                    ve.wait_ge(S["dsum_step"], c + 2)
                    ve.tensor_tensor(dsum_b[:], dh[:, :, 0:KW * row], dh[:, :, row:row + KW * row], ALU.add)\
                        .then_inc(S["dsum_step"], 1)
                if part == 2:
                    ve.wait_ge(S["e_rest"], i + 1)
                    ve.wait_ge(S["e_mid"], i + 1)
                    ve.tensor_tensor(e3v[:, :, 2, :], er, e3v[:, :, 1, :], ALU.subtract).then_inc(S["e_lo"], 1)
                    ve.wait_ge(S["dsum_step"], c + 3)
                    ve.tensor_tensor(dsum[:], dsum_b[:], dh[:, :, 2 * row:2 * row + KW * row], ALU.add)\
                        .then_inc(S["dsum_step"], 1)
                if part == 3:
                    ve.wait_ge(S["dsum_step"], c + 4)
                    ve.reciprocal(rden[:].rearrange("p t w h -> p (t w h)"), dsum[:].rearrange("p t n -> p (t n)"))\
                        .then_inc(S["r_ready"], 1)

            def soft_parts(i, part):
                r3v = r3[:].rearrange("p t o s h -> p (t o) s h")
                rr = rrest[:].rearrange("p t o h -> p (t o) h")
                if part == 0:
                    ve.wait_ge(S["r_ready"], i + 1)
                    ve.wait_ge(S["r_hi"], i + 1)
                    ve.tensor_tensor(rr, rden[:].rearrange("p t o h -> p (t o) h"), r3v[:, :, 0, :], ALU.subtract)\
                        .then_inc(S["r_rest"], 1)
                else:
                    ve.wait_ge(S["r_rest"], i + 1)
                    ve.wait_ge(S["r_mid"], i + 1)
                    ve.tensor_tensor(r3v[:, :, 2, :], rr, r3v[:, :, 1, :], ALU.subtract).then_inc(S["r_lo"], 1)

            def vary_part(i, part):
                w0, w1 = VARY[part]
                to = vary[:, w0 * TILES:w1 * TILES]
                if part < 2:
                    ve.wait_ge(S["var_turned"], 2 * i + part + 1)
                    src = psF.rearrange("p (t g c) -> p g t c", t=TILES, g=4)[:, :, :, 0]
                    to = to.rearrange("p (g t) -> p g t", t=TILES)
                else:
                    ve.wait_ge(S["vary_mm"], 3 * i + 3)
                    src = psF[:, 0:TILES]
                ve.tensor_scalar(to, src, 1.0, 1e-5, ALU.mult, ALU.add).then_inc(S["vary_ready"], 1)

            def std_valid(i, part):
                w0, w1 = (0, 4) if part == 0 else (4, WINS)
                ve.wait_ge(S["rsy_ready"], 3 * i + (1, 3)[part])
                if part == 0:
                    ve.wait_ge(S["ok_loaded"], 16 * (i + 1))
                ve.tensor_tensor(rsv[:, :, w0:w1], rsy[:].rearrange("p (w t) -> p t w", t=TILES)[:, :, w0:w1], ok[:, :, w0:w1],
                                 ALU.mult).then_inc(S["rsv_ready"], 1)

            def window_std(i, n):
                ve.wait_ge(S["rs_spread"], i * WINS + n + 1)
                ve.wait_ge(S["proj_mm"], (i + 1) * WINS)
                o_w = win[:, n // KW, n % KW, :]
                ve.tensor_tensor(o_w, o_w, psR[:, n % 3, :], ALU.mult).then_inc(S["u_ready"], 1)

            def dve_column_sums(i, dy):
                e, o, c = ev_row[dy], hs[:, dy], 5 * (i * DVE_ROWS + dy - POOL_ROWS)
                ve.wait_ge(S["ev_ready"], i * OFFS + NB * (dy + 1))
                if dy > POOL_ROWS or not isinstance(i, int) or i:
                    ve.wait_ge(S["hsum_dve"], c)
                ve.tensor_tensor(hs_b[:, 0, :], e[:, 1, :], e[:, 2, :], ALU.add).then_inc(S["hsum_dve"], 1)
                ve.tensor_tensor(hs_b[:, 1, :], e[:, 3, :], e[:, 4, :], ALU.add).then_inc(S["hsum_dve"], 1)
                ve.wait_ge(S["hsum_dve"], c + 1)
                ve.tensor_tensor(o[:, 0, :], e[:, 0, :], hs_b[:, 0, :], ALU.add).then_inc(S["hsum_dve"], 1)
                ve.tensor_tensor(o[:, 1, :], e[:, 3, :], hs_b[:, 0, :], ALU.add).then_inc(S["hsum_dve"], 1)
                ve.wait_ge(S["hsum_dve"], c + 2)
                ve.tensor_tensor(o[:, 2, :], e[:, 2, :], hs_b[:, 1, :], ALU.add).then_inc(S["hsum_dve"], 1)

            def row_sums(i, n):
                c = 5 * i
                if n == 0:
                    ve.wait_ge(S["hsum_step"], i * 5 * POOL_ROWS + 5 * KW)
                    ve.tensor_tensor(vs[:, 0], hs[:, 1], hs[:, 2], ALU.add).then_inc(S["vsum_step"], 1)
                if n == 1:
                    ve.wait_ge(S["vsum_step"], c + 1)
                    ve.tensor_tensor(win[:, 0], hs[:, 0], vs[:, 0], ALU.add).then_inc(S["vsum_step"], 1)
                if n == 2:
                    ve.wait_ge(S["hsum_step"], (i + 1) * 5 * POOL_ROWS)
                    ve.wait_ge(S["vsum_step"], c + 1)
                    ve.tensor_tensor(win[:, 1], hs[:, 3], vs[:, 0], ALU.add).then_inc(S["vsum_step"], 1)
                if n == 3:
                    ve.wait_ge(S["hsum_dve"], 5 * DVE_ROWS * (i + 1))
                    ve.tensor_tensor(vs[:, 1], hs[:, 3], hs[:, 4], ALU.add).then_inc(S["vsum_step"], 1)
                if n == 4:
                    ve.wait_ge(S["vsum_step"], c + 4)
                    ve.tensor_tensor(win[:, 2], hs[:, 2], vs[:, 1], ALU.add).then_inc(S["vsum_step"], 1)

            def route(i, part):
                k = [0 if part == 0 else 12]

                def step(ins):
                    k[0] += 1
                    ins.then_inc(S["route_step"], 1)
                    ve.wait_ge(S["route_step"], ROUTE * i + k[0])

                def per_tile(a):
                    return a.unsqueeze(2).to_broadcast([P, TILES, EXPERTS])
                if part == 0:
                    ve.wait_ge(S["logit_mm"], i + 1)
                    step(ve.tensor_tensor(logit[:], psA[:, 1, 0:TILES * EXPERTS].rearrange("p (t e) -> p t e", e=EXPERTS),
                                          rb[:].unsqueeze(1).to_broadcast([P, TILES, EXPERTS]), ALU.add))
                    for n in range(2):
                        src = logit[:] if n == 0 else rt[:, 2]
                        step(ve.tensor_reduce(top[:, n, :], src, AX.X, ALU.max))
                        step(ve.tensor_tensor(rt[:, 0], src, per_tile(top[:, n, :]), ALU.is_equal))
                        step(ve.tensor_tensor(rt[:, 1], rt[:, 0], rank[:], ALU.mult))
                        step(ve.tensor_reduce(top[:, 4, :], rt[:, 1], AX.X, ALU.min))
                        step(ve.tensor_tensor(hot[:, n], rt[:, 1], per_tile(top[:, 4, :]), ALU.is_equal))
                        if n == 0:
                            step(ve.scalar_tensor_tensor(out=rt[:, 2], in0=hot[:, 0], scalar=-3e38, in1=logit[:],
                                                         op0=ALU.mult, op1=ALU.add))
                    assert k[0] == 12
                    ve.tensor_tensor(top[:, 2, :], top[:, 1, :], top[:, 0, :], ALU.subtract).then_inc(S["gap_ready"], 1)
                else:
                    ve.wait_ge(S["exp_ready"], i + 1)
                    step(ve.tensor_scalar(top[:, 5, :], top[:, 3, :], 1.0, None, ALU.add))
                    step(ve.reciprocal(top[:, 6, :], top[:, 5, :]))
                    step(ve.tensor_tensor(top[:, 7, :], top[:, 3, :], top[:, 6, :], ALU.mult))
                    step(ve.tensor_tensor(rt[:, 0], hot[:, 0], per_tile(top[:, 6, :]), ALU.mult))
                    step(ve.tensor_tensor(rt[:, 1], hot[:, 1], per_tile(top[:, 7, :]), ALU.mult))
                    assert k[0] == ROUTE
                    ve.tensor_tensor(gate[:], rt[:, 0], rt[:, 1], ALU.add).then_inc(S["g_ready"], 1)

            def back_dve(s, i):
                if s == X1:
                    ve.wait_ge(S["final_mm"], i + 1)
                    ve.wait_ge(S["xres_loaded"], 16 * (i + 1))
                    ve.tensor_tensor(x1[:], xres[:], psF, ALU.add).then_inc(S["x1_ready"], 1)
                ln_dve("lnA", A_SLOTS, s, i, 1e-5)
                if s == ROUTE1:
                    route(i, 0)
                if s == ROUTE2:
                    route(i, 1)
                if s in XG:
                    e = XG.index(s)
                    ve.wait_ge(S["g_spread"], EXPERTS * i + e + 1)
                    if e >= 2:
                        ve.wait_ge(S["moe_mm"], EXPERTS * i + e - 1)
                    ve.tensor_tensor(xg[:, e % 2, :], xn[:], psA[:, 0, :], ALU.mult).then_inc(S["xg_ready"], 1)
                if s == XA:
                    ve.wait_ge(S["moe_mm"], EXPERTS * (i + 1))
                    ve.tensor_tensor(xa[:], x1[:], psA[:, 1, :], ALU.add).then_inc(S["xa_ready"], 1)
                ln_dve("lnB", B_SLOTS, s, i, 1e-6)
                if s == XB:
                    ve.wait_ge(S["conv_mm"], i + 1)
                    ve.wait_ge(S["xb_stored"], 16 * i)
                    ve.tensor_tensor(xb[:], xa[:], psA[:, 1, :], ALU.add).then_inc(S["xb_ready"], 1)
                ln_dve("lnC", C_SLOTS, s, i, 1e-5)
                if s == STATS:
                    ve.wait_ge(S["wx_mm"], i + 1)
                    ve.bn_stats(stats[:, bass.ds(i * 6, 6)] if n_chunks > 3 and not isinstance(i, int)
                                else stats[:, i * 6:i * 6 + 6], psA[:, 1, :]).then_inc(S["stats_ready"], 1)

            def round_dve(i, main, front, back):
                j, m = i - 1, i + 1
                for s in range(END):
                    if main and MIX <= s < MIX + OFFS:
                        o = s - MIX
                        dy = o // NB
                        if o == 0:
                            ve.wait_ge(S["v_ready"], i + 1)
                        ve.wait_ge(S["e_spread"], i * OFFS + o + 1)
                        if o == 2 * NB:
                            ve.wait_ge(S["final_mm"], i)
                        if o == 3 * NB:
                            ve.wait_ge(S["hsum_step"], i * 5 * POOL_ROWS + 5)
                        if o == 4 * NB:
                            ve.wait_ge(S["hsum_step"], i * 5 * POOL_ROWS + 10)
                        ve.tensor_tensor(rows(ev_row[dy][:, o % NB, :]), rows(psE[:, o % 4, :]), head_shift(v_pad, o), ALU.mult)\
                            .then_inc(S["ev_ready"], 1)
                    if main and VERT <= s < VERT + 2:
                        row_sums(i, s - VERT)
                    if NORM <= s < NORM + WINS:
                        n = s - NORM
                        if main:
                            ve.wait_ge(S["r_spread"], i * WINS + n + 1)
                            if n % KW == 0:
                                ve.wait_ge(S["vsum_step"], 5 * i + (2, 3, 5)[n // KW])
                            o_w = win[:, n // KW, n % KW, :]
                            ve.tensor_tensor(o_w, o_w, psB[:, n % 2, :], ALU.mult).then_inc(S["win_ready"], 1)
                        if front:
                            products(m, GROUPS[n])
                        if main and n in (1, 4, 5):
                            row_sums(i, (1, 4, 5).index(n) + 2)
                        if main and n == 2:
                            dve_column_sums(i, NB - 1)
                        if main and n == 6:
                            vary_part(i, 0)
                        if main and n == 8:
                            std_valid(i, 0)
                    if s == SOFT:
                        if main:
                            vary_part(i, 1)
                            window_std(i, 0)
                            vary_part(i, 2)
                            window_std(i, 1)
                        if front:
                            soft_shift(m)
                    if SUM <= s < SUM + WINS:
                        n = s - SUM
                        if main and n + 2 < WINS:
                            window_std(i, n + 2)
                        if main and n == 0:
                            std_valid(i, 1)
                            ve.wait_ge(S["rsv_ready"], 2 * i + 2)
                            ve.wait_ge(S["rc_turned"], i)
                            ve.tensor_reduce(rc[:, :, 0:1], rsv[:], AX.X, ALU.add).then_inc(S["rc_ready"], 1)
                            ve.tensor_copy(rc[:, :, 1:2], ok[:, :, WINS:]).then_inc(S["cnt_ready"], 1)
                        if front and n < 4:
                            soft_sums(m, n)
                        if front and n in (4, 6):
                            soft_parts(m, n // 2 - 2)
                    if back:
                        back_dve(s, j)
                    if front:
                        front_dve(s, m)
            rounds(ve, round_dve)
            ve.wait_ge(S["stats_ready"], n_chunks)
            ve.bn_aggr(mv[:], stats[:, 0:6 * n_chunks]).then_inc(S["bn_step"], 1)
            ve.wait_ge(S["bn_step"], 1)
            ve.tensor_scalar(tiny[:, 0:1], mv[:, 1:2], 1.0, 1e-5, ALU.mult, ALU.add).then_inc(S["bn_v"], 1)
            ve.wait_ge(S["bn_rs"], 1)
            ve.tensor_tensor(tiny[:, 4:5], tiny[:, 1:2], cols[:, 3:4], ALU.mult).then_inc(S["bn_step"], 1)
            ve.wait_ge(S["bn_step"], 2)
            ve.tensor_tensor(tiny[:, 6:7], mv[:, 0:1], tiny[:, 4:5], ALU.mult).then_inc(S["bn_step"], 1)
            ve.wait_ge(S["bn_step"], 3)
            ve.tensor_tensor(tiny[:, 5:6], cols[:, 4:5], tiny[:, 6:7], ALU.subtract).then_inc(S["bn_step"], 1)
            ve.wait_ge(S["bn_step"], 4)
            scan_dve(ve)


_INS = ["x_halo", "valid", "w_qkvT", "w_projT", "b_proj", "ln1_g", "ln1_b", "ln2_g", "ln2_b", "router_w", "router_b",
        "expert_w", "expert_b", "conv", "convT", "w_T", "v_T", "gamma", "beta"]


def layouts(inputs):
    import numpy as np
    x = np.asarray(inputs["x"])
    xp = np.zeros((IMGS, P, IMG + 2 * HALO, IMG), x.dtype)
    xp[:, :, HALO:HALO + IMG] = x
    halo = np.stack([xp[:, :, r:r + HROWS] for r in range(0, IMG, ROWS)], 1)
    rr, cc = np.meshgrid(np.arange(IMG), np.arange(IMG), indexing="ij")
    last = IMG - KW
    mask = np.stack([(rr - 2 + a >= 0) & (rr - 2 + a <= last) & (cc - 2 + b >= 0) & (cc - 2 + b <= last)
                     for a in range(KW) for b in range(KW)], -1).astype(np.float32)
    mask = np.concatenate([mask, mask.sum(-1, keepdims=True)], -1)
    mask = mask.reshape(IMG // ROWS, TILES, P, WINS + 1).transpose(0, 2, 1, 3).reshape(IMG // ROWS, P, TILES * (WINS + 1))
    taps = np.asarray(inputs["L1_conv_weight"]).reshape(-1)
    padded = np.zeros(2 * P + 1, taps.dtype)
    padded[P - taps.size // 2:P - taps.size // 2 + taps.size] = taps
    at = P + np.arange(P)[None, :] - np.arange(P)[:, None]
    conv = padded[at]
    got = {
        "x_halo": halo.transpose(2, 0, 1, 3, 4).reshape(P, CHUNKS * HPIX),
        "valid": np.tile(mask, (IMGS, 1, 1)).transpose(1, 0, 2).reshape(P, -1),
        "w_qkvT": inputs["L0_conv_w_qkv"].T, "w_projT": inputs["L0_conv_w_proj"].T,
        "b_proj": inputs["L0_conv_b_proj"], "ln1_g": inputs["L0_conv_ln1_g"], "ln1_b": inputs["L0_conv_ln1_b"],
        "ln2_g": inputs["L0_conv_ln2_g"], "ln2_b": inputs["L0_conv_ln2_b"],
        "router_w": inputs["L0_ffn_router_w"], "router_b": inputs["L0_ffn_router_b"],
        "expert_w": inputs["L0_ffn_expert_w"], "expert_b": inputs["L0_ffn_expert_b"],
        "conv": conv, "convT": conv.T,
        "w_T": inputs["L1_ffn_W"].T, "v_T": inputs["L1_ffn_V"].T,
        "gamma": inputs["L1_ffn_gamma"], "beta": inputs["L1_ffn_beta"],
    }
    return {n: np.ascontiguousarray(got[n]) for n in _INS}


def kernel(**inputs):
    import concourse.bacc as _bacc
    from concourse.bass_utils import run_bass_kernel_spmd as _run

    nc = _bacc.Bacc("TRN2", target_bir_lowering=False, num_devices=1)
    arrays = layouts(inputs)
    args = [nc.dram_tensor(n, a.shape, mybir.dt.from_np(a.dtype), kind="ExternalInput").ap() for n, a in arrays.items()]
    out = nc.dram_tensor("out", (IMGS, P, STEPS), F32, kind="ExternalOutput").ap()
    program(nc, *args, out)
    r = _run(nc, [arrays], core_ids=[0])
    return r.results[0]["out"].reshape(IMGS, P, IMG, IMG)
```
